# Optimizing a Trainium2 kernel written in Bass

```python
import numpy as np
import jax
import jax.numpy as jnp

def _softmax(x, axis=-1):
    return jax.nn.softmax(x, axis=axis)

def _gelu(x):
    return jax.nn.gelu(x, approximate=True)

def _silu(x):
    return jax.nn.silu(x)

def _sigmoid(x):
    return jax.nn.sigmoid(x)

def _layernorm(x, axis=-1, eps=1e-05):
    m = jnp.mean(x, axis=axis, keepdims=True)
    v = jnp.var(x, axis=axis, keepdims=True)
    return (x - m) / jnp.sqrt(v + eps)

def _scatter_add(tgt, idx, src, axis=0):
    return tgt.at[idx].add(src)

def _segment_sum(src, seg, n):
    return jax.ops.segment_sum(src, seg, n)
kernel_name = 'mk_gnn_preln_d2_gnn_r32_3442cd'

def setup_inputs(seed: int=0):
    np.random.seed(seed)
    _w = jnp.asarray

    def _rec_inputs():
        import jax
        import jax.numpy as jnp
        _gk = jax.random.key(seed)
        x = -0.0009044 + 1 * jax.random.normal(jax.random.fold_in(_gk, 1), (3125, 32), jnp.float32)
        src = jax.random.randint(jax.random.fold_in(_gk, 2), (50000,), 0, 3125, jnp.int32)
        dst = jax.random.randint(jax.random.fold_in(_gk, 3), (50000,), 0, 3125, jnp.int32)
        _o = jnp.argsort(dst, stable=True)
        src = src[_o]
        dst = dst[_o]
        edge_attr_3 = jax.random.uniform(jax.random.fold_in(_gk, 12), (50000, 3), jnp.float32, 0.0, 0.999998)
        return (x, src, dst, edge_attr_3)
    x, src, dst, edge_attr_3 = _rec_inputs()

    def _L0_gnn_setup():
        import jax, jax.numpy as jnp
        import numpy as np
        N_NODES = 50000
        N_EDGES = 25000
        IN_FEATS = 32
        OUT_FEATS = 32
        NUM_HEADS = 4
        key = jax.random.key(seed)
        ks = jax.random.split(key, 12)
        H, F, IN = (NUM_HEADS, OUT_FEATS, IN_FEATS)
        h = jax.random.normal(ks[0], (N_NODES, IN), dtype=jnp.float32)
        src = jax.random.randint(ks[1], (N_EDGES,), 0, N_NODES, dtype=jnp.int64)
        dst = jax.random.randint(ks[2], (N_EDGES,), 0, N_NODES, dtype=jnp.int64)
        s = 0.1
        W_gat = jax.random.normal(ks[3], (IN, H * F), dtype=jnp.float32) * s
        attn_l = jax.random.normal(ks[4], (H, F), dtype=jnp.float32) * s
        attn_r = jax.random.normal(ks[5], (H, F), dtype=jnp.float32) * s
        W_ih = jax.random.normal(ks[6], (3 * F, H * F), dtype=jnp.float32) * s
        W_hh = jax.random.normal(ks[7], (3 * F, F), dtype=jnp.float32) * s
        b_ih = jax.random.normal(ks[8], (3 * F,), dtype=jnp.float32) * s
        b_hh = jax.random.normal(ks[9], (3 * F,), dtype=jnp.float32) * s
        return {'h': h, 'W_gat': W_gat, 'attn_l': attn_l, 'attn_r': attn_r, 'W_ih': W_ih, 'W_hh': W_hh, 'b_ih': b_ih, 'b_hh': b_hh, 'src': src, 'dst': dst}
    _L0_gnn_all = _L0_gnn_setup()
    _L0_gnn_in = {k: v for k, v in _L0_gnn_all.items() if k in ('W_gat', 'attn_l', 'attn_r', 'W_ih', 'W_hh', 'b_ih', 'b_hh')}
    del _L0_gnn_all

    def _L1_gnn_setup():
        import jax, jax.numpy as jnp
        import numpy as np
        D = 3
        KS = 5
        K = KS ** D
        S = 2 ** D
        _COMBOS = np.array([[s >> d & 1 for d in range(D)] for s in range(S)], dtype=np.int32)
        _STRIDES = np.array([KS ** (D - 1 - d) for d in range(D)], dtype=np.int32)

        def spline_basis(pseudo):
            pos = pseudo * (KS - 1)
            i0 = jnp.clip(jnp.floor(pos), 0, KS - 2).astype(jnp.int32)
            frac = pos - i0
            combos = jnp.asarray(_COMBOS)
            basis = jnp.prod(jnp.where(combos[None] == 1, frac[:, None, :], 1.0 - frac[:, None, :]), axis=-1)
            idx = jnp.sum((i0[:, None, :] + combos[None]) * jnp.asarray(_STRIDES)[None, None, :], axis=-1)
            return (basis, idx)

        def spline_conv(x, row, col, basis, idx, W, b):
            N = x.shape[0]
            Fout = W.shape[2]
            z = jnp.einsum('ni,kio->nko', x, W).reshape(N * K, Fout)
            gathered = z[col[:, None] * K + idx]
            msg = jnp.einsum('es,eso->eo', basis, gathered)
            out = jax.ops.segment_sum(msg, row, num_segments=N)
            deg = jax.ops.segment_sum(jnp.ones_like(msg[:, 0]), row, num_segments=N)
            return out / jnp.maximum(deg, 1.0)[:, None] + b
        key = jax.random.key(seed)
        ks = jax.random.split(key, 13)
        N, E, Fin, Fout = (625, 10000, 32, 32)

        def u(k, shape, size):
            bound = 1.0 / np.sqrt(size)
            return jax.random.uniform(k, shape, jnp.float32, -bound, bound)
        return dict(x=jax.random.normal(ks[0], (N, Fin), jnp.float32), edge_index=jax.random.randint(ks[1], (2, E), 0, N, dtype=jnp.int32), pseudo=jax.random.uniform(ks[2], (E, D), jnp.float32), stn1_w=u(ks[3], (K, 1, 64), 1 * S), stn1_b=u(ks[4], (64,), 1 * S), stn2_w=u(ks[5], (K, 64, 64), 64 * S), stn2_b=u(ks[6], (64,), 64 * S), stn3_w=u(ks[7], (64, 64), 64), stn3_b=u(ks[8], (64,), 64), stn4_w=u(ks[9], (64, 3), 64), stn4_b=u(ks[10], (3,), 64), conv_w=u(ks[11], (K, Fin, Fout), Fin * S), conv_b=u(ks[12], (Fout,), Fin * S))
    _L1_gnn_all = _L1_gnn_setup()
    _L1_gnn_in = {k: v for k, v in _L1_gnn_all.items() if k in ('stn1_w', 'stn1_b', 'stn2_w', 'stn2_b', 'stn3_w', 'stn3_b', 'stn4_w', 'stn4_b', 'conv_w', 'conv_b')}
    del _L1_gnn_all
    return {'x': x, 'src': src, 'dst': dst, 'edge_attr_3': edge_attr_3, 'L0_gnn_W_gat': _L0_gnn_in['W_gat'], 'L0_gnn_attn_l': _L0_gnn_in['attn_l'], 'L0_gnn_attn_r': _L0_gnn_in['attn_r'], 'L0_gnn_W_ih': _L0_gnn_in['W_ih'], 'L0_gnn_W_hh': _L0_gnn_in['W_hh'], 'L0_gnn_b_ih': _L0_gnn_in['b_ih'], 'L0_gnn_b_hh': _L0_gnn_in['b_hh'], 'L1_gnn_stn1_w': _L1_gnn_in['stn1_w'], 'L1_gnn_stn1_b': _L1_gnn_in['stn1_b'], 'L1_gnn_stn2_w': _L1_gnn_in['stn2_w'], 'L1_gnn_stn2_b': _L1_gnn_in['stn2_b'], 'L1_gnn_stn3_w': _L1_gnn_in['stn3_w'], 'L1_gnn_stn3_b': _L1_gnn_in['stn3_b'], 'L1_gnn_stn4_w': _L1_gnn_in['stn4_w'], 'L1_gnn_stn4_b': _L1_gnn_in['stn4_b'], 'L1_gnn_conv_w': _L1_gnn_in['conv_w'], 'L1_gnn_conv_b': _L1_gnn_in['conv_b']}

def reference(x, src, dst, edge_attr_3, L0_gnn_W_gat, L0_gnn_attn_l, L0_gnn_attn_r, L0_gnn_W_ih, L0_gnn_W_hh, L0_gnn_b_ih, L0_gnn_b_hh, L1_gnn_stn1_w, L1_gnn_stn1_b, L1_gnn_stn2_w, L1_gnn_stn2_b, L1_gnn_stn3_w, L1_gnn_stn3_b, L1_gnn_stn4_w, L1_gnn_stn4_b, L1_gnn_conv_w, L1_gnn_conv_b):
    import jax
    import jax.numpy as jnp

    def _L0_gnn_ref(h, W_gat, attn_l, attn_r, W_ih, W_hh, b_ih, b_hh, src, dst):
        import jax, jax.numpy as jnp
        import numpy as np
        N_NODES = 50000
        N_EDGES = 25000
        IN_FEATS = 32
        OUT_FEATS = 32
        NUM_HEADS = 4
        N = h.shape[0]
        H, F = attn_l.shape
        feat = (h @ W_gat).reshape(N, H, F)
        el = jnp.einsum('nhf,hf->nh', feat, attn_l)
        er = jnp.einsum('nhf,hf->nh', feat, attn_r)
        e = jax.nn.leaky_relu(el[src] + er[dst], 0.2)
        emax = jax.ops.segment_max(e, dst, num_segments=N)
        ee = jnp.exp(e - emax[dst])
        denom = jax.ops.segment_sum(ee, dst, num_segments=N)
        alpha = ee / denom[dst]
        msg = feat[src] * alpha[:, :, None]
        agg = jax.ops.segment_sum(msg, dst, num_segments=N)
        x = agg.reshape(N, H * F)
        gi = x @ W_ih.T + b_ih
        gh = h @ W_hh.T + b_hh
        i_r, i_z, i_n = jnp.split(gi, 3, axis=1)
        h_r, h_z, h_n = jnp.split(gh, 3, axis=1)
        r = jax.nn.sigmoid(i_r + h_r)
        z = jax.nn.sigmoid(i_z + h_z)
        n = jnp.tanh(i_n + r * h_n)
        h_new = (1.0 - z) * n + z * h
        return jax.nn.elu(h_new)

    def _L1_gnn_ref(x, edge_index, pseudo, stn1_w, stn1_b, stn2_w, stn2_b, stn3_w, stn3_b, stn4_w, stn4_b, conv_w, conv_b):
        import jax, jax.numpy as jnp
        import numpy as np
        D = 3
        KS = 5
        K = KS ** D
        S = 2 ** D
        _COMBOS = np.array([[s >> d & 1 for d in range(D)] for s in range(S)], dtype=np.int32)
        _STRIDES = np.array([KS ** (D - 1 - d) for d in range(D)], dtype=np.int32)

        def spline_basis(pseudo):
            pos = pseudo * (KS - 1)
            i0 = jnp.clip(jnp.floor(pos), 0, KS - 2).astype(jnp.int32)
            frac = pos - i0
            combos = jnp.asarray(_COMBOS)
            basis = jnp.prod(jnp.where(combos[None] == 1, frac[:, None, :], 1.0 - frac[:, None, :]), axis=-1)
            idx = jnp.sum((i0[:, None, :] + combos[None]) * jnp.asarray(_STRIDES)[None, None, :], axis=-1)
            return (basis, idx)

        def spline_conv(x, row, col, basis, idx, W, b):
            N = x.shape[0]
            Fout = W.shape[2]
            z = jnp.einsum('ni,kio->nko', x, W).reshape(N * K, Fout)
            gathered = z[col[:, None] * K + idx]
            msg = jnp.einsum('es,eso->eo', basis, gathered)
            out = jax.ops.segment_sum(msg, row, num_segments=N)
            deg = jax.ops.segment_sum(jnp.ones_like(msg[:, 0]), row, num_segments=N)
            return out / jnp.maximum(deg, 1.0)[:, None] + b
        N = x.shape[0]
        row, col = (edge_index[0], edge_index[1])
        basis, idx = spline_basis(pseudo)
        h = jnp.ones((N, 1), x.dtype)
        h = jax.nn.elu(spline_conv(h, row, col, basis, idx, stn1_w, stn1_b))
        h = jax.nn.elu(spline_conv(h, row, col, basis, idx, stn2_w, stn2_b))
        h = jax.nn.elu(h @ stn3_w + stn3_b)
        t = h @ stn4_w + stn4_b
        new_pseudo = jnp.clip(pseudo + t[col] - t[row], 0.0, 1.0)
        basis2, idx2 = spline_basis(new_pseudo)
        return spline_conv(x, row, col, basis2, idx2, conv_w, conv_b)
    edge_index = jnp.stack([src, dst])
    h = jnp.maximum(_layernorm(x, axis=-1), 0.0)
    x = x + _L0_gnn_ref(h, L0_gnn_W_gat, L0_gnn_attn_l, L0_gnn_attn_r, L0_gnn_W_ih, L0_gnn_W_hh, L0_gnn_b_ih, L0_gnn_b_hh, src, dst)
    h = jnp.maximum(_layernorm(x, axis=-1), 0.0)
    x = x + _L1_gnn_ref(h, edge_index, edge_attr_3, L1_gnn_stn1_w, L1_gnn_stn1_b, L1_gnn_stn2_w, L1_gnn_stn2_b, L1_gnn_stn3_w, L1_gnn_stn3_b, L1_gnn_stn4_w, L1_gnn_stn4_b, L1_gnn_conv_w, L1_gnn_conv_b)
    return x

_drawn_inputs = setup_inputs


def setup_inputs(seed=0):
    import zlib

    import numpy as np

    out = dict(_drawn_inputs(seed))
    spreads = {}
    factors = {'edge_attr_3': 3.43,
     'L0_gnn_attn_l': 8.0,
     'L0_gnn_attn_r': 24.655,
     'L0_gnn_b_hh': 2.724,
     'L1_gnn_stn1_w': 8.0,
     'L1_gnn_stn1_b': 47.065,
     'L1_gnn_stn2_w': 8.0,
     'L1_gnn_stn2_b': 64.0,
     'L1_gnn_stn3_w': 8.0,
     'L1_gnn_stn3_b': 64.0,
     'L1_gnn_stn4_w': 8.0,
     'L1_gnn_stn4_b': 8.0,
     'L1_gnn_conv_w': 3.181}
    for name, (base, spread) in spreads.items():
        noise = np.random.default_rng([zlib.crc32(name.encode()), seed]).standard_normal(out[name].shape)
        drawn = base * np.exp(spread * noise) if base else spread * noise
        out[name] = jnp.asarray(drawn.astype(out[name].dtype))
    for name, factor in factors.items():
        out[name] = (out[name] * factor).astype(out[name].dtype)
    return out
```

```python
from contextlib import ExitStack

import numpy as np
import concourse.bass as bass
from concourse import mybir

F32 = mybir.dt.float32
F16 = mybir.dt.float16
BF16 = mybir.dt.bfloat16
I32 = mybir.dt.int32
U32 = mybir.dt.uint32
ALU = mybir.AluOpType
ACT = mybir.ActivationFunctionType
AX_X = mybir.AxisListType.X

N, FEAT, HEADS = 3125, 32, 4
E = 50000
KS, DIM = 5, 3
K = KS ** DIM
HID = 64

NB, BPC = 6, 21
CN = NB * BPC
NC = -(-N // CN)
LAST = N - (NC - 1) * CN
P = 128
SROWS = P * BPC
MAXSEC = NC + E // P + 1
FIXED = NC + 2
GB, NGR = 7, 3
HI = 7
LO = NC * BPC // HI
LPC = BPC // HI
EP, ET = 125, 400
GT = 25
NG = ET // GT
assert EP * ET == E and NC * BPC == LO * HI and NG % 2 == 0 and NGR * GB == BPC

SREC = 8
DREC = FEAT + 1 + HEADS + 1
TROW = FEAT + 1 + HEADS
GMX = 3
NGM = BPC // GMX
NROW = FEAT + DIM + 1
MAGIC = 12582912.0
BIG = 1.0e30


def links(eng, sem, base=0):
    count = [0]

    def link(ins):
        count[0] += 1
        ins.then_inc(sem, 1)
        eng.wait_ge(sem, base + count[0])
    return link, count


def build_sort(nc, src, dst, attr, sect, sect_count, slots_dram, drows_dram, rows_dram, ident):
    with ExitStack() as ctx:
        def sb(name, shape, dt):
            return ctx.enter_context(nc.sbuf_tensor(name, shape, dt))

        def ps(name, shape, dt=F32):
            return ctx.enter_context(nc.psum_tensor(name, shape, dt))

        def sem(name):
            return ctx.enter_context(nc.semaphore(name))

        key_i = [sb("src_i", [EP, ET], I32), sb("dst_i", [EP, ET], I32)]
        attr_sb = sb("attr_sb", [EP, ET, DIM], F32)
        kf = sb("kf", [EP, ET], F32)
        r42 = sb("r42", [EP, ET], F32)
        cm = sb("cm", [EP, ET], F32)
        l3 = sb("l3", [EP, ET], F32)
        lo = [sb(f"lo{k}", [EP, ET], F32) for k in range(2)]
        hi = [sb(f"hi{k}", [EP, ET], F32) for k in range(2)]
        jn = [sb(f"jn{k}", [EP, ET], F32) for k in range(2)]
        bc = [sb(f"bc{k}", [EP, ET], F32) for k in range(2)]
        blk = [sb(f"blk{k}", [EP, ET], F32) for k in range(2)]
        rowT = sb("rowT", [ET // 4, 4, 4 * EP], F16)
        iota_f = sb("iota_f", [P, LO], F32)
        iota_b = sb("iota_b", [P, LO], BF16)
        iota_s = sb("iota_s", [NC, MAXSEC], F32)
        part = sb("part", [P, 1], F32)
        ltri = sb("ltri", [EP, EP], F32)
        ones = sb("ones", [P, 1], F32)
        empty_s = sb("empty_s", [P, BPC, SREC], F32)
        empty_d = sb("empty_d", [P, BPC, DREC], F32)
        lo_b = [sb(f"lo_b{k}", [EP, ET], BF16) for k in range(2)]
        oh_lo = [[sb(f"oh_lo{k}{h}", [EP, GT, LO], BF16) for h in range(2)] for k in range(2)]
        oh_hi = [[sb(f"oh_hi{k}{h}", [EP, GT, HI], BF16) for h in range(2)] for k in range(2)]
        hist = [sb(f"hist{k}", [LO, HI, ET], F32) for k in range(2)]
        pref = [sb(f"pref{k}", [LO, HI, ET], F32) for k in range(2)]
        runs = sb("runs", [LO, HI, ET], F32)
        cmax = sb("cmax", [LO, 2], F32)
        crow = sb("crow", [1, 2, LO], F32)
        sq = sb("sq", [1, 2, NC], F32)
        scum = sb("scum", [1, 2, NC], F32)
        sbase = sb("sbase", [1, 2, NC], F32)
        sbase3 = sb("sbase3", [1, 2, LO], F32)
        zero_row = sb("zero_row", [1, NC], F32)
        basecol = sb("basecol", [LO, 2], F32)
        cumcol = sb("cumcol", [NC, 2], F32)
        past = [sb(f"past{k}", [NC, MAXSEC], F32) for k in range(2)]
        scount = sb("scount", [1, 2], F32)
        pg = [sb(f"pg{k}", [LO, GT, HI], F32) for k in range(2)]
        blkrow = [[sb(f"blkrow{k}{h}", [EP, GT * EP], F16) for h in range(2)] for k in range(2)]
        lorow = [[sb(f"lorow{k}{h}", [LO, GT * EP], F16) for h in range(2)] for k in range(2)]
        oh_loT = [sb(f"oh_loT{k}", [LO, GT * EP], F32) for k in range(2)]
        blk_g = [sb(f"blk_g{k}", [EP, GT], F32) for k in range(2)]
        junk = sb("junk", [EP, GT, EP], BF16)
        in_tile = [sb(f"in_tile{k}", [EP, GT], F32) for k in range(2)]
        hsel = [sb(f"hsel{k}", [EP, GT, HI], F32) for k in range(2)]
        before = [sb(f"before{k}", [EP, GT], F32) for k in range(2)]
        row21 = [sb(f"row21{k}", [EP, GT], F32) for k in range(2)]
        rec = [sb(f"rec{h}", [EP, GT, SREC], F32) for h in range(2)]
        srow = [sb(f"srow{h}", [EP, GT], U32) for h in range(2)]

        bank = [ps(f"sort_bank{i}", [P, 512]) for i in range(8)]

        edges_in = [sem("edges_in0"), sem("edges_in1"), sem("edges_in2")]
        consts_set = sem("consts_set")
        ident_step = sem("ident_step")
        empties_set = sem("empties_set")
        tables_empty = sem("tables_empty")
        more_empty = sem("more_empty")
        keys_split = sem("keys_split")
        keys_turned = sem("keys_turned")
        rowT_set = sem("rowT_set")
        rowT_out = [sem(f"rowT_out{a}") for a in range(4)]
        lohi_set = sem("lohi_set")
        hist_used = sem("hist_used")
        hist_done = sem("hist_done")
        cmax_set = sem("cmax_set")
        cmax_turned = sem("cmax_turned")
        sec_set = sem("sec_set")
        sec_turned = sem("sec_turned")
        past_set = sem("past_set")
        past_summed = sem("past_summed")
        sect_set = sem("sect_set")
        rows_in = [sem(f"rows_in{h}") for h in range(2)]
        rows_used = sem("rows_used")
        loT_set = sem("loT_set")
        before_done = sem("before_done")
        rec_set = sem("rec_set")
        rec_out = [sem(f"rec_out{h}") for h in range(2)]
        split_step = sem("split_step")
        sec_step = sem("sec_step")
        rank_step = sem("rank_step")

        block = ctx.enter_context(nc.Block())

        def bcast_rows(a, g, parts):
            return rows_dram[a:a + 1, bass.ds(g * (GT * EP), GT * EP)].to_broadcast([parts, GT * EP])

        @block.sync
        def _(sp):
            sp.dma_start(key_i[0][:, :], src).then_inc(edges_in[0], 16)
            sp.dma_start(key_i[1][:, :], dst).then_inc(edges_in[1], 16)
            sp.dma_start(attr_sb[:, :, :], attr).then_inc(edges_in[2], 16)
            for a in range(4):
                sp.wait_ge(rowT_set, a + 1)
                sp.dma_start(rows_dram[a, :].rearrange("(q r x) -> r q x", q=4, x=EP),
                             rowT[:, a, :].rearrange("r (q x) -> r q x", q=4)).then_inc(rowT_out[a], 16)
            for a in range(4):
                sp.wait_ge(rowT_out[a], 16)
            sp.sem_inc(rows_used, 2)
            with sp.Fori(0, NG // 2) as i:
                for h in range(2):
                    sp.wait_ge(rows_used, i * 2 + (h + 1))
                    for k in range(2):
                        sp.dma_start(blkrow[k][h][:, :], bcast_rows(k, i * 2 + h, EP)).then_inc(rows_in[h], 16)
                        sp.dma_start(lorow[k][h][:, :], bcast_rows(2 + k, i * 2 + h, LO)).then_inc(rows_in[h], 16)

        @block.scalar
        def _(act):
            act.wait_ge(empties_set, 5)
            act.dma_start(slots_dram[0:FIXED * SROWS, :].rearrange("(s p b) w -> p s (b w)", p=P, b=BPC),
                          empty_s[:, :, :].rearrange("p b w -> p (b w)").unsqueeze(1)
                          .to_broadcast([P, FIXED, BPC * SREC])).then_inc(tables_empty, 16)
            act.dma_start(drows_dram[0:FIXED * SROWS, :].rearrange("(s p b) w -> p s (b w)", p=P, b=BPC),
                          empty_d[:, :, :].rearrange("p b w -> p (b w)").unsqueeze(1)
                          .to_broadcast([P, FIXED, BPC * DREC])).then_inc(tables_empty, 16)
            for a in range(4):
                act.wait_ge(keys_turned, a + 1)
                nc.scalar.copy(rowT[:, a, :], bank[a][0:ET // 4, 0:4 * EP]).then_inc(rowT_set, 1)
            act.wait_ge(sect_set, 1)
            upto = act.value_load(sect_count[0:1, 1:2], min_val=FIXED + 1, max_val=MAXSEC)
            with act.Fori(FIXED, upto) as s:
                act.dma_start(slots_dram[bass.ds(s * SROWS, SROWS), :].rearrange("(p b) w -> p (b w)", b=BPC),
                              empty_s[:, :, :].rearrange("p b w -> p (b w)")).then_inc(more_empty, 16)
                act.dma_start(drows_dram[bass.ds(s * SROWS, SROWS), :].rearrange("(p b) w -> p (b w)", b=BPC),
                              empty_d[:, :, :].rearrange("p b w -> p (b w)")).then_inc(more_empty, 16)
                act.wait_ge(more_empty, (s - (FIXED - 1)) * 32)
            act.sem_inc(sect_set, 1)

        @block.gpsimd
        def _(pool):
            nc.gpsimd.memset(ident[:, :], 0.0).then_inc(ident_step, 1)
            nc.gpsimd.memset(ltri[:, :], 1.0).then_inc(ident_step, 1)
            pool.wait_ge(ident_step, 2)
            nc.gpsimd.affine_select(out=ident[:, :], in_=ident[:, :], compare_op=ALU.not_equal, fill=1.0, base=0,
                                    pattern=[[-1, P]], channel_multiplier=1).then_inc(ident_step, 1)
            nc.gpsimd.affine_select(out=ltri[:, :], in_=ltri[:, :], compare_op=ALU.is_gt, fill=0.0, base=0,
                                    pattern=[[-1, EP]], channel_multiplier=1).then_inc(ident_step, 1)
            nc.gpsimd.iota(iota_f[:, :], pattern=[[1, LO]], base=0, channel_multiplier=0,
                           allow_small_or_imprecise_dtypes=True).then_inc(consts_set, 1)
            nc.gpsimd.iota(iota_b[:, :], pattern=[[1, LO]], base=0, channel_multiplier=0,
                           allow_small_or_imprecise_dtypes=True).then_inc(consts_set, 1)
            nc.gpsimd.iota(iota_s[:, :], pattern=[[1, MAXSEC]], base=0, channel_multiplier=0,
                           allow_small_or_imprecise_dtypes=True).then_inc(consts_set, 1)
            nc.gpsimd.iota(part[:, :], pattern=[[0, 1]], base=0, channel_multiplier=1,
                           allow_small_or_imprecise_dtypes=True).then_inc(consts_set, 1)
            nc.gpsimd.memset(ones[:, :], 1.0).then_inc(consts_set, 1)
            nc.gpsimd.memset(empty_s[:, :, :], 0.0).then_inc(empties_set, 1)
            nc.gpsimd.memset(empty_d[:, :, :], 0.0).then_inc(empties_set, 1)
            pool.wait_ge(empties_set, 2)
            nc.gpsimd.memset(empty_s[:, :, 0:1], -1.0).then_inc(empties_set, 1)
            nc.gpsimd.memset(empty_d[:, :, DREC - 1:DREC], -1.0).then_inc(empties_set, 1)
            pool.wait_ge(empties_set, 4)
            nc.gpsimd.memset(empty_s[:, :, 2:3].bitcast(I32), 1 << 28).then_inc(empties_set, 1)
            pool.wait_ge(tables_empty, 32)
            pool.wait_ge(sect_set, 2)
            with pool.Fori(0, NG // 2) as i:
                for h in range(2):
                    pool.wait_ge(rec_set, i * 2 + (h + 1))
                    pool.nop(nofuse=True)
                    for t in range(GT):
                        nc.gpsimd.indirect_dma_start(
                            slots_dram[:, :], bass.IndirectOffsetOnAxis(ap=srow[h][:, t:t + 1], axis=0),
                            rec[h][:, t, :], None).then_inc(rec_out[h], 16)
            for h in range(2):
                pool.wait_ge(rec_out[h], NG // 2 * GT * 16)

        @block.tensor
        def _(pe):
            pe.wait_ge(ident_step, 4)
            for a in range(4):
                pe.wait_ge(keys_split, a % 2 + 1)
                arr = (blk[0], blk[1], lo[0], lo[1])[a]
                for q in range(4):
                    last = nc.tensor.transpose(bank[a][0:ET // 4, q * EP:(q + 1) * EP],
                                               arr[:, q * (ET // 4):(q + 1) * (ET // 4)], ident[0:EP, 0:EP])
                last.then_inc(keys_turned, 1)
            with pe.Fori(0, NG // 2) as i:
                for h in range(2):
                    pe.wait_ge(lohi_set, i * 2 + (h + 1))
                    pe.wait_ge(hist_used, i * 2 + (h + 1))
                    for k in range(2):
                        for t in range(GT):
                            last = nc.tensor.matmul(bank[4 + 2 * k + h][0:LO, t * HI:(t + 1) * HI],
                                                    oh_lo[k][h][:, t, :], oh_hi[k][h][:, t, :], start=True, stop=True)
                    last.then_inc(hist_done, 1)
            pe.wait_ge(cmax_set, 1)
            pe.wait_ge(rowT_set, 4)
            for k in range(2):
                last = nc.tensor.transpose(bank[0][0:1, k * P:k * P + LO], cmax[:, k:k + 1], ident[0:LO, 0:LO])
            last.then_inc(cmax_turned, 1)
            pe.wait_ge(sec_set, 1)
            for k in range(2):
                nc.tensor.matmul(bank[1][0:LO, k:k + 1], sbase3[0:1, k, :], ones[0:1, 0:1], start=True, stop=True)
                last = nc.tensor.matmul(bank[1][0:NC, 4 + k:5 + k], scum[0:1, k, :], ones[0:1, 0:1],
                                        start=True, stop=True)
            last.then_inc(sec_turned, 1)
            pe.wait_ge(past_set, 1)
            for k in range(2):
                last = nc.tensor.matmul(bank[2 + k][0:1, 0:MAXSEC], ones[0:NC, 0:1], past[k][:, :],
                                        start=True, stop=True)
            last.then_inc(past_summed, 1)
            with pe.Fori(0, NG) as g:
                pe.wait_ge(loT_set, g + 1)
                for k in range(2):
                    for t in range(GT):
                        last = nc.tensor.matmul(bank[4 + k][0:EP, t * HI:(t + 1) * HI],
                                                oh_loT[k][:, t * EP:(t + 1) * EP], pg[k][:, t, :],
                                                start=True, stop=True)
                last.then_inc(before_done, 1)

        @block.vector
        def _(dve):
            link, _c = links(dve, split_step)
            dve.wait_ge(consts_set, 5)

            def floor_div(out, x, d):
                link(nc.vector.tensor_scalar(out, x, 1.0 / d, 0.5 / d - 0.5, ALU.mult, ALU.add))
                link(nc.vector.tensor_scalar(out, out, MAGIC, -MAGIC, ALU.add, ALU.add))

            for k in range(2):
                dve.wait_ge(edges_in[k], 16)
                link(nc.vector.tensor_copy(kf[:, :], key_i[k][:, :]))
                floor_div(lo[k][:, :], kf[:, :], NB * HI)
                link(nc.vector.scalar_tensor_tensor(r42[:, :], lo[k][:, :], -float(NB * HI), kf[:, :],
                                                    ALU.mult, ALU.add))
                floor_div(hi[k][:, :], r42[:, :], NB)
                link(nc.vector.scalar_tensor_tensor(blk[k][:, :], lo[k][:, :], float(HI), hi[k][:, :],
                                                    ALU.mult, ALU.add))
                dve.sem_inc(keys_split, 1)
                link(nc.vector.scalar_tensor_tensor(jn[k][:, :], hi[k][:, :], -float(NB), r42[:, :],
                                                    ALU.mult, ALU.add))
                floor_div(cm[:, :], lo[k][:, :], LPC)
                link(nc.vector.scalar_tensor_tensor(l3[:, :], cm[:, :], -float(LPC), lo[k][:, :],
                                                    ALU.mult, ALU.add))
                link(nc.vector.scalar_tensor_tensor(bc[k][:, :], l3[:, :], float(HI), hi[k][:, :],
                                                    ALU.mult, ALU.add))
                link(nc.vector.tensor_copy(lo_b[k][:, :], lo[k][:, :]))
            dve.sem_inc(hist_used, 2)
            dve.sem_inc(hist_done, 2)

            def one_hots(g, h):
                for k in range(2):
                    nc.vector.tensor_tensor(
                        oh_lo[k][h][:, :, :], iota_b[0:EP, 0:LO].unsqueeze(1).to_broadcast([EP, GT, LO]),
                        lo_b[k][:, bass.ds(g * GT, GT)].unsqueeze(2).to_broadcast([EP, GT, LO]), ALU.is_equal)
                    last = nc.vector.tensor_tensor(
                        oh_hi[k][h][:, :, :], iota_f[0:EP, 0:HI].unsqueeze(1).to_broadcast([EP, GT, HI]),
                        hi[k][:, bass.ds(g * GT, GT)].unsqueeze(2).to_broadcast([EP, GT, HI]), ALU.is_equal)
                last.then_inc(lohi_set, 1)

            def counts_out(g, h):
                for k in range(2):
                    last = nc.vector.tensor_scalar(
                        hist[k][:, :, bass.ds(g * GT, GT)],
                        bank[4 + 2 * k + h][0:LO, 0:GT * HI].rearrange("l (t h) -> l h t", h=HI),
                        1.0, None, ALU.mult)
                last.then_inc(hist_used, 1)

            with dve.Fori(0, NG // 2) as i:
                for h in range(2):
                    dve.wait_ge(hist_done, i * 2 + (h + 1))
                    one_hots(i * 2 + h, h)
                for h in range(2):
                    dve.wait_ge(hist_done, i * 2 + (h + 3))
                    counts_out(i * 2 + h, h)
            nc.vector.memset(runs[:, :, :], 1.0).then_inc(sec_step, 1)
            nc.vector.memset(zero_row[:, :], 0.0).then_inc(sec_step, 1)
            dve.wait_ge(sec_step, 2)
            link, count = links(dve, sec_step, 2)
            dve.wait_ge(hist_used, NG + 2)
            link(nc.vector.memset(runs[:, :, 0:1], 0.0))
            for k in range(2):
                link(nc.vector.tensor_tensor_scan(pref[k][:, :, :].rearrange("l h t -> l (h t)"),
                                                  runs[:, :, :].rearrange("l h t -> l (h t)"),
                                                  hist[k][:, :, :].rearrange("l h t -> l (h t)"), 0.0,
                                                  ALU.mult, ALU.add))
                link(nc.vector.tensor_reduce(cmax[:, k:k + 1], pref[k][:, :, ET - 1:ET].rearrange("l h o -> l (h o)"),
                                             AX_X, ALU.max))
                link(nc.vector.tensor_tensor(pref[k][:, :, :].rearrange("l h t -> l (h t)"),
                                             pref[k][:, :, :].rearrange("l h t -> l (h t)"),
                                             hist[k][:, :, :].rearrange("l h t -> l (h t)"), ALU.subtract))
            dve.sem_inc(cmax_set, 1)
            dve.wait_ge(cmax_turned, 1)
            link(nc.vector.tensor_copy(crow[:, :, :], bank[0][0:1, 0:2 * P].rearrange("o (k l) -> o k l", k=2)[:, :, 0:LO]))
            for k in range(2):
                link(nc.vector.tensor_reduce(sq[:, k, :], crow[:, k, :].rearrange("o (c l) -> o c l", l=LPC),
                                             AX_X, ALU.max))
            sqf = sq[:, :, :].rearrange("o k c -> o (k c)")
            link(nc.vector.tensor_scalar(sqf, sqf, float(P - 1), None, ALU.add))
            floor_div(sqf, sqf, P)
            link(nc.vector.tensor_scalar(sqf, sqf, 1.0, None, ALU.max))
            for k in range(2):
                link(nc.vector.tensor_tensor_scan(scum[:, k, :], sq[:, k, :], zero_row[:, :], 0.0, ALU.add, ALU.add))
                link(nc.vector.tensor_tensor(sbase[:, k, :], scum[:, k, :], sq[:, k, :], ALU.subtract))
                link(nc.vector.tensor_scalar(
                    sbase3[:, k, :].rearrange("o (c l) -> o c l", l=LPC),
                    sbase[:, k, :].unsqueeze(2).to_broadcast([1, NC, LPC]), float(P), None, ALU.mult))
            dve.sem_inc(sec_set, 1)
            link(nc.vector.tensor_tensor(scount[:, 0:1], scum[:, 0, NC - 1:NC], scum[:, 1, NC - 1:NC], ALU.max))
            link(nc.vector.tensor_scalar(scount[:, 1:2], scount[:, 0:1], 1.0, float(FIXED + 1), ALU.add, ALU.max))
            link(nc.vector.tensor_copy(sect_count[:, :], scount[:, :]))
            dve.wait_ge(sec_turned, 1)
            link(nc.vector.tensor_copy(basecol[:, :], bank[1][0:LO, 0:2]))
            link(nc.vector.tensor_copy(cumcol[:, :], bank[1][0:NC, 4:6]))
            for k in range(2):
                link(nc.vector.tensor_scalar(past[k][:, :], iota_s[:, :], cumcol[:, k:k + 1], None, ALU.is_ge))
            dve.sem_inc(past_set, 1)
            for k in range(2):
                link(nc.vector.tensor_scalar(pref[k][:, :, :].rearrange("l h t -> l (h t)"),
                                             pref[k][:, :, :].rearrange("l h t -> l (h t)"),
                                             basecol[:, k:k + 1], None, ALU.add))
            dve.wait_ge(past_summed, 1)
            for k in range(2):
                link(nc.vector.tensor_scalar(sect[:, k, :], bank[2 + k][0:1, 0:MAXSEC], float(NC - 1), None, ALU.min))
            dve.sem_inc(sect_set, 1)

            dve.wait_ge(edges_in[2], 16)

            def rank_group(g, i, h, first=False):
                link, count = links(dve, rank_step, g * RANK_STEPS)
                dve.wait_ge(rows_in[h], i * 64 + 64)
                for k in range(2):
                    nc.vector.tensor_scalar(oh_loT[k][:, :], lorow[k][h][:, :], part[0:LO, :], None, ALU.is_equal)
                    link(nc.vector.tensor_scalar(pg[k][:, :, :].rearrange("l t h -> l h t"),
                                                 pref[k][:, :, bass.ds(g * GT, GT)], 1.0, None, ALU.mult))
                dve.sem_inc(loT_set, 1)
                for k in range(2):
                    link(nc.vector.tensor_scalar(blk_g[k][:, :], blk[k][:, bass.ds(g * GT, GT)], 1.0, None, ALU.mult))
                    nc.vector.tensor_tensor(
                        hsel[k][:, :, :], iota_f[0:EP, 0:HI].unsqueeze(1).to_broadcast([EP, GT, HI]),
                        hi[k][:, bass.ds(g * GT, GT)].unsqueeze(2).to_broadcast([EP, GT, HI]), ALU.is_equal)
                    for t in range(GT):
                        last = nc.vector.scalar_tensor_tensor(
                            junk[:, t, :], blkrow[k][h][:, t * EP:(t + 1) * EP], blk_g[k][:, t:t + 1], ltri[:, :],
                            ALU.is_equal, ALU.mult, accum_out=in_tile[k][:, t:t + 1])
                    link(last)
                dve.sem_inc(rows_used, 1)
                dve.wait_ge(before_done, g + 1)
                for k in range(2):
                    link(nc.vector.tensor_tensor(hsel[k][:, :, :], hsel[k][:, :, :],
                                                 bank[4 + k][0:EP, 0:GT * HI].rearrange("e (t h) -> e t h", h=HI),
                                                 ALU.mult))
                    link(nc.vector.tensor_reduce(before[k][:, :], hsel[k][:, :, :], AX_X, ALU.add))
                    link(nc.vector.tensor_tensor(before[k][:, :], before[k][:, :], in_tile[k][:, :], ALU.add))
                    link(nc.vector.tensor_scalar(row21[k][:, :], bc[k][:, bass.ds(g * GT, GT)], 1.0, None, ALU.mult))
                    link(nc.vector.scalar_tensor_tensor(row21[k][:, :], before[k][:, :], float(BPC), row21[k][:, :],
                                                        ALU.mult, ALU.add))
                if not first:
                    dve.wait_ge(rec_out[h], i * (GT * 16))
                link(nc.vector.tensor_copy(srow[h][:, :], row21[0][:, :]))
                link(nc.vector.tensor_copy(rec[h][:, :, 2:3].bitcast(U32).rearrange("e t o -> e (t o)"), row21[1][:, :]))
                for c, a in ((0, jn[0]), (6, jn[1]), (7, jn[1])):
                    link(nc.vector.tensor_scalar(rec[h][:, :, c:c + 1].rearrange("e t o -> e (t o)"),
                                                 a[:, bass.ds(g * GT, GT)], 1.0, None, ALU.mult))
                link(nc.vector.tensor_scalar(rec[h][:, :, 1:2].bitcast(I32).rearrange("e t o -> e (t o)"),
                                             key_i[1][:, bass.ds(g * GT, GT)], 1.0, None, ALU.mult))
                link(nc.vector.tensor_scalar(rec[h][:, :, 3:3 + DIM], attr_sb[:, bass.ds(g * GT, GT), :], 1.0, None,
                                             ALU.mult))
                dve.sem_inc(rec_set, 1)
                return count[0]

            RANK_STEPS = 23
            for h in range(2):
                rank_group(h, 0, h, first=True)
            with dve.Fori(1, NG // 2) as i:
                for h in range(2):
                    n = rank_group(i * 2 + h, i, h)
                    assert n == RANK_STEPS, n



class Keep:
    pass


def keep_tiles(nc, ctx):
    k = Keep()

    def sb(name, shape, dt=F32):
        return ctx.enter_context(nc.sbuf_tensor(name, shape, dt))

    k.sect = sb("sect", [1, 2, MAXSEC], I32)
    k.sect_count = sb("sect_count", [1, 2], I32)
    k.ident = sb("ident", [P, P])
    return k


def keep_node_tiles(nc, ctx, k):
    def sb(name, shape, dt=F32):
        return ctx.enter_context(nc.sbuf_tensor(name, shape, dt))

    k.iota_j = sb("iota_j", [P, NB])
    k.bmask = sb("bmask", [CN, BPC])
    k.pieces = sb("pieces", [P, 4, KS])
    k.x = sb("x_sb", [CN, NC, FEAT])
    k.x1 = sb("x1", [CN, NC, FEAT])
    k.tab_a = sb("tab_a", [CN, NC, TROW])
    k.er = sb("er", [CN, NC, HEADS])
    k.hT = sb("hT", [FEAT, NC, CN])
    k.inv_deg = sb("inv_deg", [CN, NC])
    k.shift = sb("shift", [CN, NC, DIM])


def hat_weights(nc, link, k, pos, w, rise, fall, blocks):
    def knots(row):
        return k.pieces[:, row:row + 1, :].to_broadcast([P, blocks * DIM, KS])
    wv, rv, fv = (t.rearrange("p b d i -> p (b d) i") for t in (w, rise, fall))
    pv = pos.rearrange("p b d -> p (b d)").unsqueeze(2).to_broadcast([P, blocks * DIM, KS])
    nc.vector.tensor_tensor(rv, pv, knots(0), ALU.add)
    link(nc.vector.tensor_tensor(fv, knots(2), pv, ALU.subtract))
    nc.vector.tensor_tensor(rv, rv, knots(1), ALU.max)
    link(nc.vector.tensor_tensor(fv, fv, knots(3), ALU.max))
    link(nc.vector.tensor_tensor(wv, rv, fv, ALU.min))


def layer_norm(nc, dve, link, x, xm, sq, stat, h, var_set, sd_set, at):
    shape = [CN, NC, FEAT]
    link(nc.vector.tensor_reduce(stat[:, 0, :], x, AX_X, ALU.add))
    link(nc.vector.tensor_scalar(stat[:, 0, :], stat[:, 0, :], 1.0 / FEAT, None, ALU.mult))
    link(nc.vector.tensor_tensor(xm[:, :, :], x, stat[:, 0, :].unsqueeze(2).to_broadcast(shape), ALU.subtract))
    link(nc.vector.tensor_tensor(sq[:, :, :], xm[:, :, :], xm[:, :, :], ALU.mult))
    link(nc.vector.tensor_reduce(stat[:, 1, :], sq[:, :, :], AX_X, ALU.add))
    link(nc.vector.tensor_scalar(stat[:, 1, :], stat[:, 1, :], 1.0 / FEAT, 1e-5, ALU.mult, ALU.add))
    dve.sem_inc(var_set, 1)
    dve.wait_ge(sd_set, at)
    link(nc.vector.reciprocal(stat[:, 3, :], stat[:, 2, :]))
    link(nc.vector.tensor_tensor(xm[:, :, :], xm[:, :, :], stat[:, 3, :].unsqueeze(2).to_broadcast(shape), ALU.mult))
    link(nc.vector.tensor_scalar(h, xm[:, :, :], 0.0, None, ALU.max))


def rows_of(dram, f):
    return dram.rearrange("(c p) f -> p c f", p=CN)


def build_send(nc, a, k, slots_dram, drows_dram, h1_dram):
    with ExitStack() as ctx:
        def sb(name, shape, dt=F32):
            return ctx.enter_context(nc.sbuf_tensor(name, shape, dt))

        def sem(name):
            return ctx.enter_context(nc.semaphore(name))

        xm = sb("xm", [CN, NC, FEAT])
        sq = sb("sq2", [CN, NC, FEAT])
        stat = sb("stat", [CN, 4, NC])
        wgat = sb("wgat", [FEAT, HEADS, FEAT])
        attn = sb("attn", [FEAT, 2, HEADS, FEAT])
        wat = sb("wat", [FEAT, 2, HEADS, FEAT])
        wa = sb("wa", [FEAT, 2 * HEADS])
        w1 = sb("w1", [K + 1, HID + 1])
        b1 = sb("b1", [CN, HID])
        slot = sb("slot", [P, BPC, SREC])
        oh = sb("oh", [P, BPC, NB])
        ohT = sb("ohT", [CN, P])
        bd = sb("bd", [CN, BPC, TROW])
        posd = [sb(f"posd{g}", [P, GB], U32) for g in range(NGR)]
        load = [sb(f"load{g}", [P, GB, DREC]) for g in range(NGR)]
        pos = sb("pos", [P, BPC, DIM])
        rise = sb("rise", [P, BPC, DIM, KS])
        fall = sb("fall", [P, BPC, DIM, KS])
        hat = sb("hat", [P, BPC, DIM, KS])
        uv = [sb(f"uv{g}", [P, GB, KS, KS]) for g in range(NGR)]
        bas = [sb(f"bas{g}", [P, GB, K + 1]) for g in range(NGR)]
        t1 = sb("t1", [K + 1, CN])
        acc = sb("acc", [CN, NC, HID + 1])
        v1 = sb("v1", [CN, NC, HID])
        e1 = sb("e1", [CN, NC, HID])
        bank = [ctx.enter_context(nc.psum_tensor(f"send_bank{i}", [P, 512], F32)) for i in range(8)]

        x_in = sem("x_in")
        w_in = sem("w_in")
        w1_in = sem("w1_in")
        const_step = sem("const_step")
        x_pad = sem("x_pad")
        var_set = sem("var_set")
        sd_set = sem("sd_set")
        ln_step = sem("ln_step")
        h_set = sem("h_set")
        turned = sem("turned")
        hT_set = sem("hT_set")
        el_done = sem("el_done")
        el_out = sem("el_out")
        slot_in = sem("slot_in")
        slot_used = sem("slot_used")
        oh_set = sem("oh_set")
        ohT_done = sem("ohT_done")
        ohT_set = sem("ohT_set")
        bd_set = sem("bd_set")
        spread_done = sem("spread_done")
        load_set = sem("load_set")
        posd_set = sem("posd_set")
        sent = [sem(f"sent{g}") for g in range(NGR)]
        bas_set = sem("bas_set")
        t1_done = sem("t1_done")
        t1_set = sem("t1_set")
        out1_done = sem("out1_done")
        acc_set = sem("acc_set")
        sec_step = sem("sec_step2")
        neg_set = sem("neg_set")
        exp_set = sem("exp_set")
        h1_set = sem("h1_set")
        h1_out = sem("h1_out")
        end_step = sem("end_step")

        block = ctx.enter_context(nc.Block())

        @block.sync
        def _(sp):
            sp.wait_ge(x_pad, 1)
            sp.dma_start(k.x[:, 0:NC - 1, :], a["x"][0:(NC - 1) * CN, :].rearrange("(c p) f -> p c f", p=CN))\
              .then_inc(x_in, 16)
            sp.dma_start(k.x[0:LAST, NC - 1, :], a["x"][(NC - 1) * CN:N, :]).then_inc(x_in, 16)
            sp.dma_start(wgat[:, :, :], a["L0_gnn_W_gat"].rearrange("i (h o) -> i h o", h=HEADS)).then_inc(w_in, 16)
            for i, name in enumerate(("L0_gnn_attn_l", "L0_gnn_attn_r")):
                sp.dma_start(attn[:, i, :, :].rearrange("p h f -> p (h f)"),
                             a[name].rearrange("(o h) f -> o (h f)", o=1).to_broadcast([FEAT, HEADS * FEAT]))\
                  .then_inc(w_in, 16)
            sp.wait_ge(const_step, 4)
            sp.dma_start(w1[0:K, 0:HID], a["L1_gnn_stn1_w"].rearrange("k o f -> k (o f)")).then_inc(w1_in, 16)
            sp.dma_start(b1[:, :], a["L1_gnn_stn1_b"].rearrange("(o f) -> o f", o=1).to_broadcast([CN, HID]))\
              .then_inc(w1_in, 16)

            def load_slots(s):
                sp.dma_start(slot[:, :, :].rearrange("p b w -> p (b w)"),
                             slots_dram[bass.ds(s * SROWS, SROWS), :].rearrange("(p b) w -> p (b w)", b=BPC))\
                  .then_inc(slot_in, 16)

            sections = sp.value_load(k.sect_count[0:1, 0:1], min_val=NC, max_val=MAXSEC)
            load_slots(0)
            with sp.Fori(1, sections) as s:
                sp.wait_ge(slot_used, s)
                load_slots(s)
            sp.wait_ge(h1_set, 1)
            sp.dma_start(rows_of(h1_dram, HID), v1[:, :, :]).then_inc(h1_out, 16)
            sp.wait_ge(h1_out, 16)

        @block.gpsimd
        def _(pool):
            nc.gpsimd.memset(k.x[:, NC - 1, :], 0.0).then_inc(x_pad, 1)
            nc.gpsimd.iota(k.iota_j[:, :], pattern=[[1, NB]], base=0, channel_multiplier=0,
                           allow_small_or_imprecise_dtypes=True).then_inc(const_step, 1)
            nc.gpsimd.memset(k.bmask[:, :], 1.0).then_inc(const_step, 1)
            nc.gpsimd.memset(w1[:, :], 0.0).then_inc(const_step, 1)
            pool.wait_ge(const_step, 3)
            nc.gpsimd.affine_select(out=w1[:, HID:HID + 1], in_=w1[:, HID:HID + 1], compare_op=ALU.not_equal, fill=1.0,
                                    base=-K, pattern=[[0, 1]], channel_multiplier=1).then_inc(const_step, 1)
            nc.gpsimd.affine_select(out=k.bmask[:, :], in_=k.bmask[:, :], compare_op=ALU.is_ge, fill=0.0,
                                    base=0, pattern=[[-NB, BPC]], channel_multiplier=1).then_inc(const_step, 1)
            pool.wait_ge(const_step, 5)
            nc.gpsimd.affine_select(out=k.bmask[:, :], in_=k.bmask[:, :], compare_op=ALU.is_ge, fill=0.0,
                                    base=NB - 1, pattern=[[NB, BPC]], channel_multiplier=-1).then_inc(const_step, 1)
            sections = pool.value_load(k.sect_count[0:1, 0:1], min_val=NC, max_val=MAXSEC)

            def send(s):
                for g in range(NGR):
                    pool.wait_ge(load_set, s * NGR + (g + 1))
                    pool.wait_ge(posd_set, s * NGR + (g + 1))
                    pool.nop(nofuse=True)
                    for b in range(GB):
                        nc.gpsimd.indirect_dma_start(
                            drows_dram[:, :], bass.IndirectOffsetOnAxis(ap=posd[g][:, b:b + 1], axis=0),
                            load[g][:, b, :], None, bounds_check=MAXSEC * SROWS - 1, oob_is_err=False)\
                            .then_inc(sent[g], 16)
            send(0)
            with pool.Fori(1, sections) as s:
                send(s)
            for g in range(NGR):
                pool.wait_ge(sent[g], sections * (GB * 16))

        @block.scalar
        def _(act):
            act.wait_ge(var_set, 1)
            nc.scalar.activation(stat[:, 2, :], stat[:, 1, :], ACT.Sqrt).then_inc(sd_set, 1)
            for q in range(-(-NC // 4)):
                cs = range(4 * q, min(4 * q + 4, NC))
                act.wait_ge(turned, q + 1)
                nc.scalar.copy(k.hT[:, cs[0]:cs[-1] + 1, :].rearrange("f c n -> f (c n)"),
                               bank[q % 2][0:FEAT, 0:len(cs) * CN]).then_inc(hT_set, 1)
            sections = act.value_load(k.sect_count[0:1, 0:1], min_val=NC, max_val=MAXSEC)

            def section(s, first):
                act.wait_ge(ohT_done, s + 1)
                if not first:
                    act.wait_ge(spread_done, s * NGR)
                nc.scalar.copy(ohT[:, :], bank[0][0:CN, 0:P]).then_inc(ohT_set, 1)
                for g in range(NGR):
                    act.wait_ge(spread_done, s * NGR + (g + 1))
                    if not first:
                        act.wait_ge(sent[g], s * (GB * 16))
                    nc.scalar.copy(load[g][:, :, 0:TROW],
                                   bank[1 + g][:, 0:GB * TROW].rearrange("p (b f) -> p b f", b=GB)).then_inc(load_set, 1)
                act.wait_ge(t1_done, s + 1)
                if not first:
                    act.wait_ge(out1_done, s)
                nc.scalar.copy(t1[:, :], bank[4][0:K + 1, 0:CN]).then_inc(t1_set, 1)

            section(0, True)
            with act.Fori(1, sections) as s:
                section(s, False)
            act.wait_ge(neg_set, 1)
            nc.scalar.activation(e1[:, :, :], e1[:, :, :], ACT.Exp).then_inc(exp_set, 1)

        @block.tensor
        def _(pe):
            pe.wait_ge(h_set, 1)
            for q in range(-(-NC // 4)):
                cs = range(4 * q, min(4 * q + 4, NC))
                if q >= 2:
                    pe.wait_ge(hT_set, q - 1)
                for c in cs:
                    last = nc.tensor.transpose(bank[q % 2][0:FEAT, (c - cs[0]) * CN:(c - cs[0] + 1) * CN],
                                               k.tab_a[:, c, 0:FEAT], k.ident[0:CN, 0:CN])
                last.then_inc(turned, 1)
            pe.wait_ge(hT_set, -(-NC // 4))
            for c in range(NC):
                last = nc.tensor.matmul(bank[2][0:CN, c * 8:(c + 1) * 8], k.hT[:, c, :], wa[:, :], start=True, stop=True)
            last.then_inc(el_done, 1)
            pe.wait_ge(w1_in, 32)
            sections = pe.value_load(k.sect_count[0:1, 0:1], min_val=NC, max_val=MAXSEC)

            def section(s, first):
                pe.wait_ge(oh_set, s + 1)
                if first:
                    pe.wait_ge(el_out, 1)
                nc.tensor.transpose(bank[0][0:CN, 0:P], oh[:, :, :].rearrange("p b j -> p (b j)"), k.ident[:, :])\
                    .then_inc(ohT_done, 1)
                pe.wait_ge(ohT_set, s + 1)
                pe.wait_ge(bd_set, s + 1)
                for g in range(NGR):
                    if not first:
                        pe.wait_ge(load_set, s * NGR - (NGR - 1 - g))
                    nc.tensor.matmul(bank[1 + g][:, 0:GB * TROW], ohT[:, :],
                                     bd[:, g * GB:(g + 1) * GB, :].rearrange("n b f -> n (b f)"),
                                     start=True, stop=True).then_inc(spread_done, 1)
                if not first:
                    pe.wait_ge(t1_set, s)
                for g in range(NGR):
                    pe.wait_ge(bas_set, s * NGR + (g + 1))
                    for b in range(g * GB, (g + 1) * GB):
                        last = nc.tensor.matmul(bank[4][0:K + 1, b * NB:(b + 1) * NB], bas[g][:, b - g * GB, :],
                                                oh[:, b, :], start=True, stop=True)
                last.then_inc(t1_done, 1)
                pe.wait_ge(t1_set, s + 1)
                if not first:
                    pe.wait_ge(acc_set, s)
                nc.tensor.matmul(bank[5][0:CN, 0:HID + 1], t1[:, :], w1[:, :], start=True, stop=True)\
                    .then_inc(out1_done, 1)

            section(0, True)
            with pe.Fori(1, sections) as s:
                section(s, False)

        @block.vector
        def _(dve):
            link, count = links(dve, ln_step)
            for row, (v, odd, at) in enumerate(((0.0, 0.0, None), (0.0, -BIG, 1), (0.0, 0.0, None), (0.0, -BIG, 3))):
                if row in (0, 2):
                    for i in range(KS):
                        val = (BIG if i == 0 else 1.0 - i) if row == 0 else (BIG if i == KS - 1 else 1.0 + i)
                        last = nc.vector.memset(k.pieces[:, row, i:i + 1], val)
                else:
                    link(nc.vector.memset(k.pieces[:, row, :], v))
                    last = nc.vector.memset(k.pieces[:, row, at:at + 1], odd)
            for g in range(NGR):
                last = nc.vector.memset(bas[g][:, :, K:K + 1], 1.0)
            nc.vector.memset(k.tab_a[:, :, FEAT:FEAT + 1], 1.0)
            link(nc.vector.memset(acc[:, :, :], 0.0))
            dve.wait_ge(w_in, 48)
            for i in range(2):
                link(nc.vector.tensor_tensor(wat[:, i, :, :], wgat[:, :, :], attn[:, i, :, :], ALU.mult))
            link(nc.vector.tensor_reduce(wa[:, :], wat[:, :, :, :].rearrange("p i h f -> p (i h) f"), AX_X, ALU.add))
            dve.wait_ge(x_in, 32)
            layer_norm(nc, dve, link, k.x[:, :, :], xm, sq, stat, k.tab_a[:, :, 0:FEAT], var_set, sd_set, 1)
            dve.sem_inc(h_set, 1)
            dve.wait_ge(el_done, 1)
            el = bank[2][0:CN, 0:NC * 8].rearrange("n (c w) -> n c w", w=8)
            link(nc.vector.tensor_copy(k.tab_a[:, :, FEAT + 1:TROW], el[:, :, 0:HEADS]))
            link(nc.vector.tensor_copy(k.er[:, :, :], el[:, :, HEADS:2 * HEADS]))
            dve.sem_inc(el_out, 1)
            dve.wait_ge(const_step, 6)
            sections = dve.value_load(k.sect_count[0:1, 0:1], min_val=NC, max_val=MAXSEC)

            def add_out(s_last):
                c = dve.value_load(k.sect[0:1, 0, bass.ds(s_last, 1)], min_val=0, max_val=NC - 1)
                sl = acc[:, bass.ds(c, 1), :].rearrange("n c f -> n (c f)")
                return nc.vector.tensor_tensor(sl, sl, bank[5][0:CN, 0:HID + 1], ALU.add)

            def section(s, first):
                link, count = links(dve, sec_step, s * SEND_STEPS)
                c = dve.value_load(k.sect[0:1, 0, bass.ds(s, 1)], min_val=0, max_val=NC - 1)
                dve.wait_ge(slot_in, s * 16 + 16)
                if not first:
                    dve.wait_ge(t1_done, s)
                link(nc.vector.tensor_tensor(oh[:, :, :], k.iota_j[:, :].unsqueeze(1).to_broadcast([P, BPC, NB]),
                                             slot[:, :, 0:1].to_broadcast([P, BPC, NB]), ALU.is_equal))
                dve.sem_inc(oh_set, 1)
                if not first:
                    dve.wait_ge(spread_done, s * NGR)
                link(nc.vector.tensor_tensor(
                    bd[:, :, :], k.tab_a[:, bass.ds(c, 1), :].to_broadcast([CN, BPC, TROW]),
                    k.bmask[:, :].unsqueeze(2).to_broadcast([CN, BPC, TROW]), ALU.mult))
                dve.sem_inc(bd_set, 1)
                for g in range(NGR):
                    if not first:
                        dve.wait_ge(sent[g], s * (GB * 16))
                    part = slot[:, g * GB:(g + 1) * GB, :]
                    nc.vector.tensor_copy(load[g][:, :, DREC - 1:DREC], part[:, :, 6:7])
                    nc.vector.tensor_copy(posd[g][:, :], part[:, :, 2:3].bitcast(U32).rearrange("p b o -> p (b o)"))\
                        .then_inc(posd_set, 1)
                dve.wait_ge(posd_set, s * NGR + NGR)
                link(nc.vector.tensor_scalar(pos[:, :, :], slot[:, :, 3:3 + DIM], float(KS - 1), None, ALU.mult))
                dve.sem_inc(slot_used, 1)
                hat_weights(nc, link, k, pos[:, :, :], hat[:, :, :, :], rise[:, :, :, :], fall[:, :, :, :], BPC)
                for g in range(NGR):
                    w = hat[:, g * GB:(g + 1) * GB, :, :]
                    link(nc.vector.tensor_tensor(uv[g][:, :, :, :], w[:, :, 0, :].unsqueeze(3).to_broadcast([P, GB, KS, KS]),
                                                 w[:, :, 1, :].unsqueeze(2).to_broadcast([P, GB, KS, KS]), ALU.mult))
                    nc.vector.tensor_tensor(
                        bas[g][:, :, 0:K].rearrange("p b (u i) -> p b u i", i=KS),
                        uv[g][:, :, :, :].rearrange("p b i j -> p b (i j)").unsqueeze(3).to_broadcast([P, GB, KS * KS, KS]),
                        w[:, :, 2, :].unsqueeze(2).to_broadcast([P, GB, KS * KS, KS]), ALU.mult).then_inc(bas_set, 1)
                if not first:
                    dve.wait_ge(out1_done, s)
                    link(add_out(s - 1))
                    dve.sem_inc(acc_set, 1)
                else:
                    dve.sem_inc(sec_step, 1)
                return count[0]

            SEND_STEPS = 10
            section(0, True)
            with dve.Fori(1, sections) as s:
                n = section(s, False)
                assert n == SEND_STEPS, n
            link, count = links(dve, end_step)
            dve.wait_ge(out1_done, sections)
            link(add_out(sections - 1))
            link(nc.vector.tensor_scalar(k.inv_deg[:, :], acc[:, :, HID:HID + 1].rearrange("n c o -> n (c o)"), 1.0, None,
                                         ALU.max))
            link(nc.vector.reciprocal(k.inv_deg[:, :], k.inv_deg[:, :]))
            link(nc.vector.tensor_tensor(v1[:, :, :], acc[:, :, 0:HID],
                                         k.inv_deg[:, :].unsqueeze(2).to_broadcast([CN, NC, HID]), ALU.mult))
            link(nc.vector.tensor_tensor(v1[:, :, :], v1[:, :, :], b1[:, :].unsqueeze(1).to_broadcast([CN, NC, HID]),
                                         ALU.add))
            link(nc.vector.tensor_scalar(e1[:, :, :], v1[:, :, :], 0.0, None, ALU.min))
            dve.sem_inc(neg_set, 1)
            link(nc.vector.tensor_scalar(v1[:, :, :], v1[:, :, :], 0.0, None, ALU.max))
            dve.wait_ge(exp_set, 1)
            link(nc.vector.scalar_tensor_tensor(v1[:, :, :], e1[:, :, :], -1.0, v1[:, :, :], ALU.add, ALU.add))
            dve.sem_inc(h1_set, 1)


def conv_tiles(nc, ctx, fi, prefix):
    t = Keep()

    def sb(name, shape, dt=F32):
        return ctx.enter_context(nc.sbuf_tensor(prefix + name, shape, dt))

    t.slot = sb("slot", [P, BPC, SREC])
    t.slot_ix = sb("slot_ix", [P, BPC, SREC])
    t.index = [sb(f"index{g}", [P, GB], U32) for g in range(NGR)]
    t.oh = sb("oh", [P, BPC, NB])
    t.rise = sb("rise", [P, BPC, DIM, KS])
    t.fall = sb("fall", [P, BPC, DIM, KS])
    t.hat = sb("hat", [P, BPC, DIM, KS])
    t.uv = [sb(f"uv{g}", [P, GB, KS, KS]) for g in range(NGR)]
    t.bas = [sb(f"bas{g}", [P, GB, K]) for g in range(NGR)]
    t.mixed = [sb(f"mixed{g}", [P, GB, NB, fi]) for g in range(NGR)]
    t.sums = sb("sums", [K, CN, fi])
    return t


def basis_group(nc, t, g, link):
    w = t.hat[:, g * GB:(g + 1) * GB, :, :]
    link(nc.vector.tensor_tensor(t.uv[g][:, :, :, :], w[:, :, 0, :].unsqueeze(3).to_broadcast([P, GB, KS, KS]),
                                 w[:, :, 1, :].unsqueeze(2).to_broadcast([P, GB, KS, KS]), ALU.mult))
    return nc.vector.tensor_tensor(
        t.bas[g][:, :, :].rearrange("p b (u i) -> p b u i", i=KS),
        t.uv[g][:, :, :, :].rearrange("p b i j -> p b (i j)").unsqueeze(3).to_broadcast([P, GB, KS * KS, KS]),
        w[:, :, 2, :].unsqueeze(2).to_broadcast([P, GB, KS * KS, KS]), ALU.mult)


def build_mid(nc, a, k, slots_dram, drows_dram, h1_dram, m_dram, acc, gacc):
    with ExitStack() as ctx:
        def sb(name, shape, dt=F32):
            return ctx.enter_context(nc.sbuf_tensor(name, shape, dt))

        def sem(name):
            return ctx.enter_context(nc.semaphore(name))

        t = conv_tiles(nc, ctx, HID, "mid_")
        rows = [sb(f"mid_rows{g}", [P, GB, HID]) for g in range(NGR)]
        w2 = sb("w2", [K, HID, HID])
        pos = sb("mid_pos", [P, BPC, DIM])
        drow = sb("drow", [P, BPC, DREC])
        ohd = sb("ohd", [P, BPC, NB])
        pen = sb("pen", [P, BPC, NB])
        masked = sb("masked", [P, BPC, NB, HEADS])
        top = sb("top", [NB * HEADS * GMX, NGM])
        tops = sb("tops", [NB * HEADS * GMX, NC, NGM])
        topT = sb("topT", [P, 2, NB * HEADS * GMX])
        m_el = sb("m_el", [CN, NC, HEADS])
        er_m = sb("er_m", [CN, NC, 2 * HEADS])
        ohdT = sb("ohdT", [CN, P])
        bde = sb("bde", [CN, BPC, 2 * HEADS])
        score = sb("score", [P, BPC, HEADS])
        wexp = sb("wexp", [P, BPC, HEADS])
        bank = [ctx.enter_context(nc.psum_tensor(f"mid_bank{i}", [P, 512], F32)) for i in range(8)]

        w2_in = sem("w2_in")
        slot_in = sem("mid_slot_in")
        slot_used = sem("mid_slot_used")
        ix_in = sem("mid_ix_in")
        index_set = sem("mid_index_set")
        rows_in = [sem(f"mid_rows_in{g}") for g in range(NGR)]
        mixed_set = sem("mid_mixed_set")
        sum_done = sem("mid_sum_done")
        sum_set = sem("mid_sum_set")
        out_done = sem("mid_out_done")
        acc_set = sem("mid_acc_set")
        mid_step = sem("mid_step")
        max_step = sem("max_step")
        init_step = sem("mid_init_step")
        drow_in = sem("drow_in")
        drow_used = sem("drow_used")
        masked_set = sem("masked_set")
        masked_turned = sem("masked_turned")
        tops_set = sem("tops_set")
        tops_turned = sem("tops_turned")
        topT_set = sem("topT_set")
        m_out = sem("m_out")
        m_in = sem("m_in")
        w_in = sem("att_in")
        ohd_set = sem("ohd_set")
        ohdT_done = sem("ohdT_done")
        ohdT_set = sem("ohdT_set")
        bde_set = sem("bde_set")
        erm_done = sem("erm_done")
        score_set = sem("score_set")
        wexp_set = sem("wexp_set")
        weights_set = sem("weights_set")
        att_done = sem("att_done")
        gacc_set = sem("gacc_set")

        block = ctx.enter_context(nc.Block())
        MW = NB * HEADS * GMX

        @block.sync
        def _(sp):
            def load_slots(s, tile, signal):
                sp.dma_start(tile[:, :, :].rearrange("p b w -> p (b w)"),
                             slots_dram[bass.ds(s * SROWS, SROWS), :].rearrange("(p b) w -> p (b w)", b=BPC))\
                  .then_inc(signal, 16)

            def load_drows(s, signal):
                sp.dma_start(drow[:, :, :].rearrange("p b w -> p (b w)"),
                             drows_dram[bass.ds(s * SROWS, SROWS), :].rearrange("(p b) w -> p (b w)", b=BPC))\
                  .then_inc(signal, 16)

            sections = sp.value_load(k.sect_count[0:1, 0:1], min_val=NC, max_val=MAXSEC)
            load_slots(0, t.slot_ix, ix_in)
            load_drows(0, drow_in)
            load_slots(0, t.slot, slot_in)
            sp.dma_start(w2[:, :, :], a["L1_gnn_stn2_w"]).then_inc(w2_in, 16)
            with sp.Fori(1, sections) as s:
                sp.wait_ge(drow_used, s)
                load_drows(s, drow_in)
            sp.wait_ge(topT_set, 2)
            sp.dma_start(m_dram[0:P, :], topT[:, 0, :]).then_inc(m_out, 16)
            sp.dma_start(m_dram[P:NC * NGM, :], topT[0:NC * NGM - P, 1, :]).then_inc(m_out, 16)
            sp.wait_ge(m_out, 32)
            sp.dma_start(m_el[:, :, :],
                         m_dram.rearrange("(c q) w -> c (q w)", c=NC).rearrange("c (n h) -> n c h", h=HEADS))\
              .then_inc(m_in, 16)
            sp.wait_ge(drow_used, sections)
            load_drows(0, w_in)
            sp.wait_ge(index_set, NGR)
            load_slots(1, t.slot_ix, ix_in)
            with sp.Fori(1, sections) as s:
                sp.wait_ge(slot_used, s)
                load_slots(s, t.slot, slot_in)
                sp.wait_ge(index_set, s * NGR + NGR)
                load_slots(s + 1, t.slot_ix, ix_in)
                sp.wait_ge(att_done, s)
                load_drows(s, w_in)
            sp.wait_ge(ix_in, sections * 16 + 16)
            sp.nop(nofuse=True)

        @block.gpsimd
        def _(pool):
            sections = pool.value_load(k.sect_count[0:1, 0:1], min_val=NC, max_val=MAXSEC)

            def fetch(s, first):
                for g in range(NGR):
                    pool.wait_ge(index_set, s * NGR + (g + 1))
                    if not first:
                        pool.wait_ge(mixed_set, s * NGR - (NGR - 1 - g))
                    pool.nop(nofuse=True)
                    for b in range(GB):
                        nc.gpsimd.indirect_dma_start(
                            rows[g][:, b, :], None, h1_dram[:, :],
                            bass.IndirectOffsetOnAxis(ap=t.index[g][:, b:b + 1], axis=0)).then_inc(rows_in[g], 16)
            fetch(0, True)
            with pool.Fori(1, sections) as s:
                fetch(s, False)

        @block.scalar
        def _(act):
            def indices(g):
                nc.scalar.copy(t.index[g][:, :], t.slot_ix[:, g * GB:(g + 1) * GB, 1:2].bitcast(U32)
                               .rearrange("p b o -> p (b o)")).then_inc(index_set, 1)

            act.wait_ge(ix_in, 16)
            for g in range(NGR):
                indices(g)
            act.wait_ge(tops_turned, 1)
            nc.scalar.copy(topT[:, 0, :], bank[0][:, 0:MW]).then_inc(topT_set, 1)
            nc.scalar.copy(topT[0:NC * NGM - P, 1, :], bank[0][0:NC * NGM - P, MW:2 * MW]).then_inc(topT_set, 1)
            sections = act.value_load(k.sect_count[0:1, 0:1], min_val=NC, max_val=MAXSEC)

            def section(s, first):
                act.wait_ge(ohdT_done, s + 1)
                if not first:
                    act.wait_ge(erm_done, s)
                nc.scalar.copy(ohdT[:, :], bank[4][0:CN, 0:P]).then_inc(ohdT_set, 1)
                for g in range(NGR):
                    for b in range(g * GB, (g + 1) * GB):
                        act.wait_ge(sum_done, s * BPC + (b + 1))
                        if b == 0 and not first:
                            act.wait_ge(out_done, s)
                        nc.scalar.copy(t.sums[:, b * NB:(b + 1) * NB, :].rearrange("k n f -> k (n f)"),
                                       bank[b % 3][0:K, 0:NB * HID]).then_inc(sum_set, 1)
                    act.wait_ge(ix_in, s * 16 + 32)
                    act.wait_ge(rows_in[g], s * (GB * 16) + GB * 16)
                    indices(g)
                    if g == 0:
                        act.wait_ge(score_set, s + 1)
                        nc.scalar.activation(wexp[:, :, :], score[:, :, :], ACT.Exp).then_inc(wexp_set, 1)

            section(0, True)
            with act.Fori(1, sections) as s:
                section(s, False)

        @block.tensor
        def _(pe):
            sections = pe.value_load(k.sect_count[0:1, 0:1], min_val=NC, max_val=MAXSEC)

            def turn(s, first):
                pe.wait_ge(masked_set, s + 1)
                if not first:
                    pe.wait_ge(tops_set, s)
                for q in range(NGM):
                    last = nc.tensor.transpose(
                        bank[q // 4][0:MW, (q % 4) * P:(q % 4 + 1) * P],
                        masked[:, q * GMX:(q + 1) * GMX, :, :].rearrange("p b j h -> p (b j h)"), k.ident[:, :])
                last.then_inc(masked_turned, 1)
            turn(0, True)
            with pe.Fori(1, sections) as s:
                turn(s, False)
            pe.wait_ge(tops_set, sections)
            flat = tops[:, :, :].rearrange("w c q -> w (c q)")
            nc.tensor.transpose(bank[0][0:P, 0:MW], flat[:, 0:P], k.ident[0:MW, 0:MW])
            nc.tensor.transpose(bank[0][0:NC * NGM - P, MW:2 * MW], flat[:, P:NC * NGM], k.ident[0:MW, 0:MW])\
                .then_inc(tops_turned, 1)
            pe.wait_ge(topT_set, 2)
            pe.wait_ge(w2_in, 16)

            def section(s, first):
                pe.wait_ge(ohd_set, s + 1)
                nc.tensor.transpose(bank[4][0:CN, 0:P], ohd[:, :, :].rearrange("p b j -> p (b j)"), k.ident[:, :])\
                    .then_inc(ohdT_done, 1)
                for g in range(NGR):
                    pe.wait_ge(mixed_set, s * NGR + (g + 1))
                    for b in range(g * GB, (g + 1) * GB):
                        if b >= 3 or not first:
                            pe.wait_ge(sum_set, s * BPC + (b - 2))
                        nc.tensor.matmul(bank[b % 3][0:K, 0:NB * HID], t.bas[g][:, b - g * GB, :],
                                         t.mixed[g][:, b - g * GB, :, :].rearrange("p j f -> p (j f)"),
                                         start=True, stop=True).then_inc(sum_done, 1)
                    if g == 0:
                        pe.wait_ge(ohdT_set, s + 1)
                        pe.wait_ge(bde_set, s + 1)
                        nc.tensor.matmul(bank[5][:, 0:BPC * 2 * HEADS], ohdT[:, :],
                                         bde[:, :, :].rearrange("n b w -> n (b w)"), start=True, stop=True)\
                            .then_inc(erm_done, 1)
                pe.wait_ge(weights_set, s + 1)
                if not first:
                    pe.wait_ge(gacc_set, s)
                for b in range(BPC):
                    last = nc.tensor.matmul(bank[6][0:FEAT + 1, b * NB * HEADS:(b + 1) * NB * HEADS],
                                            drow[:, b, 0:FEAT + 1],
                                            masked[:, b, :, :].rearrange("p j h -> p (j h)"), start=True, stop=True)
                last.then_inc(att_done, 1)
                pe.wait_ge(sum_set, s * BPC + BPC)
                if not first:
                    pe.wait_ge(acc_set, s)
                for i in range(HID):
                    last = nc.tensor.matmul(bank[3][0:CN, 0:HID], t.sums[:, :, i], w2[:, i, :],
                                            start=(i == 0), stop=(i == HID - 1))
                last.then_inc(out_done, 1)

            section(0, True)
            with pe.Fori(1, sections) as s:
                section(s, False)

        @block.vector
        def _(dve):
            sections = dve.value_load(k.sect_count[0:1, 0:1], min_val=NC, max_val=MAXSEC)
            link, count = links(dve, init_step)
            nc.vector.memset(acc[:, :, :], 0.0)
            nc.vector.memset(gacc[:, :, :], 0.0)
            link(nc.vector.memset(tops[:, :, :], -BIG))

            def one_hot_d():
                return nc.vector.tensor_tensor(
                    ohd[:, :, :], k.iota_j[:, :].unsqueeze(1).to_broadcast([P, BPC, NB]),
                    drow[:, :, DREC - 1:DREC].to_broadcast([P, BPC, NB]), ALU.is_equal)

            def find_max(s, first):
                link, count = links(dve, max_step, s * 5)
                c = dve.value_load(k.sect[0:1, 1, bass.ds(s, 1)], min_val=0, max_val=NC - 1)
                dve.wait_ge(drow_in, s * 16 + 16)
                link(one_hot_d())
                link(nc.vector.tensor_scalar(pen[:, :, :], ohd[:, :, :], -1.0, BIG, ALU.add, ALU.mult))
                link(nc.vector.tensor_tensor(
                    masked[:, :, :, :], pen[:, :, :].unsqueeze(3).to_broadcast([P, BPC, NB, HEADS]),
                    drow[:, :, FEAT + 1:TROW].unsqueeze(2).to_broadcast([P, BPC, NB, HEADS]), ALU.add))
                dve.sem_inc(masked_set, 1)
                dve.sem_inc(drow_used, 1)
                dve.wait_ge(masked_turned, s + 1)
                for q in range(0, NGM, 4):
                    n = min(4, NGM - q)
                    last = nc.vector.tensor_reduce(top[:, q:q + n],
                                                   bank[q // 4][0:MW, 0:n * P].rearrange("w (q e) -> w q e", e=P),
                                                   AX_X, ALU.max)
                    if q + 4 >= NGM:
                        link(last)
                sl = tops[:, bass.ds(c, 1), :].rearrange("w c q -> w (c q)")
                link(nc.vector.tensor_tensor(sl, sl, top[:, :], ALU.max))
                dve.sem_inc(tops_set, 1)

            find_max(0, True)
            with dve.Fori(1, sections) as s:
                find_max(s, False)
            dve.wait_ge(m_in, 16)
            link(nc.vector.tensor_copy(er_m[:, :, 0:HEADS], k.er[:, :, :]))
            link(nc.vector.tensor_tensor(m_el[:, :, :], m_el[:, :, :], k.er[:, :, :], ALU.add))
            link(nc.vector.scalar_tensor_tensor(er_m[:, :, HEADS:2 * HEADS], m_el[:, :, :], 0.2, m_el[:, :, :],
                                                ALU.mult, ALU.max))

            def add_outs(s_last):
                cs = dve.value_load(k.sect[0:1, 0, bass.ds(s_last, 1)], min_val=0, max_val=NC - 1)
                sl = acc[:, bass.ds(cs, 1), :].rearrange("n c f -> n (c f)")
                link1 = nc.vector.tensor_tensor(sl, sl, bank[3][0:CN, 0:HID], ALU.add)
                cd = dve.value_load(k.sect[0:1, 1, bass.ds(s_last, 1)], min_val=0, max_val=NC - 1)
                sg = gacc[:, bass.ds(cd, 1), :].rearrange("f c w -> f (c w)")
                return link1, nc.vector.tensor_tensor(sg, sg, bank[6][0:FEAT + 1, 0:BPC * NB * HEADS], ALU.add)

            def section(s, first):
                link, count = links(dve, mid_step, s * MID_STEPS)
                dve.wait_ge(w_in, s * 16 + 16)
                if not first:
                    dve.wait_ge(att_done, s)
                link(one_hot_d())
                dve.sem_inc(ohd_set, 1)
                cd = dve.value_load(k.sect[0:1, 1, bass.ds(s, 1)], min_val=0, max_val=NC - 1)
                link(nc.vector.tensor_tensor(
                    bde[:, :, :], er_m[:, bass.ds(cd, 1), :].to_broadcast([CN, BPC, 2 * HEADS]),
                    k.bmask[:, :].unsqueeze(2).to_broadcast([CN, BPC, 2 * HEADS]), ALU.mult))
                dve.sem_inc(bde_set, 1)
                dve.wait_ge(slot_in, s * 16 + 16)
                link(nc.vector.tensor_tensor(t.oh[:, :, :], k.iota_j[:, :].unsqueeze(1).to_broadcast([P, BPC, NB]),
                                             t.slot[:, :, 0:1].to_broadcast([P, BPC, NB]), ALU.is_equal))
                link(nc.vector.tensor_scalar(pos[:, :, :], t.slot[:, :, 3:3 + DIM], float(KS - 1), None, ALU.mult))
                dve.sem_inc(slot_used, 1)
                hat_weights(nc, link, k, pos[:, :, :], t.hat[:, :, :, :], t.rise[:, :, :, :], t.fall[:, :, :, :], BPC)
                for g in range(NGR):
                    if not first:
                        dve.wait_ge(sum_done, s * BPC - (NGR - 1 - g) * GB)
                    basis_group(nc, t, g, link)
                    dve.wait_ge(rows_in[g], s * (GB * 16) + GB * 16)
                    link(nc.vector.tensor_tensor(
                        t.mixed[g][:, :, :, :],
                        t.oh[:, g * GB:(g + 1) * GB, :].unsqueeze(3).to_broadcast([P, GB, NB, HID]),
                        rows[g][:, :, :].unsqueeze(2).to_broadcast([P, GB, NB, HID]), ALU.mult))
                    dve.sem_inc(mixed_set, 1)
                    if g == 0:
                        dve.wait_ge(erm_done, s + 1)
                        erm = bank[5][:, 0:BPC * 2 * HEADS].rearrange("p (b w) -> p b w", b=BPC)
                        link(nc.vector.tensor_tensor(score[:, :, :], drow[:, :, FEAT + 1:TROW], erm[:, :, 0:HEADS],
                                                     ALU.add))
                        link(nc.vector.scalar_tensor_tensor(score[:, :, :], score[:, :, :], 0.2, score[:, :, :],
                                                            ALU.mult, ALU.max))
                        link(nc.vector.tensor_tensor(score[:, :, :], score[:, :, :], erm[:, :, HEADS:2 * HEADS],
                                                     ALU.subtract))
                        dve.sem_inc(score_set, 1)
                    if g == 1:
                        dve.wait_ge(wexp_set, s + 1)
                        link(nc.vector.tensor_tensor(
                            masked[:, :, :, :], ohd[:, :, :].unsqueeze(3).to_broadcast([P, BPC, NB, HEADS]),
                            wexp[:, :, :].unsqueeze(2).to_broadcast([P, BPC, NB, HEADS]), ALU.mult))
                        dve.sem_inc(weights_set, 1)
                        if not first:
                            dve.wait_ge(out_done, s)
                            one, two = add_outs(s - 1)
                            link(one)
                            link(two)
                            dve.sem_inc(acc_set, 1)
                            dve.sem_inc(gacc_set, 1)
                        else:
                            dve.sem_inc(mid_step, 2)
                            count[0] += 2
                return count[0]

            MID_STEPS = 19
            section(0, True)
            with dve.Fori(1, sections) as s:
                n = section(s, False)
                assert n == MID_STEPS, n
            dve.wait_ge(out_done, sections)
            one, two = add_outs(sections - 1)
            link, count = links(dve, init_step, 4)
            link(one)
            link(two)


def build_nodes(nc, a, k, acc, gacc, node3_dram):
    with ExitStack() as ctx:
        def sb(name, shape, dt=F32):
            return ctx.enter_context(nc.sbuf_tensor(name, shape, dt))

        def sem(name):
            return ctx.enter_context(nc.semaphore(name))

        G3 = 3 * FEAT
        HW = G3 + 1
        wgat = sb("n_wgat", [FEAT, HEADS, FEAT])
        wih = sb("n_wih", [G3, HEADS, FEAT])
        whh = sb("n_whh", [G3, FEAT])
        wgatT = sb("n_wgatT", [FEAT, HEADS, FEAT])
        wihT = sb("n_wihT", [FEAT, HEADS, G3])
        whhT = sb("n_whhT", [FEAT, G3])
        wc = sb("n_wc", [FEAT + 1, HEADS, HW])
        bih = sb("n_bih", [CN, G3])
        bhh = sb("n_bhh", [CN, G3])
        b2 = sb("n_b2", [CN, HID])
        b3 = sb("n_b3", [CN, HID])
        b4 = sb("n_b4", [CN, DIM])
        w3 = sb("n_w3", [HID, HID])
        w4 = sb("n_w4", [HID, DIM])
        rden = sb("n_rden", [CN, 2, HEADS])
        gih = [sb(f"n_gih{i}", [CN, HEADS, G3]) for i in range(2)]
        gi = sb("n_gi", [CN, NC, G3])
        gh = sb("n_gh", [CN, NC, G3])
        v = sb("n_v", [CN, NC, HID])
        e = sb("n_e", [CN, NC, HID])
        y3 = sb("n_y3", [CN, NC, HID])
        yT = [sb(f"n_yT{i}", [HID, 4, CN]) for i in range(2)]
        nn = sb("n_n", [CN, NC, FEAT])
        xm = sb("n_xm", [CN, NC, FEAT])
        sq = sb("n_sq", [CN, NC, FEAT])
        stat = sb("n_stat", [CN, 4, NC])
        node3 = sb("n_node3", [CN, NC, NROW])
        bank = [ctx.enter_context(nc.psum_tensor(f"n_bank{i}", [P, 512], F32)) for i in range(8)]
        NQ = -(-NC // 4)
        NQ5 = NC // 5

        w_in = sem("n_w_in")
        wc_clear = sem("wc_clear")
        turned = sem("n_turned")
        turned_out = sem("n_turned_out")
        wc_done = sem("wc_done")
        wc_set = sem("wc_set")
        gh_done = sem("gh_done")
        gh_set = sem("gh_set")
        gi_done = sem("gi_done")
        gi_out = sem("gi_out")
        act_in = sem("act_in")
        act_out = sem("act_out")
        v_set = sem("v_set")
        yT_done = sem("yT_done")
        yT_set = sem("yT_set")
        lin_done = sem("lin_done")
        lin_out = sem("lin_out")
        node3_set = sem("node3_set")
        node3_out = sem("node3_out")
        n_step = sem("n_step")
        var_set = sem("n_var_set")
        sd_set = sem("n_sd_set")

        block = ctx.enter_context(nc.Block())

        def row(name, n, parts):
            return a[name].rearrange("(o f) -> o f", o=1).to_broadcast([parts, n])

        @block.sync
        def _(sp):
            for tile, source in (
                    (b2[:, :], row("L1_gnn_stn2_b", HID, CN)), (wih[:, :, :].rearrange("g h o -> g (h o)"), a["L0_gnn_W_ih"]),
                    (wgat[:, :, :].rearrange("i h o -> i (h o)"), a["L0_gnn_W_gat"]), (whh[:, :], a["L0_gnn_W_hh"]),
                    (w3[:, :], a["L1_gnn_stn3_w"]), (w4[:, :], a["L1_gnn_stn4_w"]),
                    (bih[:, :], row("L0_gnn_b_ih", G3, CN)), (bhh[:, :], row("L0_gnn_b_hh", G3, CN)),
                    (b3[:, :], row("L1_gnn_stn3_b", HID, CN)), (b4[:, :], row("L1_gnn_stn4_b", DIM, CN))):
                sp.dma_start(tile, source).then_inc(w_in, 16)
            sp.wait_ge(node3_set, 2)
            sp.dma_start(rows_of(node3_dram, NROW), node3[:, :, :]).then_inc(node3_out, 16)
            sp.wait_ge(node3_out, 16)

        @block.gpsimd
        def _(pool):
            nc.gpsimd.memset(wc[:, :, :], 0.0).then_inc(wc_clear, 1)
            pool.wait_ge(wc_clear, 1)
            nc.gpsimd.affine_select(out=wc[:, :, G3:HW], in_=wc[:, :, G3:HW], compare_op=ALU.not_equal, fill=1.0,
                                    base=-FEAT, pattern=[[0, HEADS], [0, 1]], channel_multiplier=1).then_inc(wc_clear, 1)
            nc.gpsimd.memset(node3[:, :, FEAT + DIM:NROW], 0.0).then_inc(node3_set, 1)

        @block.scalar
        def _(act):
            act.wait_ge(turned, 1)
            nc.scalar.copy(wihT[:, :, :].rearrange("o h g -> o (h g)"), bank[0][0:FEAT, 0:HEADS * G3]).then_inc(turned_out, 1)
            nc.scalar.copy(wgatT[:, :, :].rearrange("o h f -> o (h f)"), bank[1][0:FEAT, 0:HEADS * FEAT])\
                .then_inc(turned_out, 1)
            nc.scalar.copy(whhT[:, :], bank[2][0:FEAT, 0:G3]).then_inc(turned_out, 1)
            act.wait_ge(wc_done, 1)
            act.wait_ge(wc_clear, 2)
            nc.scalar.copy(wc[0:FEAT, :, 0:G3], bank[3][0:FEAT, 0:HEADS * G3].rearrange("f (h g) -> f h g", h=HEADS))\
                .then_inc(wc_set, 1)
            for q in range(NQ5):
                act.wait_ge(gh_done, q + 1)
                nc.scalar.copy(gh[:, 5 * q:5 * q + 5, :].rearrange("n c g -> n (c g)"), bank[6 + q % 2][0:CN, 0:5 * G3])\
                    .then_inc(gh_set, 1)

            def exp(i, ap, scale=1.0):
                act.wait_ge(act_in, i)
                nc.scalar.activation(ap, ap, ACT.Exp, scale=scale).then_inc(act_out, 1)

            def turned_rows(base):
                for q in range(NQ):
                    n = min(4, NC - 4 * q)
                    act.wait_ge(yT_done, base + q + 1)
                    if base + q >= 2:
                        act.wait_ge(lin_done, base + q - 1)
                    nc.scalar.copy(yT[(base + q) % 2][:, 0:n, :].rearrange("f c n -> f (c n)"),
                                   bank[4 + (base + q) % 2][0:HID, 0:n * CN]).then_inc(yT_set, 1)
            exp(1, e[:, :, :])
            turned_rows(0)
            exp(2, e[:, :, :])
            turned_rows(NQ)
            exp(3, gi[:, :, 0:2 * FEAT], -1.0)
            exp(4, nn[:, :, :], 2.0)
            exp(5, nn[:, :, :])
            act.wait_ge(var_set, 1)
            nc.scalar.activation(stat[:, 2, :], stat[:, 1, :], ACT.Sqrt).then_inc(sd_set, 1)

        @block.tensor
        def _(pe):
            pe.wait_ge(w_in, 160)
            for h in range(HEADS):
                nc.tensor.transpose(bank[0][0:FEAT, h * G3:(h + 1) * G3], wih[:, h, :], k.ident[0:G3, 0:G3])
                nc.tensor.transpose(bank[1][0:FEAT, h * FEAT:(h + 1) * FEAT], wgat[:, h, :], k.ident[0:FEAT, 0:FEAT])
            nc.tensor.transpose(bank[2][0:FEAT, 0:G3], whh[:, :], k.ident[0:G3, 0:G3]).then_inc(turned, 1)
            pe.wait_ge(turned_out, 3)
            for h in range(HEADS):
                last = nc.tensor.matmul(bank[3][0:FEAT, h * G3:(h + 1) * G3], wgatT[:, h, :], wihT[:, h, :],
                                        start=True, stop=True)
            last.then_inc(wc_done, 1)
            for q in range(NQ5):
                if q >= 2:
                    pe.wait_ge(gh_set, q - 1)
                for c in range(5 * q, 5 * q + 5):
                    last = nc.tensor.matmul(bank[6 + q % 2][0:CN, (c - 5 * q) * G3:(c - 5 * q + 1) * G3], k.hT[:, c, :],
                                            whhT[:, :], start=True, stop=True)
                last.then_inc(gh_done, 1)
            pe.wait_ge(wc_set, 1)

            def layer(base, x, w, n_out, bank_of):
                for q in range(NQ):
                    n = min(4, NC - 4 * q)
                    if base + q >= 2:
                        pe.wait_ge(yT_set, base + q - 1)
                    for c in range(n):
                        last = nc.tensor.transpose(bank[4 + (base + q) % 2][0:HID, c * CN:(c + 1) * CN],
                                                   x[:, 4 * q + c, :], k.ident[0:CN, 0:CN])
                    last.then_inc(yT_done, 1)
                    pe.wait_ge(yT_set, base + q + 1)
                    for c in range(n):
                        last = nc.tensor.matmul(bank_of(q, c, n_out), yT[(base + q) % 2][:, c, :], w, start=True, stop=True)
                    last.then_inc(lin_done, 1)

            def lin_bank(q, c, n_out):
                if c == 0 and q >= 2:
                    pe.wait_ge(lin_out, q - 1)
                return bank[2 + q % 2][0:CN, c * n_out:(c + 1) * n_out]

            pe.wait_ge(gh_set, NQ5)
            pe.wait_ge(v_set, 1)
            layer(0, v, w3[:, :], HID, lin_bank)
            for c in range(NC):
                if c >= 2:
                    pe.wait_ge(gi_out, c - 1)
                for h in range(HEADS):
                    last = nc.tensor.matmul(
                        bank[c % 2][0:CN, h * HW:(h + 1) * HW],
                        gacc[:, c, :].rearrange("f (n h) -> f n h", h=HEADS)[:, :, h], wc[:, h, :], start=True, stop=True)
                last.then_inc(gi_done, 1)
            pe.wait_ge(v_set, 2)
            layer(NQ, y3, w4[:, :], DIM,
                  lambda q, c, n_out: bank[6][0:CN, (4 * q + c) * n_out:(4 * q + c + 1) * n_out])

        @block.vector
        def _(dve):
            link, count = links(dve, n_step)
            link(nc.vector.tensor_tensor(v[:, :, :], acc[:, :, :], k.inv_deg[:, :].unsqueeze(2)
                                         .to_broadcast([CN, NC, HID]), ALU.mult))
            dve.wait_ge(w_in, 160)
            link(nc.vector.tensor_tensor(v[:, :, :], v[:, :, :], b2[:, :].unsqueeze(1).to_broadcast([CN, NC, HID]), ALU.add))

            def elu(v, e, i):
                link(nc.vector.tensor_scalar(e, v, 0.0, None, ALU.min))
                dve.sem_inc(act_in, 1)
                link(nc.vector.tensor_scalar(v, v, 0.0, None, ALU.max))
                dve.wait_ge(act_out, i)
                link(nc.vector.scalar_tensor_tensor(v, e, -1.0, v, ALU.add, ALU.add))
            elu(v[:, :, :], e[:, :, :], 1)
            dve.sem_inc(v_set, 1)
            for q in range(NQ):
                n = min(4, NC - 4 * q)
                dve.wait_ge(lin_done, q + 1)
                nc.vector.tensor_tensor(y3[:, 4 * q:4 * q + n, :],
                                        bank[2 + q % 2][0:CN, 0:n * HID].rearrange("n (c f) -> n c f", c=n),
                                        b3[:, :].unsqueeze(1).to_broadcast([CN, n, HID]), ALU.add).then_inc(lin_out, 1)
            dve.wait_ge(lin_out, NQ)
            elu(y3[:, :, :], e[:, :, :], 2)
            dve.sem_inc(v_set, 1)
            for c in range(NC):
                ps = bank[c % 2][0:CN, 0:HEADS * HW].rearrange("n (h g) -> n h g", h=HEADS)
                dve.wait_ge(gi_done, c + 1)
                link(nc.vector.tensor_scalar(rden[:, c % 2, :], ps[:, :, G3:HW].rearrange("n h o -> n (h o)"), 1e-30, None,
                                             ALU.max))
                link(nc.vector.reciprocal(rden[:, c % 2, :], rden[:, c % 2, :]))
                link(nc.vector.tensor_tensor(gih[c % 2][:, :, :], ps[:, :, 0:G3],
                                             rden[:, c % 2, :].unsqueeze(2).to_broadcast([CN, HEADS, G3]), ALU.mult))
                dve.sem_inc(gi_out, 1)
                link(nc.vector.tensor_reduce(gi[:, c, :], gih[c % 2][:, :, :].rearrange("n h g -> n g h"), AX_X, ALU.add))
            wide = [CN, NC, G3]
            link(nc.vector.tensor_tensor(gi[:, :, :], gi[:, :, :], bih[:, :].unsqueeze(1).to_broadcast(wide), ALU.add))
            dve.wait_ge(gh_set, NQ5)
            link(nc.vector.tensor_tensor(gh[:, :, :], gh[:, :, :], bhh[:, :].unsqueeze(1).to_broadcast(wide), ALU.add))
            rz = gi[:, :, 0:2 * FEAT]
            link(nc.vector.tensor_tensor(rz, rz, gh[:, :, 0:2 * FEAT], ALU.add))
            dve.sem_inc(act_in, 1)
            dve.wait_ge(act_out, 3)
            link(nc.vector.tensor_scalar(rz, rz, 1.0, None, ALU.add))
            link(nc.vector.reciprocal(rz, rz))
            link(nc.vector.tensor_tensor(nn[:, :, :], gi[:, :, 0:FEAT], gh[:, :, 2 * FEAT:G3], ALU.mult))
            link(nc.vector.tensor_tensor(nn[:, :, :], nn[:, :, :], gi[:, :, 2 * FEAT:G3], ALU.add))
            dve.sem_inc(act_in, 1)
            dve.wait_ge(act_out, 4)
            link(nc.vector.tensor_scalar(nn[:, :, :], nn[:, :, :], 1.0, None, ALU.add))
            link(nc.vector.reciprocal(nn[:, :, :], nn[:, :, :]))
            link(nc.vector.tensor_scalar(nn[:, :, :], nn[:, :, :], -2.0, 1.0, ALU.mult, ALU.add))
            link(nc.vector.tensor_tensor(xm[:, :, :], k.tab_a[:, :, 0:FEAT], nn[:, :, :], ALU.subtract))
            link(nc.vector.tensor_tensor(xm[:, :, :], xm[:, :, :], gi[:, :, FEAT:2 * FEAT], ALU.mult))
            link(nc.vector.tensor_tensor(xm[:, :, :], xm[:, :, :], nn[:, :, :], ALU.add))
            elu(xm[:, :, :], nn[:, :, :], 5)
            link(nc.vector.tensor_tensor(k.x1[:, :, :], k.x[:, :, :], xm[:, :, :], ALU.add))
            layer_norm(nc, dve, link, k.x1[:, :, :], xm, sq, stat, node3[:, :, 0:FEAT], var_set, sd_set, 1)
            dve.wait_ge(lin_done, 2 * NQ)
            link(nc.vector.tensor_tensor(node3[:, :, FEAT:FEAT + DIM],
                                         bank[6][0:CN, 0:NC * DIM].rearrange("n (c d) -> n c d", d=DIM),
                                         b4[:, :].unsqueeze(1).to_broadcast([CN, NC, DIM]), ALU.add))
            link(nc.vector.tensor_copy(k.shift[:, :, :], node3[:, :, FEAT:FEAT + DIM]))
            dve.sem_inc(node3_set, 1)


def build_last(nc, a, k, slots_dram, node3_dram, out_dram):
    with ExitStack() as ctx:
        def sb(name, shape, dt=F32):
            return ctx.enter_context(nc.sbuf_tensor(name, shape, dt))

        def sem(name):
            return ctx.enter_context(nc.semaphore(name))

        t = conv_tiles(nc, ctx, FEAT, "last_")
        rows = [sb(f"last_rows{g}", [P, GB, NROW]) for g in range(NGR)]
        wt = sb("last_w", [K, FEAT, FEAT])
        bias = sb("last_bias", [CN, FEAT])
        ohT = sb("last_ohT", [CN, P])
        bds = sb("last_bds", [CN, BPC, DIM])
        moved = sb("moved", [P, BPC, DIM])
        pos = sb("last_pos", [P, BPC, DIM])
        acc = sb("acc3", [CN, NC, FEAT])
        bank = [ctx.enter_context(nc.psum_tensor(f"last_bank{i}", [P, 512], F32)) for i in range(8)]

        w_in = sem("last_w_in")
        slot_in = sem("last_slot_in")
        slot_used = sem("last_slot_used")
        ix_in = sem("last_ix_in")
        index_set = sem("last_index_set")
        rows_in = [sem(f"last_rows_in{g}") for g in range(NGR)]
        oh_set = sem("last_oh_set")
        ohT_done = sem("last_ohT_done")
        ohT_set = sem("last_ohT_set")
        bds_set = sem("last_bds_set")
        shift_done = sem("last_shift_done")
        mixed_set = sem("last_mixed_set")
        sum_done = sem("last_sum_done")
        sum_set = sem("last_sum_set")
        out_done = sem("last_out_done")
        acc_set = sem("last_acc_set")
        last_step = sem("last_step")
        end_step = sem("last_end_step")
        result_set = sem("result_set")
        result_out = sem("result_out")

        block = ctx.enter_context(nc.Block())

        @block.sync
        def _(sp):
            def load_slots(s, tile, signal):
                sp.dma_start(tile[:, :, :].rearrange("p b w -> p (b w)"),
                             slots_dram[bass.ds(s * SROWS, SROWS), :].rearrange("(p b) w -> p (b w)", b=BPC))\
                  .then_inc(signal, 16)

            sections = sp.value_load(k.sect_count[0:1, 0:1], min_val=NC, max_val=MAXSEC)
            load_slots(0, t.slot_ix, ix_in)
            load_slots(0, t.slot, slot_in)
            sp.dma_start(wt[:, :, :], a["L1_gnn_conv_w"]).then_inc(w_in, 16)
            sp.dma_start(bias[:, :], a["L1_gnn_conv_b"].rearrange("(o f) -> o f", o=1).to_broadcast([CN, FEAT]))\
              .then_inc(w_in, 16)
            sp.wait_ge(index_set, NGR)
            load_slots(1, t.slot_ix, ix_in)
            with sp.Fori(1, sections) as s:
                sp.wait_ge(slot_used, s)
                load_slots(s, t.slot, slot_in)
                sp.wait_ge(index_set, s * NGR + NGR)
                load_slots(s + 1, t.slot_ix, ix_in)
            sp.wait_ge(ix_in, sections * 16 + 16)
            sp.nop(nofuse=True)
            sp.wait_ge(result_set, 1)
            sp.dma_start(out_dram[0:(NC - 1) * CN, :].rearrange("(c p) f -> p c f", p=CN), acc[:, 0:NC - 1, :])\
              .then_inc(result_out, 16)
            sp.dma_start(out_dram[(NC - 1) * CN:N, :], acc[0:LAST, NC - 1, :]).then_inc(result_out, 16)
            sp.wait_ge(result_out, 32)

        @block.gpsimd
        def _(pool):
            sections = pool.value_load(k.sect_count[0:1, 0:1], min_val=NC, max_val=MAXSEC)

            def fetch(s, first):
                for g in range(NGR):
                    pool.wait_ge(index_set, s * NGR + (g + 1))
                    if not first:
                        pool.wait_ge(mixed_set, s * NGR - (NGR - 1 - g))
                    pool.nop(nofuse=True)
                    for b in range(GB):
                        nc.gpsimd.indirect_dma_start(
                            rows[g][:, b, :], None, node3_dram[:, :],
                            bass.IndirectOffsetOnAxis(ap=t.index[g][:, b:b + 1], axis=0)).then_inc(rows_in[g], 16)
            fetch(0, True)
            with pool.Fori(1, sections) as s:
                fetch(s, False)

        @block.scalar
        def _(act):
            def indices(g):
                nc.scalar.copy(t.index[g][:, :], t.slot_ix[:, g * GB:(g + 1) * GB, 1:2].bitcast(U32)
                               .rearrange("p b o -> p (b o)")).then_inc(index_set, 1)

            act.wait_ge(ix_in, 16)
            for g in range(NGR):
                indices(g)
            sections = act.value_load(k.sect_count[0:1, 0:1], min_val=NC, max_val=MAXSEC)

            def section(s, first):
                act.wait_ge(ohT_done, s + 1)
                if not first:
                    act.wait_ge(shift_done, s)
                nc.scalar.copy(ohT[:, :], bank[4][0:CN, 0:P]).then_inc(ohT_set, 1)
                for g in range(NGR):
                    for b in range(g * GB, (g + 1) * GB):
                        act.wait_ge(sum_done, s * BPC + (b + 1))
                        if b == 0 and not first:
                            act.wait_ge(out_done, s)
                        nc.scalar.copy(t.sums[:, b * NB:(b + 1) * NB, :].rearrange("k n f -> k (n f)"),
                                       bank[b % 3][0:K, 0:NB * FEAT]).then_inc(sum_set, 1)
                    act.wait_ge(ix_in, s * 16 + 32)
                    act.wait_ge(rows_in[g], s * (GB * 16) + GB * 16)
                    indices(g)

            section(0, True)
            with act.Fori(1, sections) as s:
                section(s, False)

        @block.tensor
        def _(pe):
            sections = pe.value_load(k.sect_count[0:1, 0:1], min_val=NC, max_val=MAXSEC)
            pe.wait_ge(w_in, 32)

            def section(s, first):
                pe.wait_ge(oh_set, s + 1)
                nc.tensor.transpose(bank[4][0:CN, 0:P], t.oh[:, :, :].rearrange("p b j -> p (b j)"), k.ident[:, :])\
                    .then_inc(ohT_done, 1)
                pe.wait_ge(ohT_set, s + 1)
                pe.wait_ge(bds_set, s + 1)
                nc.tensor.matmul(bank[5][:, 0:BPC * DIM], ohT[:, :], bds[:, :, :].rearrange("n b w -> n (b w)"),
                                 start=True, stop=True).then_inc(shift_done, 1)
                for g in range(NGR):
                    pe.wait_ge(mixed_set, s * NGR + (g + 1))
                    for b in range(g * GB, (g + 1) * GB):
                        if b >= 3 or not first:
                            pe.wait_ge(sum_set, s * BPC + (b - 2))
                        nc.tensor.matmul(bank[b % 3][0:K, 0:NB * FEAT], t.bas[g][:, b - g * GB, :],
                                         t.mixed[g][:, b - g * GB, :, :].rearrange("p j f -> p (j f)"),
                                         start=True, stop=True).then_inc(sum_done, 1)
                pe.wait_ge(sum_set, s * BPC + BPC)
                if not first:
                    pe.wait_ge(acc_set, s)
                for i in range(FEAT):
                    last = nc.tensor.matmul(bank[3][0:CN, 0:FEAT], t.sums[:, :, i], wt[:, i, :],
                                            start=(i == 0), stop=(i == FEAT - 1))
                last.then_inc(out_done, 1)

            section(0, True)
            with pe.Fori(1, sections) as s:
                section(s, False)

        @block.vector
        def _(dve):
            sections = dve.value_load(k.sect_count[0:1, 0:1], min_val=NC, max_val=MAXSEC)
            link, count = links(dve, end_step)
            link(nc.vector.memset(acc[:, :, :], 0.0))

            def add_out(s_last):
                c = dve.value_load(k.sect[0:1, 0, bass.ds(s_last, 1)], min_val=0, max_val=NC - 1)
                sl = acc[:, bass.ds(c, 1), :].rearrange("n c f -> n (c f)")
                return nc.vector.tensor_tensor(sl, sl, bank[3][0:CN, 0:FEAT], ALU.add)

            def section(s, first):
                link, count = links(dve, last_step, s * LAST_STEPS)
                dve.wait_ge(slot_in, s * 16 + 16)
                if not first:
                    dve.wait_ge(ohT_done, s)
                link(nc.vector.tensor_tensor(t.oh[:, :, :], k.iota_j[:, :].unsqueeze(1).to_broadcast([P, BPC, NB]),
                                             t.slot[:, :, 0:1].to_broadcast([P, BPC, NB]), ALU.is_equal))
                dve.sem_inc(oh_set, 1)
                c = dve.value_load(k.sect[0:1, 0, bass.ds(s, 1)], min_val=0, max_val=NC - 1)
                link(nc.vector.tensor_tensor(
                    bds[:, :, :], k.shift[:, bass.ds(c, 1), :].to_broadcast([CN, BPC, DIM]),
                    k.bmask[:, :].unsqueeze(2).to_broadcast([CN, BPC, DIM]), ALU.mult))
                dve.sem_inc(bds_set, 1)
                dve.wait_ge(shift_done, s + 1)
                link(nc.vector.tensor_tensor(moved[:, :, :], t.slot[:, :, 3:3 + DIM],
                                             bank[5][:, 0:BPC * DIM].rearrange("p (b d) -> p b d", b=BPC),
                                             ALU.subtract))
                dve.sem_inc(slot_used, 1)
                for g in range(NGR):
                    b0, b1 = g * GB, (g + 1) * GB
                    dve.wait_ge(rows_in[g], s * (GB * 16) + GB * 16)
                    link(nc.vector.tensor_tensor(pos[:, b0:b1, :], moved[:, b0:b1, :], rows[g][:, :, FEAT:FEAT + DIM],
                                                 ALU.add))
                    link(nc.vector.tensor_scalar(pos[:, b0:b1, :], pos[:, b0:b1, :], 0.0, 1.0, ALU.max, ALU.min))
                    link(nc.vector.tensor_scalar(pos[:, b0:b1, :], pos[:, b0:b1, :], float(KS - 1), None, ALU.mult))
                    hat_weights(nc, link, k, pos[:, b0:b1, :], t.hat[:, b0:b1, :, :], t.rise[:, b0:b1, :, :],
                                t.fall[:, b0:b1, :, :], GB)
                    if not first:
                        dve.wait_ge(sum_done, s * BPC - (NGR - 1 - g) * GB)
                    link(basis_group(nc, t, g, link))
                    link(nc.vector.tensor_tensor(
                        t.mixed[g][:, :, :, :],
                        t.oh[:, b0:b1, :].unsqueeze(3).to_broadcast([P, GB, NB, FEAT]),
                        rows[g][:, :, 0:FEAT].unsqueeze(2).to_broadcast([P, GB, NB, FEAT]), ALU.mult))
                    dve.sem_inc(mixed_set, 1)
                    if g == 1:
                        if not first:
                            dve.wait_ge(out_done, s)
                            link(add_out(s - 1))
                            dve.sem_inc(acc_set, 1)
                        else:
                            dve.sem_inc(last_step, 1)
                            count[0] += 1
                return count[0]

            LAST_STEPS = 31
            section(0, True)
            with dve.Fori(1, sections) as s:
                n = section(s, False)
                assert n == LAST_STEPS, n
            dve.wait_ge(out_done, sections)
            link(add_out(sections - 1))
            shape = [CN, NC, FEAT]
            link(nc.vector.tensor_tensor(acc[:, :, :], acc[:, :, :], k.inv_deg[:, :].unsqueeze(2).to_broadcast(shape),
                                         ALU.mult))
            link(nc.vector.tensor_tensor(acc[:, :, :], acc[:, :, :], bias[:, :].unsqueeze(1).to_broadcast(shape), ALU.add))
            link(nc.vector.tensor_tensor(acc[:, :, :], acc[:, :, :], k.x1[:, :, :], ALU.add))
            dve.sem_inc(result_set, 1)



_INS = ["x", "src", "dst", "edge_attr_3", "L0_gnn_W_gat", "L0_gnn_attn_l", "L0_gnn_attn_r", "L0_gnn_W_ih",
        "L0_gnn_W_hh", "L0_gnn_b_ih", "L0_gnn_b_hh", "L1_gnn_stn1_w", "L1_gnn_stn1_b", "L1_gnn_stn2_w",
        "L1_gnn_stn2_b", "L1_gnn_stn3_w", "L1_gnn_stn3_b", "L1_gnn_stn4_w", "L1_gnn_stn4_b", "L1_gnn_conv_w",
        "L1_gnn_conv_b"]


def build(nc, a, out):
    slots_dram = nc.dram_tensor("slots", ((MAXSEC + 1) * SROWS, SREC), F32).ap()
    drows_dram = nc.dram_tensor("drows", ((MAXSEC + 1) * SROWS, DREC), F32).ap()
    h1_dram = nc.dram_tensor("h1rows", (NC * CN, HID), F32).ap()
    m_dram = nc.dram_tensor("maxima", (NC * NGM, NB * HEADS * GMX), F32).ap()
    node3_dram = nc.dram_tensor("node3", (NC * CN, NROW), F32).ap()
    rows_dram = nc.dram_tensor("key_rows", (4, E), F16).ap()
    with ExitStack() as ctx:
        k = keep_tiles(nc, ctx)
        build_sort(nc, a["src"].rearrange("(p t) -> p t", p=EP), a["dst"].rearrange("(p t) -> p t", p=EP),
                   a["edge_attr_3"].rearrange("(p t) d -> p t d", p=EP), k.sect, k.sect_count, slots_dram,
                   drows_dram, rows_dram, k.ident)
        keep_node_tiles(nc, ctx, k)
        build_send(nc, a, k, slots_dram, drows_dram, h1_dram)
        with nc.sbuf_tensor("acc2", [CN, NC, HID], F32) as acc, \
                nc.sbuf_tensor("gacc", [FEAT + 1, NC, BPC * NB * HEADS], F32) as gacc:
            build_mid(nc, a, k, slots_dram, drows_dram, h1_dram, m_dram, acc, gacc)
            build_nodes(nc, a, k, acc, gacc, node3_dram)
        build_last(nc, a, k, slots_dram, node3_dram, out)


def kernel(**inputs):
    import numpy as _np
    import concourse.bacc as _bacc
    from concourse import mybir as _mybir
    from concourse.bass_utils import run_bass_kernel_spmd as _run

    nc = _bacc.Bacc("TRN2", target_bir_lowering=False, num_devices=1)
    arrays, args = {}, {}
    for name in _INS:
        a = _np.ascontiguousarray(inputs[name])
        arrays[f"in_{name}_dram"] = a
        args[name] = nc.dram_tensor(f"in_{name}_dram", a.shape, _mybir.dt.from_np(a.dtype),
                                    kind="ExternalInput").ap()
    out = nc.dram_tensor("out_0_dram", (N, FEAT), F32, kind="ExternalOutput").ap()
    build(nc, args, out)
    r = _run(nc, [arrays], core_ids=[0])
    return r.results[0]["out_0_dram"]
```

```python
from contextlib import ExitStack

import numpy as np
import concourse.bass as bass
from concourse import mybir

F32 = mybir.dt.float32
F16 = mybir.dt.float16
BF16 = mybir.dt.bfloat16
I32 = mybir.dt.int32
U32 = mybir.dt.uint32
ALU = mybir.AluOpType
ACT = mybir.ActivationFunctionType
AX_X = mybir.AxisListType.X

N, FEAT, HEADS = 3125, 32, 4
E = 50000
KS, DIM = 5, 3
K = KS ** DIM
HID = 64

NB, BPC = 6, 21
CN = NB * BPC
NC = -(-N // CN)
LAST = N - (NC - 1) * CN
P = 128
SROWS = P * BPC
MAXSEC = NC + E // P + 1
FIXED = NC + 2
GB, NGR = 7, 3
HI = 7
LO = NC * BPC // HI
LPC = BPC // HI
EP, ET = 125, 400
GT = 25
NG = ET // GT
assert EP * ET == E and NC * BPC == LO * HI and NG % 2 == 0 and NGR * GB == BPC

SREC = 8
DREC = FEAT + 1 + HEADS + 1
TROW = FEAT + 1 + HEADS
G3 = 3 * FEAT
HW = G3 + 1
NROW = FEAT + DIM + 1
MAGIC = 12582912.0
BIG = 1.0e30


def links(eng, sem, base=0):
    count = [0]

    def link(ins):
        count[0] += 1
        ins.then_inc(sem, 1)
        eng.wait_ge(sem, base + count[0])
    return link, count


def node_prep(nc, ctx, a, k, bank):
    def sb(name, shape, dt=F32):
        return ctx.enter_context(nc.sbuf_tensor(name, shape, dt))

    def sem(name):
        return ctx.enter_context(nc.semaphore(name))

    xm = k.gh[:, :, 0:FEAT]
    sq = k.gh[:, :, FEAT:2 * FEAT]
    stat = sb("stat", [CN, 4, NC])
    wgat = sb("wgat", [FEAT, HEADS, FEAT])
    attn = sb("attn", [FEAT, 2, HEADS, FEAT])
    wat = sb("wat", [FEAT, 2, HEADS, FEAT])
    wa = sb("wa", [FEAT, 2 * HEADS])
    hT = [sb(f"hT{i}", [FEAT, 4, CN]) for i in range(2)]
    wih = sb("wih", [G3, HEADS, FEAT])
    whh = sb("whh", [G3, FEAT])
    bhh = sb("bhh", [CN, G3])
    wgatT = sb("wgatT", [FEAT, HEADS, FEAT])
    wihT = sb("wihT", [FEAT, HEADS, G3])
    whhT = sb("whhT", [FEAT, G3])

    x_in = sem("x_in")
    w_in = sem("w_in")
    gru_in = sem("gru_in")
    x_pad = sem("x_pad")
    wc_clear = sem("wc_clear")
    var_set = sem("var_set")
    sd_set = sem("sd_set")
    ln_step = sem("ln_step")
    h_set = sem("h_set")
    h_turned = sem("h_turned")
    hT_set = sem("hT_set")
    weights_turned = sem("weights_turned")
    turned_out = sem("turned_out")
    wc_done = sem("wc_done")
    wc_set = sem("wc_set")
    gh_done = sem("gh_done")
    gh_set = sem("gh_set")
    NQ = -(-NC // 4)

    def on_sync(sp):
        sp.wait_ge(x_pad, 1)
        sp.dma_start(k.x[:, 0:NC - 1, :], a["x"][0:(NC - 1) * CN, :].rearrange("(c p) f -> p c f", p=CN))\
          .then_inc(x_in, 16)
        sp.dma_start(k.x[0:LAST, NC - 1, :], a["x"][(NC - 1) * CN:N, :]).then_inc(x_in, 16)
        sp.dma_start(wgat[:, :, :], a["L0_gnn_W_gat"].rearrange("i (h o) -> i h o", h=HEADS)).then_inc(w_in, 16)
        for i, name in enumerate(("L0_gnn_attn_l", "L0_gnn_attn_r")):
            sp.dma_start(attn[:, i, :, :].rearrange("p h f -> p (h f)"),
                         a[name].rearrange("(o h) f -> o (h f)", o=1).to_broadcast([FEAT, HEADS * FEAT]))\
              .then_inc(w_in, 16)
        for tile, source in (
                (wih[:, :, :].rearrange("g h o -> g (h o)"), a["L0_gnn_W_ih"]), (whh[:, :], a["L0_gnn_W_hh"]),
                (k.bih[:, :], a["L0_gnn_b_ih"].rearrange("(o f) -> o f", o=1).to_broadcast([CN, G3])),
                (bhh[:, :], a["L0_gnn_b_hh"].rearrange("(o f) -> o f", o=1).to_broadcast([CN, G3]))):
            sp.dma_start(tile, source).then_inc(gru_in, 16)

    def on_gpsimd(pool):
        nc.gpsimd.memset(k.x[:, NC - 1, :], 0.0).then_inc(x_pad, 1)
        nc.gpsimd.memset(k.wc[:, :, :], 0.0).then_inc(wc_clear, 1)
        pool.wait_ge(wc_clear, 1)
        nc.gpsimd.affine_select(out=k.wc[:, :, G3:HW], in_=k.wc[:, :, G3:HW], compare_op=ALU.not_equal, fill=1.0,
                                base=-FEAT, pattern=[[0, HEADS], [0, 1]], channel_multiplier=1).then_inc(wc_clear, 1)

    def on_scalar(act):
        act.wait_ge(var_set, 1)
        nc.scalar.activation(stat[:, 2, :], stat[:, 1, :], ACT.Sqrt).then_inc(sd_set, 1)
        act.wait_ge(weights_turned, 1)
        nc.scalar.copy(wihT[:, :, :].rearrange("o h g -> o (h g)"), bank[6][0:FEAT, 0:HEADS * G3]).then_inc(turned_out, 1)
        nc.scalar.copy(wgatT[:, :, :].rearrange("o h f -> o (h f)"), bank[7][0:FEAT, 0:HEADS * FEAT])\
            .then_inc(turned_out, 1)
        nc.scalar.copy(whhT[:, :], bank[7][0:FEAT, HEADS * FEAT:HEADS * FEAT + G3]).then_inc(turned_out, 1)
        act.wait_ge(wc_done, 1)
        act.wait_ge(wc_clear, 2)
        nc.scalar.copy(k.wc[0:FEAT, :, 0:G3], bank[3][0:FEAT, 0:HEADS * G3].rearrange("f (h g) -> f h g", h=HEADS))\
            .then_inc(wc_set, 1)
        def gates_out(q):
            n = min(4, NC - 4 * q)
            act.wait_ge(gh_done, q + 1)
            nc.scalar.copy(k.gh[:, 4 * q:4 * q + n, :].rearrange("n c g -> n (c g)"), bank[6 + q % 2][0:CN, 0:n * G3])\
                .then_inc(gh_set, 1)

        for q in range(NQ):
            cs = range(4 * q, min(4 * q + 4, NC))
            act.wait_ge(h_turned, q + 1)
            if q >= 2:
                act.wait_ge(gh_done, q - 1)
            nc.scalar.copy(hT[q % 2][:, 0:len(cs), :].rearrange("f c n -> f (c n)"),
                           bank[q % 2][0:FEAT, 0:len(cs) * CN]).then_inc(hT_set, 1)
            if q >= 1:
                gates_out(q - 1)
        gates_out(NQ - 1)

    def on_tensor(pe):
        pe.wait_ge(gru_in, 64)
        pe.wait_ge(w_in, 48)
        for h in range(HEADS):
            nc.tensor.transpose(bank[6][0:FEAT, h * G3:(h + 1) * G3], wih[:, h, :], k.ident[0:G3, 0:G3])
            nc.tensor.transpose(bank[7][0:FEAT, h * FEAT:(h + 1) * FEAT], wgat[:, h, :], k.ident[0:FEAT, 0:FEAT])
        nc.tensor.transpose(bank[7][0:FEAT, HEADS * FEAT:HEADS * FEAT + G3], whh[:, :], k.ident[0:G3, 0:G3])\
            .then_inc(weights_turned, 1)
        pe.wait_ge(turned_out, 3)
        for h in range(HEADS):
            last = nc.tensor.matmul(bank[3][0:FEAT, h * G3:(h + 1) * G3], wgatT[:, h, :], wihT[:, h, :],
                                    start=True, stop=True)
        last.then_inc(wc_done, 1)
        pe.wait_ge(h_set, 1)

        def turn(q):
            for c in range(4 * q, min(4 * q + 4, NC)):
                last = nc.tensor.transpose(bank[q % 2][0:FEAT, (c - 4 * q) * CN:(c - 4 * q + 1) * CN],
                                           k.tab_a[:, c, 0:FEAT], k.ident[0:CN, 0:CN])
            last.then_inc(h_turned, 1)

        turn(0)
        for q in range(NQ):
            if q + 1 < NQ:
                turn(q + 1)
            pe.wait_ge(hT_set, q + 1)
            if q >= 2:
                pe.wait_ge(gh_set, q - 1)
            for c in range(4 * q, min(4 * q + 4, NC)):
                nc.tensor.matmul(bank[2][0:CN, c * 8:(c + 1) * 8], hT[q % 2][:, c - 4 * q, :], wa[:, :],
                                 start=True, stop=True)
                last = nc.tensor.matmul(bank[6 + q % 2][0:CN, (c - 4 * q) * G3:(c - 4 * q + 1) * G3],
                                        hT[q % 2][:, c - 4 * q, :], whhT[:, :], start=True, stop=True)
            last.then_inc(gh_done, 1)

    def on_vector(dve):
        link, count = links(dve, ln_step)
        link(nc.vector.memset(k.tab_a[:, :, FEAT:FEAT + 1], 1.0))
        dve.wait_ge(w_in, 48)
        for i in range(2):
            link(nc.vector.tensor_tensor(wat[:, i, :, :], wgat[:, :, :], attn[:, i, :, :], ALU.mult))
        link(nc.vector.tensor_reduce(wa[:, :], wat[:, :, :, :].rearrange("p i h f -> p (i h) f"), AX_X, ALU.add))
        dve.wait_ge(x_in, 32)
        layer_norm(nc, dve, link, k.x[:, :, :], xm, sq, stat, k.tab_a[:, :, 0:FEAT], var_set, sd_set, 1)
        dve.sem_inc(h_set, 1)
        dve.wait_ge(gh_done, NQ)
        el = bank[2][0:CN, 0:NC * 8].rearrange("n (c w) -> n c w", w=8)
        link(nc.vector.tensor_copy(k.tab_a[:, :, FEAT + 1:TROW], el[:, :, 0:HEADS]))
        link(nc.vector.tensor_copy(k.er[:, :, :], el[:, :, HEADS:2 * HEADS]))
        dve.wait_ge(gh_set, NQ)
        link(nc.vector.tensor_tensor(k.gh[:, :, :], k.gh[:, :, :],
                                     bhh[:, :].unsqueeze(1).to_broadcast([CN, NC, G3]), ALU.add))
        link(nc.vector.tensor_tensor(k.gh[:, :, 0:2 * FEAT], k.gh[:, :, 0:2 * FEAT],
                                     k.bih[:, 0:2 * FEAT].unsqueeze(1).to_broadcast([CN, NC, 2 * FEAT]), ALU.add))

    return on_sync, on_gpsimd, on_scalar, on_tensor, on_vector


def build_sort(nc, a, k_nodes, src, dst, attr, sect, sect_count, slots_dram, drows_dram, rows_dram, ident):
    with ExitStack() as ctx:
        def sb(name, shape, dt):
            return ctx.enter_context(nc.sbuf_tensor(name, shape, dt))

        def ps(name, shape, dt=F32):
            return ctx.enter_context(nc.psum_tensor(name, shape, dt))

        def sem(name):
            return ctx.enter_context(nc.semaphore(name))

        key_i = [sb("src_i", [EP, ET], I32), sb("dst_i", [EP, ET], I32)]
        attr_sb = sb("attr_sb", [EP, ET, DIM], F32)
        kf = sb("kf", [EP, ET], F32)
        r42 = sb("r42", [EP, ET], F32)
        cm, l3 = kf, r42
        lo = [sb(f"lo{k}", [EP, ET], F32) for k in range(2)]
        hi = [sb(f"hi{k}", [EP, ET], F32) for k in range(2)]
        jn = [sb(f"jn{k}", [EP, ET], F32) for k in range(2)]
        bc = [sb(f"bc{k}", [EP, ET], F32) for k in range(2)]
        blk = [sb(f"blk{k}", [EP, ET], F32) for k in range(2)]
        rowT = sb("rowT", [ET // 4, 4, 4 * EP], F16)
        iota_f = sb("iota_f", [P, LO], F32)
        iota_b = sb("iota_b", [P, LO], BF16)
        iota_s = sb("iota_s", [NC, MAXSEC], F32)
        part = sb("part", [P, 1], F32)
        ltri = sb("ltri", [EP, EP], F32)
        ones = sb("ones", [P, 1], F32)
        empty_s = sb("empty_s", [P, BPC, SREC], F32)
        empty_d = sb("empty_d", [P, BPC, DREC], F32)
        lo_b = [sb(f"lo_b{k}", [EP, ET], BF16) for k in range(2)]
        oh_lo = [[sb(f"oh_lo{k}{h}", [EP, GT, LO], BF16) for h in range(2)] for k in range(2)]
        oh_hi = [[sb(f"oh_hi{k}{h}", [EP, GT, HI], BF16) for h in range(2)] for k in range(2)]
        hist = [sb(f"hist{k}", [LO, HI, ET], F32) for k in range(2)]
        pref = [sb(f"pref{k}", [LO, HI, ET], F32) for k in range(2)]
        zeros = sb("zeros", [LO, ET], F32)
        cmax = sb("cmax", [LO, 2], F32)
        crow = sb("crow", [1, 2, LO], F32)
        sq = sb("sq", [1, 2, NC], F32)
        scum = sb("scum", [1, 2, NC], F32)
        sbase = sb("sbase", [1, 2, NC], F32)
        sbase3 = sb("sbase3", [1, 2, LO], F32)
        zero_row = sb("zero_row", [1, NC], F32)
        basecol = sb("basecol", [LO, 2], F32)
        cumcol = sb("cumcol", [NC, 2], F32)
        past = [sb(f"past{k}", [NC, MAXSEC], F32) for k in range(2)]
        scount = sb("scount", [1, 3], F32)
        pg = [sb(f"pg{k}", [LO, GT, HI], F32) for k in range(2)]
        pg_hi = [sb(f"pg_hi{k}", [LO, GT, HI], BF16) for k in range(2)]
        pg_lo = [sb(f"pg_lo{k}", [LO, GT, HI], BF16) for k in range(2)]
        blkrow = [[sb(f"blkrow{k}{h}", [EP, GT * EP], F16) for h in range(2)] for k in range(2)]
        lorow = [[sb(f"lorow{k}{h}", [LO, GT * EP], F16) for h in range(2)] for k in range(2)]
        oh_loT = [sb(f"oh_loT{k}", [LO, GT * EP], BF16) for k in range(2)]
        blk_g = [sb(f"blk_g{k}", [EP, GT], F32) for k in range(2)]
        unused = [flat[:, i * EP:(i + 1) * EP]
                  for flat in (oh_lo[0][h][:, :, :].rearrange("e t l -> e (t l)") for h in range(2))
                  for i in range(GT * LO // EP)]
        in_tile = [sb(f"in_tile{k}", [EP, GT], F32) for k in range(2)]
        hsel = [sb(f"hsel{k}", [EP, GT, HI], F32) for k in range(2)]
        before = [sb(f"before{k}", [EP, GT], F32) for k in range(2)]
        row21 = [sb(f"row21{k}", [EP, GT], F32) for k in range(2)]
        rec = [sb(f"rec{h}", [EP, GT, SREC], F32) for h in range(2)]
        srow = [sb(f"srow{h}", [EP, GT], U32) for h in range(2)]

        bank = [ps(f"sort_bank{i}", [P, 512]) for i in range(8)]
        prep_sync, prep_gpsimd, prep_scalar, prep_tensor, prep_vector = node_prep(nc, ctx, a, k_nodes, bank)

        edges_in = [sem("edges_in0"), sem("edges_in1"), sem("edges_in2")]
        consts_set = sem("consts_set")
        ident_step = sem("ident_step")
        empties_set = sem("empties_set")
        tables_empty = sem("tables_empty")
        more_empty = sem("more_empty")
        keys_split = sem("keys_split")
        keys_turned = sem("keys_turned")
        rowT_set = sem("rowT_set")
        rowT_out = [sem(f"rowT_out{a}") for a in range(4)]
        lohi_set = sem("lohi_set")
        hist_used = sem("hist_used")
        hist_done = sem("hist_done")
        zeros_set = sem("zeros_set")
        cmax_set = sem("cmax_set")
        cmax_turned = sem("cmax_turned")
        sec_set = sem("sec_set")
        sec_turned = sem("sec_turned")
        past_set = sem("past_set")
        past_summed = sem("past_summed")
        sect_set = sem("sect_set")
        rows_in = [sem(f"rows_in{h}") for h in range(2)]
        rows_used = sem("rows_used")
        loT_set = sem("loT_set")
        before_done = sem("before_done")
        rec_set = sem("rec_set")
        rec_out = [sem(f"rec_out{h}") for h in range(2)]
        split_step = sem("split_step")
        sec_step = sem("sec_step")
        rank_step = sem("rank_step")

        block = ctx.enter_context(nc.Block())

        def bcast_rows(a, g, parts):
            return rows_dram[a:a + 1, bass.ds(g * (GT * EP), GT * EP)].to_broadcast([parts, GT * EP])

        @block.sync
        def _(sp):
            sp.dma_start(key_i[0][:, :], src).then_inc(edges_in[0], 16)
            sp.dma_start(key_i[1][:, :], dst).then_inc(edges_in[1], 16)
            sp.dma_start(attr_sb[:, :, :], attr).then_inc(edges_in[2], 16)
            prep_sync(sp)
            for a in range(4):
                sp.wait_ge(rowT_set, a + 1)
                sp.dma_start(rows_dram[a, :].rearrange("(q r x) -> r q x", q=4, x=EP),
                             rowT[:, a, :].rearrange("r (q x) -> r q x", q=4)).then_inc(rowT_out[a], 16)
            for a in range(4):
                sp.wait_ge(rowT_out[a], 16)
            sp.sem_inc(rows_used, 2)
            with sp.Fori(0, NG // 2) as i:
                for h in range(2):
                    sp.wait_ge(rows_used, i * 2 + (h + 1))
                    for k in range(2):
                        sp.dma_start(blkrow[k][h][:, :], bcast_rows(k, i * 2 + h, EP)).then_inc(rows_in[h], 16)
                        sp.dma_start(lorow[k][h][:, :], bcast_rows(2 + k, i * 2 + h, LO)).then_inc(rows_in[h], 16)

        @block.scalar
        def _(act):
            act.wait_ge(empties_set, 5)
            act.dma_start(slots_dram[0:FIXED * SROWS, :].rearrange("(s p b) w -> p s (b w)", p=P, b=BPC),
                          empty_s[:, :, :].rearrange("p b w -> p (b w)").unsqueeze(1)
                          .to_broadcast([P, FIXED, BPC * SREC])).then_inc(tables_empty, 16)
            act.dma_start(drows_dram[0:FIXED * SROWS, :].rearrange("(s p b) w -> p s (b w)", p=P, b=BPC),
                          empty_d[:, :, :].rearrange("p b w -> p (b w)").unsqueeze(1)
                          .to_broadcast([P, FIXED, BPC * DREC])).then_inc(tables_empty, 16)
            for a in range(4):
                act.wait_ge(keys_turned, a + 1)
                nc.scalar.copy(rowT[:, a, :], bank[a][0:ET // 4, 0:4 * EP]).then_inc(rowT_set, 1)
            with act.Fori(0, NG // 2) as i:
                for h in range(2):
                    act.wait_ge(hist_done, i * 2 + (h + 1))
                    for k in range(2):
                        last = nc.scalar.copy(
                            hist[k][:, :, bass.ds(i * (2 * GT) + h * GT, GT)],
                            bank[4 + 2 * k + h][0:LO, 0:GT * HI].rearrange("l (t h) -> l h t", h=HI))
                    last.then_inc(hist_used, 1)
            act.wait_ge(sect_set, 1)
            upto = act.value_load(sect_count[0:1, 1:2], min_val=FIXED + 1, max_val=MAXSEC)
            with act.Fori(FIXED, upto) as s:
                act.dma_start(slots_dram[bass.ds(s * SROWS, SROWS), :].rearrange("(p b) w -> p (b w)", b=BPC),
                              empty_s[:, :, :].rearrange("p b w -> p (b w)")).then_inc(more_empty, 16)
                act.dma_start(drows_dram[bass.ds(s * SROWS, SROWS), :].rearrange("(p b) w -> p (b w)", b=BPC),
                              empty_d[:, :, :].rearrange("p b w -> p (b w)")).then_inc(more_empty, 16)
                act.wait_ge(more_empty, (s - (FIXED - 1)) * 32)
            act.sem_inc(sect_set, 1)
            prep_scalar(act)

        @block.gpsimd
        def _(pool):
            nc.gpsimd.memset(ident[:, :], 0.0).then_inc(ident_step, 1)
            nc.gpsimd.memset(ltri[:, :], 1.0).then_inc(ident_step, 1)
            pool.wait_ge(ident_step, 2)
            nc.gpsimd.affine_select(out=ident[:, :], in_=ident[:, :], compare_op=ALU.not_equal, fill=1.0, base=0,
                                    pattern=[[-1, P]], channel_multiplier=1).then_inc(ident_step, 1)
            nc.gpsimd.affine_select(out=ltri[:, :], in_=ltri[:, :], compare_op=ALU.is_gt, fill=0.0, base=0,
                                    pattern=[[-1, EP]], channel_multiplier=1).then_inc(ident_step, 1)
            nc.gpsimd.iota(iota_f[:, :], pattern=[[1, LO]], base=0, channel_multiplier=0,
                           allow_small_or_imprecise_dtypes=True).then_inc(consts_set, 1)
            nc.gpsimd.iota(iota_b[:, :], pattern=[[1, LO]], base=0, channel_multiplier=0,
                           allow_small_or_imprecise_dtypes=True).then_inc(consts_set, 1)
            nc.gpsimd.iota(iota_s[:, :], pattern=[[1, MAXSEC]], base=0, channel_multiplier=0,
                           allow_small_or_imprecise_dtypes=True).then_inc(consts_set, 1)
            nc.gpsimd.iota(part[:, :], pattern=[[0, 1]], base=0, channel_multiplier=1,
                           allow_small_or_imprecise_dtypes=True).then_inc(consts_set, 1)
            nc.gpsimd.memset(ones[:, :], 1.0).then_inc(consts_set, 1)
            nc.gpsimd.memset(empty_s[:, :, :], 0.0).then_inc(empties_set, 1)
            nc.gpsimd.memset(empty_d[:, :, :], 0.0).then_inc(empties_set, 1)
            pool.wait_ge(empties_set, 2)
            nc.gpsimd.memset(empty_s[:, :, 0:1], -1.0).then_inc(empties_set, 1)
            nc.gpsimd.memset(empty_d[:, :, DREC - 1:DREC], -1.0).then_inc(empties_set, 1)
            pool.wait_ge(empties_set, 4)
            nc.gpsimd.memset(empty_s[:, :, 2:3].bitcast(I32), 1 << 28).then_inc(empties_set, 1)
            nc.gpsimd.memset(zero_row[:, :], 0.0).then_inc(zeros_set, 1)
            nc.gpsimd.memset(zeros[:, :], 0.0).then_inc(zeros_set, 1)
            prep_gpsimd(pool)
            pool.wait_ge(tables_empty, 32)
            pool.wait_ge(sect_set, 2)
            with pool.Fori(0, NG // 2) as i:
                for h in range(2):
                    pool.wait_ge(rec_set, i * 2 + (h + 1))
                    pool.nop(nofuse=True)
                    for t in range(GT):
                        nc.gpsimd.indirect_dma_start(
                            slots_dram[:, :], bass.IndirectOffsetOnAxis(ap=srow[h][:, t:t + 1], axis=0),
                            rec[h][:, t, :], None).then_inc(rec_out[h], 16)
            for h in range(2):
                pool.wait_ge(rec_out[h], NG // 2 * GT * 16)

        @block.tensor
        def _(pe):
            pe.wait_ge(ident_step, 4)
            for a in range(4):
                pe.wait_ge(keys_split, a % 2 + 1)
                arr = (blk[0], blk[1], lo[0], lo[1])[a]
                for q in range(4):
                    last = nc.tensor.transpose(bank[a][0:ET // 4, q * EP:(q + 1) * EP],
                                               arr[:, q * (ET // 4):(q + 1) * (ET // 4)], ident[0:EP, 0:EP])
                last.then_inc(keys_turned, 1)
            with pe.Fori(0, NG // 2) as i:
                for h in range(2):
                    pe.wait_ge(lohi_set, i * 2 + (h + 1))
                    pe.wait_ge(hist_used, i * 2 + (h + 1))
                    for k in range(2):
                        for t in range(GT):
                            last = nc.tensor.matmul(bank[4 + 2 * k + h][0:LO, t * HI:(t + 1) * HI],
                                                    oh_lo[k][h][:, t, :], oh_hi[k][h][:, t, :], start=True, stop=True)
                    last.then_inc(hist_done, 1)
            pe.wait_ge(cmax_set, 1)
            pe.wait_ge(rowT_set, 4)
            for k in range(2):
                last = nc.tensor.transpose(bank[0][0:1, k * P:k * P + LO], cmax[:, k:k + 1], ident[0:LO, 0:LO])
            last.then_inc(cmax_turned, 1)
            pe.wait_ge(sec_set, 1)
            for k in range(2):
                nc.tensor.matmul(bank[1][0:LO, k:k + 1], sbase3[0:1, k, :], ones[0:1, 0:1], start=True, stop=True)
                last = nc.tensor.matmul(bank[1][0:NC, 4 + k:5 + k], scum[0:1, k, :], ones[0:1, 0:1],
                                        start=True, stop=True)
            last.then_inc(sec_turned, 1)
            pe.wait_ge(past_set, 1)
            for k in range(2):
                last = nc.tensor.matmul(bank[2 + k][0:1, 0:MAXSEC], ones[0:NC, 0:1], past[k][:, :],
                                        start=True, stop=True)
            last.then_inc(past_summed, 1)
            with pe.Fori(0, NG) as g:
                pe.wait_ge(loT_set, g + 1)
                for k in range(2):
                    for t in range(GT):
                        nc.tensor.matmul(bank[4 + k][0:EP, t * HI:(t + 1) * HI],
                                         oh_loT[k][:, t * EP:(t + 1) * EP], pg_hi[k][:, t, :],
                                         start=True, stop=False)
                        last = nc.tensor.matmul(bank[4 + k][0:EP, t * HI:(t + 1) * HI],
                                                oh_loT[k][:, t * EP:(t + 1) * EP], pg_lo[k][:, t, :],
                                                start=False, stop=True)
                last.then_inc(before_done, 1)
            prep_tensor(pe)

        @block.vector
        def _(dve):
            link, _c = links(dve, split_step)
            dve.wait_ge(consts_set, 5)

            def floor_div(out, x, d):
                link(nc.vector.tensor_scalar(out, x, 1.0 / d, 0.5 / d - 0.5, ALU.mult, ALU.add))
                link(nc.vector.tensor_scalar(out, out, MAGIC, -MAGIC, ALU.add, ALU.add))

            for k in range(2):
                dve.wait_ge(edges_in[k], 16)
                link(nc.vector.tensor_copy(kf[:, :], key_i[k][:, :]))
                floor_div(lo[k][:, :], kf[:, :], NB * HI)
                link(nc.vector.scalar_tensor_tensor(r42[:, :], lo[k][:, :], -float(NB * HI), kf[:, :],
                                                    ALU.mult, ALU.add))
                floor_div(hi[k][:, :], r42[:, :], NB)
                link(nc.vector.scalar_tensor_tensor(blk[k][:, :], lo[k][:, :], float(HI), hi[k][:, :],
                                                    ALU.mult, ALU.add))
                dve.sem_inc(keys_split, 1)
                link(nc.vector.scalar_tensor_tensor(jn[k][:, :], hi[k][:, :], -float(NB), r42[:, :],
                                                    ALU.mult, ALU.add))
                floor_div(cm[:, :], lo[k][:, :], LPC)
                link(nc.vector.scalar_tensor_tensor(l3[:, :], cm[:, :], -float(LPC), lo[k][:, :],
                                                    ALU.mult, ALU.add))
                link(nc.vector.scalar_tensor_tensor(bc[k][:, :], l3[:, :], float(HI), hi[k][:, :],
                                                    ALU.mult, ALU.add))
                link(nc.vector.tensor_copy(lo_b[k][:, :], lo[k][:, :]))
            dve.sem_inc(hist_used, 2)

            def one_hots(g, h):
                for k in range(2):
                    nc.vector.tensor_tensor(
                        oh_lo[k][h][:, :, :], iota_b[0:EP, 0:LO].unsqueeze(1).to_broadcast([EP, GT, LO]),
                        lo_b[k][:, bass.ds(g * GT, GT)].unsqueeze(2).to_broadcast([EP, GT, LO]), ALU.is_equal)
                    last = nc.vector.tensor_tensor(
                        oh_hi[k][h][:, :, :], iota_f[0:EP, 0:HI].unsqueeze(1).to_broadcast([EP, GT, HI]),
                        hi[k][:, bass.ds(g * GT, GT)].unsqueeze(2).to_broadcast([EP, GT, HI]), ALU.is_equal)
                last.then_inc(lohi_set, 1)

            for h in range(2):
                one_hots(h, h)
            with dve.Fori(1, NG // 2) as i:
                for h in range(2):
                    dve.wait_ge(hist_done, i * 2 + (h - 1))
                    one_hots(i * 2 + h, h)
            link, count = links(dve, sec_step)
            dve.wait_ge(zeros_set, 2)
            dve.wait_ge(hist_used, NG + 2)
            for k in range(2):
                for h in range(HI):
                    last = nc.vector.tensor_tensor_scan(pref[k][:, h, :], hist[k][:, h, :], zeros[:, :], 0.0,
                                                        ALU.add, ALU.add)
                link(last)
                link(nc.vector.tensor_reduce(cmax[:, k:k + 1], pref[k][:, :, ET - 1:ET].rearrange("l h o -> l (h o)"),
                                             AX_X, ALU.max))
            dve.sem_inc(cmax_set, 1)
            dve.wait_ge(cmax_turned, 1)
            link(nc.vector.tensor_copy(crow[:, :, :], bank[0][0:1, 0:2 * P].rearrange("o (k l) -> o k l", k=2)[:, :, 0:LO]))
            for k in range(2):
                link(nc.vector.tensor_reduce(sq[:, k, :], crow[:, k, :].rearrange("o (c l) -> o c l", l=LPC),
                                             AX_X, ALU.max))
            sqf = sq[:, :, :].rearrange("o k c -> o (k c)")
            link(nc.vector.tensor_scalar(sqf, sqf, float(P - 1), None, ALU.add))
            floor_div(sqf, sqf, P)
            link(nc.vector.tensor_scalar(sqf, sqf, 1.0, None, ALU.max))
            for k in range(2):
                link(nc.vector.tensor_tensor_scan(scum[:, k, :], sq[:, k, :], zero_row[:, :], 0.0, ALU.add, ALU.add))
                link(nc.vector.tensor_tensor(sbase[:, k, :], scum[:, k, :], sq[:, k, :], ALU.subtract))
                link(nc.vector.tensor_scalar(
                    sbase3[:, k, :].rearrange("o (c l) -> o c l", l=LPC),
                    sbase[:, k, :].unsqueeze(2).to_broadcast([1, NC, LPC]), float(P), None, ALU.mult))
            dve.sem_inc(sec_set, 1)
            link(nc.vector.tensor_tensor(scount[:, 0:1], scum[:, 0, NC - 1:NC], scum[:, 1, NC - 1:NC], ALU.max))
            link(nc.vector.tensor_scalar(scount[:, 1:2], scount[:, 0:1], 1.0, float(FIXED + 1), ALU.add, ALU.max))
            link(nc.vector.tensor_scalar(scount[:, 2:3], scount[:, 0:1], 0.5, 0.25, ALU.mult, ALU.add))
            link(nc.vector.tensor_scalar(scount[:, 2:3], scount[:, 2:3], MAGIC, -MAGIC, ALU.add, ALU.add))
            link(nc.vector.tensor_copy(sect_count[:, :], scount[:, :]))
            dve.wait_ge(sec_turned, 1)
            link(nc.vector.tensor_copy(basecol[:, :], bank[1][0:LO, 0:2]))
            link(nc.vector.tensor_copy(cumcol[:, :], bank[1][0:NC, 4:6]))
            for k in range(2):
                link(nc.vector.tensor_scalar(past[k][:, :], iota_s[:, :], cumcol[:, k:k + 1], None, ALU.is_ge))
            dve.sem_inc(past_set, 1)
            dve.wait_ge(past_summed, 1)
            for k in range(2):
                link(nc.vector.tensor_scalar(sect[:, k, :], bank[2 + k][0:1, 0:MAXSEC], float(NC - 1), None, ALU.min))
            dve.sem_inc(sect_set, 1)

            dve.wait_ge(edges_in[2], 16)

            def rank_group(g, i, h, first=False):
                link, count = links(dve, rank_step, g * RANK_STEPS)
                dve.wait_ge(rows_in[h], i * 64 + 64)
                for k in range(2):
                    nc.vector.tensor_scalar(oh_loT[k][:, :], lorow[k][h][:, :], part[0:LO, :], None, ALU.is_equal)
                    link(nc.vector.scalar_tensor_tensor(
                        pg[k][:, :, :].rearrange("l t h -> l h t"), pref[k][:, :, bass.ds(g * GT, GT)],
                        basecol[:, k:k + 1], hist[k][:, :, bass.ds(g * GT, GT)], ALU.add, ALU.subtract))
                    link(nc.vector.tensor_scalar(pg_hi[k][:, :, :], pg[k][:, :, :], 256 * MAGIC, -256 * MAGIC,
                                                 ALU.add, ALU.add))
                    link(nc.vector.tensor_tensor(pg_lo[k][:, :, :], pg[k][:, :, :], pg_hi[k][:, :, :], ALU.subtract))
                dve.sem_inc(loT_set, 1)
                for k in range(2):
                    link(nc.vector.tensor_scalar(blk_g[k][:, :], blk[k][:, bass.ds(g * GT, GT)], 1.0, None, ALU.mult))
                    nc.vector.tensor_tensor(
                        hsel[k][:, :, :], iota_f[0:EP, 0:HI].unsqueeze(1).to_broadcast([EP, GT, HI]),
                        hi[k][:, bass.ds(g * GT, GT)].unsqueeze(2).to_broadcast([EP, GT, HI]), ALU.is_equal)
                    for t in range(GT):
                        last = nc.vector.scalar_tensor_tensor(
                            unused[t], blkrow[k][h][:, t * EP:(t + 1) * EP], blk_g[k][:, t:t + 1], ltri[:, :],
                            ALU.is_equal, ALU.mult, accum_out=in_tile[k][:, t:t + 1])
                    link(last)
                dve.sem_inc(rows_used, 1)
                dve.wait_ge(before_done, g + 1)
                for k in range(2):
                    link(nc.vector.tensor_tensor(hsel[k][:, :, :], hsel[k][:, :, :],
                                                 bank[4 + k][0:EP, 0:GT * HI].rearrange("e (t h) -> e t h", h=HI),
                                                 ALU.mult))
                    link(nc.vector.tensor_reduce(before[k][:, :], hsel[k][:, :, :], AX_X, ALU.add))
                    link(nc.vector.tensor_tensor(before[k][:, :], before[k][:, :], in_tile[k][:, :], ALU.add))
                    link(nc.vector.tensor_scalar(row21[k][:, :], bc[k][:, bass.ds(g * GT, GT)], 1.0, None, ALU.mult))
                    link(nc.vector.scalar_tensor_tensor(row21[k][:, :], before[k][:, :], float(BPC), row21[k][:, :],
                                                        ALU.mult, ALU.add))
                if not first:
                    dve.wait_ge(rec_out[h], i * (GT * 16))
                link(nc.vector.tensor_copy(srow[h][:, :], row21[0][:, :]))
                link(nc.vector.tensor_copy(rec[h][:, :, 2:3].bitcast(U32).rearrange("e t o -> e (t o)"), row21[1][:, :]))
                for c, a in ((0, jn[0]), (6, jn[1]), (7, jn[1])):
                    link(nc.vector.tensor_scalar(rec[h][:, :, c:c + 1].rearrange("e t o -> e (t o)"),
                                                 a[:, bass.ds(g * GT, GT)], 1.0, None, ALU.mult))
                link(nc.vector.tensor_scalar(rec[h][:, :, 1:2].bitcast(I32).rearrange("e t o -> e (t o)"),
                                             key_i[1][:, bass.ds(g * GT, GT)], 1.0, None, ALU.mult))
                link(nc.vector.tensor_scalar(rec[h][:, :, 3:3 + DIM], attr_sb[:, bass.ds(g * GT, GT), :], 1.0, None,
                                             ALU.mult))
                dve.sem_inc(rec_set, 1)
                return count[0]

            RANK_STEPS = 27
            for h in range(2):
                rank_group(h, 0, h, first=True)
            with dve.Fori(1, NG // 2) as i:
                for h in range(2):
                    n = rank_group(i * 2 + h, i, h)
                    assert n == RANK_STEPS, n
            prep_vector(dve)



class Keep:
    pass


def keep_tiles(nc, ctx):
    k = Keep()

    def sb(name, shape, dt=F32):
        return ctx.enter_context(nc.sbuf_tensor(name, shape, dt))

    k.sect = sb("sect", [1, 2, MAXSEC], I32)
    k.sect_count = sb("sect_count", [1, 3], I32)
    k.ident = sb("ident", [P, P])
    return k


def keep_node_tiles(nc, ctx, k):
    def sb(name, shape, dt=F32):
        return ctx.enter_context(nc.sbuf_tensor(name, shape, dt))

    k.iota_j = sb("iota_j", [P, NB])
    k.bmask = sb("bmask", [CN, BPC])
    k.pieces = sb("pieces", [P, 4, KS])
    k.x = sb("x_sb", [CN, NC, FEAT])
    k.tab_a = sb("tab_a", [CN, NC, TROW])
    k.er = sb("er", [CN, NC, HEADS])
    k.wc = sb("wc", [FEAT + 1, HEADS, HW])
    k.gh = sb("gh", [CN, NC, G3])
    k.bih = sb("bih", [CN, G3])
    k.inv_deg = sb("inv_deg", [CN, NC])
    k.shift = sb("shift", [CN, NC, DIM])


def hat_weights(nc, link, k, pos, w, rise, fall, blocks):
    def knots(row):
        return k.pieces[:, row:row + 1, :].to_broadcast([P, blocks * DIM, KS])
    wv, rv, fv = (t.rearrange("p b d i -> p (b d) i") for t in (w, rise, fall))
    pv = pos.rearrange("p b d -> p (b d)").unsqueeze(2).to_broadcast([P, blocks * DIM, KS])
    nc.vector.tensor_tensor(rv, pv, knots(0), ALU.add)
    link(nc.vector.tensor_tensor(fv, knots(2), pv, ALU.subtract))
    nc.vector.tensor_tensor(rv, rv, knots(1), ALU.max)
    link(nc.vector.tensor_tensor(fv, fv, knots(3), ALU.max))
    link(nc.vector.tensor_tensor(wv, rv, fv, ALU.min))


def layer_norm(nc, dve, link, x, xm, sq, stat, h, var_set, sd_set, at):
    shape = [CN, NC, FEAT]
    link(nc.vector.tensor_reduce(stat[:, 0, :], x, AX_X, ALU.add))
    link(nc.vector.tensor_scalar(stat[:, 0, :], stat[:, 0, :], 1.0 / FEAT, None, ALU.mult))
    link(nc.vector.tensor_tensor(xm[:, :, :], x, stat[:, 0, :].unsqueeze(2).to_broadcast(shape), ALU.subtract))
    link(nc.vector.tensor_tensor(sq[:, :, :], xm[:, :, :], xm[:, :, :], ALU.mult))
    link(nc.vector.tensor_reduce(stat[:, 1, :], sq[:, :, :], AX_X, ALU.add))
    link(nc.vector.tensor_scalar(stat[:, 1, :], stat[:, 1, :], 1.0 / FEAT, 1e-5, ALU.mult, ALU.add))
    dve.sem_inc(var_set, 1)
    dve.wait_ge(sd_set, at)
    link(nc.vector.reciprocal(stat[:, 3, :], stat[:, 2, :]))
    link(nc.vector.tensor_tensor(xm[:, :, :], xm[:, :, :], stat[:, 3, :].unsqueeze(2).to_broadcast(shape), ALU.mult))
    link(nc.vector.tensor_scalar(h, xm[:, :, :], 0.0, None, ALU.max))


def rows_of(dram, f):
    return dram.rearrange("(c p) f -> p c f", p=CN)


def build_send(nc, a, k, slots_dram, drows_dram, h1_dram):
    with ExitStack() as ctx:
        def sb(name, shape, dt=F32):
            return ctx.enter_context(nc.sbuf_tensor(name, shape, dt))

        def sem(name):
            return ctx.enter_context(nc.semaphore(name))

        w1 = sb("w1", [K + 1, HID + 1])
        b1 = sb("b1", [CN, HID])
        slot = sb("slot", [P, BPC, SREC])
        oh = sb("oh", [P, BPC, NB])
        ohT = sb("ohT", [CN, P])
        bd = sb("bd", [CN, BPC, TROW])
        posd = [sb(f"posd{g}", [P, GB], U32) for g in range(NGR)]
        load = [sb(f"load{g}", [P, GB, DREC]) for g in range(NGR)]
        pos = sb("pos", [P, BPC, DIM])
        rise = sb("rise", [P, BPC, DIM, KS])
        fall = sb("fall", [P, BPC, DIM, KS])
        hat = sb("hat", [P, BPC, DIM, KS])
        uv = [sb(f"uv{g}", [P, GB, KS, KS]) for g in range(NGR)]
        bas = [sb(f"bas{g}", [P, GB, K + 1]) for g in range(NGR)]
        t1 = sb("t1", [K + 1, CN])
        acc = sb("acc", [CN, NC, HID + 1])
        v1 = sb("v1", [CN, NC, HID])
        e1 = sb("e1", [CN, NC, HID])
        bank = [ctx.enter_context(nc.psum_tensor(f"send_bank{i}", [P, 512], F32)) for i in range(8)]

        w1_in = sem("w1_in")
        const_step = sem("const_step")
        const2_step = sem("const2_step")
        slot_in = sem("slot_in")
        slot_used = sem("slot_used")
        oh_set = sem("oh_set")
        ohT_done = sem("ohT_done")
        ohT_set = sem("ohT_set")
        bd_set = sem("bd_set")
        spread_done = sem("spread_done")
        load_set = sem("load_set")
        posd_set = sem("posd_set")
        sent = [sem(f"sent{g}") for g in range(NGR)]
        bas_set = sem("bas_set")
        t1_done = sem("t1_done")
        t1_set = sem("t1_set")
        out1_done = sem("out1_done")
        acc_set = sem("acc_set")
        sec_step = sem("sec_step2")
        neg_set = sem("neg_set")
        exp_set = sem("exp_set")
        h1_set = sem("h1_set")
        h1_out = sem("h1_out")
        end_step = sem("end_step")

        block = ctx.enter_context(nc.Block())

        @block.sync
        def _(sp):
            sp.wait_ge(const_step, 4)
            sp.dma_start(w1[0:K, 0:HID], a["L1_gnn_stn1_w"].rearrange("k o f -> k (o f)")).then_inc(w1_in, 16)
            sp.dma_start(b1[:, :], a["L1_gnn_stn1_b"].rearrange("(o f) -> o f", o=1).to_broadcast([CN, HID]))\
              .then_inc(w1_in, 16)

            def load_slots(s):
                sp.dma_start(slot[:, :, :].rearrange("p b w -> p (b w)"),
                             slots_dram[bass.ds(s * SROWS, SROWS), :].rearrange("(p b) w -> p (b w)", b=BPC))\
                  .then_inc(slot_in, 16)

            sections = sp.value_load(k.sect_count[0:1, 0:1], min_val=NC, max_val=MAXSEC - 1)
            load_slots(0)
            with sp.Fori(1, sections) as s:
                sp.wait_ge(slot_used, s)
                load_slots(s)
            sp.wait_ge(h1_set, 1)
            sp.dma_start(rows_of(h1_dram, HID), v1[:, :, :]).then_inc(h1_out, 16)
            sp.wait_ge(h1_out, 16)

        @block.gpsimd
        def _(pool):
            nc.gpsimd.iota(k.iota_j[:, :], pattern=[[1, NB]], base=0, channel_multiplier=0,
                           allow_small_or_imprecise_dtypes=True).then_inc(const_step, 1)
            nc.gpsimd.memset(k.bmask[:, :], 1.0).then_inc(const_step, 1)
            nc.gpsimd.memset(w1[:, :], 0.0).then_inc(const_step, 1)
            pool.wait_ge(const_step, 3)
            nc.gpsimd.affine_select(out=w1[:, HID:HID + 1], in_=w1[:, HID:HID + 1], compare_op=ALU.not_equal, fill=1.0,
                                    base=-K, pattern=[[0, 1]], channel_multiplier=1).then_inc(const_step, 1)
            nc.gpsimd.affine_select(out=k.bmask[:, :], in_=k.bmask[:, :], compare_op=ALU.is_ge, fill=0.0,
                                    base=0, pattern=[[-NB, BPC]], channel_multiplier=1).then_inc(const_step, 1)
            pool.wait_ge(const_step, 5)
            nc.gpsimd.affine_select(out=k.bmask[:, :], in_=k.bmask[:, :], compare_op=ALU.is_ge, fill=0.0,
                                    base=NB - 1, pattern=[[NB, BPC]], channel_multiplier=-1).then_inc(const_step, 1)
            sections = pool.value_load(k.sect_count[0:1, 0:1], min_val=NC, max_val=MAXSEC - 1)

            def send(s):
                for g in range(NGR):
                    pool.wait_ge(load_set, s * NGR + (g + 1))
                    pool.wait_ge(posd_set, s * NGR + (g + 1))
                    pool.nop(nofuse=True)
                    for b in range(GB):
                        nc.gpsimd.indirect_dma_start(
                            drows_dram[:, :], bass.IndirectOffsetOnAxis(ap=posd[g][:, b:b + 1], axis=0),
                            load[g][:, b, :], None, bounds_check=MAXSEC * SROWS - 1, oob_is_err=False)\
                            .then_inc(sent[g], 16)
            send(0)
            with pool.Fori(1, sections) as s:
                send(s)
            for g in range(NGR):
                pool.wait_ge(sent[g], sections * (GB * 16))

        @block.scalar
        def _(act):
            sections = act.value_load(k.sect_count[0:1, 0:1], min_val=NC, max_val=MAXSEC - 1)

            def section(s, first):
                act.wait_ge(ohT_done, s + 1)
                if not first:
                    act.wait_ge(spread_done, s * NGR)
                nc.scalar.copy(ohT[:, :], bank[0][0:CN, 0:P]).then_inc(ohT_set, 1)
                for g in range(NGR):
                    act.wait_ge(spread_done, s * NGR + (g + 1))
                    if not first:
                        act.wait_ge(sent[g], s * (GB * 16))
                    nc.scalar.copy(load[g][:, :, 0:TROW],
                                   bank[1 + g][:, 0:GB * TROW].rearrange("p (b f) -> p b f", b=GB)).then_inc(load_set, 1)
                act.wait_ge(t1_done, s + 1)
                if not first:
                    act.wait_ge(out1_done, s)
                nc.scalar.copy(t1[:, :], bank[4][0:K + 1, 0:CN]).then_inc(t1_set, 1)

            section(0, True)
            with act.Fori(1, sections) as s:
                section(s, False)
            act.wait_ge(neg_set, 1)
            nc.scalar.activation(e1[:, :, :], e1[:, :, :], ACT.Exp).then_inc(exp_set, 1)

        @block.tensor
        def _(pe):
            pe.wait_ge(w1_in, 32)
            sections = pe.value_load(k.sect_count[0:1, 0:1], min_val=NC, max_val=MAXSEC - 1)

            def section(s, first):
                pe.wait_ge(oh_set, s + 1)
                nc.tensor.transpose(bank[0][0:CN, 0:P], oh[:, :, :].rearrange("p b j -> p (b j)"), k.ident[:, :])\
                    .then_inc(ohT_done, 1)
                pe.wait_ge(ohT_set, s + 1)
                pe.wait_ge(bd_set, s + 1)
                for g in range(NGR):
                    if not first:
                        pe.wait_ge(load_set, s * NGR - (NGR - 1 - g))
                    nc.tensor.matmul(bank[1 + g][:, 0:GB * TROW], ohT[:, :],
                                     bd[:, g * GB:(g + 1) * GB, :].rearrange("n b f -> n (b f)"),
                                     start=True, stop=True).then_inc(spread_done, 1)
                if not first:
                    pe.wait_ge(t1_set, s)
                for g in range(NGR):
                    pe.wait_ge(bas_set, s * NGR + (g + 1))
                    for b in range(g * GB, (g + 1) * GB):
                        last = nc.tensor.matmul(bank[4][0:K + 1, b * NB:(b + 1) * NB], bas[g][:, b - g * GB, :],
                                                oh[:, b, :], start=True, stop=True)
                last.then_inc(t1_done, 1)
                pe.wait_ge(t1_set, s + 1)
                if not first:
                    pe.wait_ge(acc_set, s)
                nc.tensor.matmul(bank[5][0:CN, 0:HID + 1], t1[:, :], w1[:, :], start=True, stop=True)\
                    .then_inc(out1_done, 1)

            section(0, True)
            with pe.Fori(1, sections) as s:
                section(s, False)

        @block.vector
        def _(dve):
            link, count = links(dve, const2_step)
            for row, (v, odd, at) in enumerate(((0.0, 0.0, None), (0.0, -BIG, 1), (0.0, 0.0, None), (0.0, -BIG, 3))):
                if row in (0, 2):
                    for i in range(KS):
                        val = (BIG if i == 0 else 1.0 - i) if row == 0 else (BIG if i == KS - 1 else 1.0 + i)
                        last = nc.vector.memset(k.pieces[:, row, i:i + 1], val)
                else:
                    link(nc.vector.memset(k.pieces[:, row, :], v))
                    last = nc.vector.memset(k.pieces[:, row, at:at + 1], odd)
            for g in range(NGR):
                last = nc.vector.memset(bas[g][:, :, K:K + 1], 1.0)
            link(nc.vector.memset(acc[:, :, :], 0.0))
            dve.wait_ge(const_step, 6)
            sections = dve.value_load(k.sect_count[0:1, 0:1], min_val=NC, max_val=MAXSEC - 1)

            def add_out(s_last):
                c = dve.value_load(k.sect[0:1, 0, bass.ds(s_last, 1)], min_val=0, max_val=NC - 1)
                sl = acc[:, bass.ds(c, 1), :].rearrange("n c f -> n (c f)")
                return nc.vector.tensor_tensor(sl, sl, bank[5][0:CN, 0:HID + 1], ALU.add)

            def section(s, first):
                link, count = links(dve, sec_step, s * SEND_STEPS)
                c = dve.value_load(k.sect[0:1, 0, bass.ds(s, 1)], min_val=0, max_val=NC - 1)
                dve.wait_ge(slot_in, s * 16 + 16)
                if not first:
                    dve.wait_ge(t1_done, s)
                link(nc.vector.tensor_tensor(oh[:, :, :], k.iota_j[:, :].unsqueeze(1).to_broadcast([P, BPC, NB]),
                                             slot[:, :, 0:1].to_broadcast([P, BPC, NB]), ALU.is_equal))
                dve.sem_inc(oh_set, 1)
                if not first:
                    dve.wait_ge(spread_done, s * NGR)
                link(nc.vector.tensor_tensor(
                    bd[:, :, :], k.tab_a[:, bass.ds(c, 1), :].to_broadcast([CN, BPC, TROW]),
                    k.bmask[:, :].unsqueeze(2).to_broadcast([CN, BPC, TROW]), ALU.mult))
                dve.sem_inc(bd_set, 1)
                for g in range(NGR):
                    if not first:
                        dve.wait_ge(sent[g], s * (GB * 16))
                    part = slot[:, g * GB:(g + 1) * GB, :]
                    nc.vector.tensor_copy(load[g][:, :, DREC - 1:DREC], part[:, :, 6:7])
                    nc.vector.tensor_copy(posd[g][:, :], part[:, :, 2:3].bitcast(U32).rearrange("p b o -> p (b o)"))\
                        .then_inc(posd_set, 1)
                dve.wait_ge(posd_set, s * NGR + NGR)
                link(nc.vector.tensor_scalar(pos[:, :, :], slot[:, :, 3:3 + DIM], float(KS - 1), None, ALU.mult))
                dve.sem_inc(slot_used, 1)
                hat_weights(nc, link, k, pos[:, :, :], hat[:, :, :, :], rise[:, :, :, :], fall[:, :, :, :], BPC)
                for g in range(NGR):
                    w = hat[:, g * GB:(g + 1) * GB, :, :]
                    link(nc.vector.tensor_tensor(uv[g][:, :, :, :], w[:, :, 0, :].unsqueeze(3).to_broadcast([P, GB, KS, KS]),
                                                 w[:, :, 1, :].unsqueeze(2).to_broadcast([P, GB, KS, KS]), ALU.mult))
                    nc.vector.tensor_tensor(
                        bas[g][:, :, 0:K].rearrange("p b (u i) -> p b u i", i=KS),
                        uv[g][:, :, :, :].rearrange("p b i j -> p b (i j)").unsqueeze(3).to_broadcast([P, GB, KS * KS, KS]),
                        w[:, :, 2, :].unsqueeze(2).to_broadcast([P, GB, KS * KS, KS]), ALU.mult).then_inc(bas_set, 1)
                if not first:
                    dve.wait_ge(out1_done, s)
                    link(add_out(s - 1))
                    dve.sem_inc(acc_set, 1)
                else:
                    dve.sem_inc(sec_step, 1)
                return count[0]

            SEND_STEPS = 10
            section(0, True)
            with dve.Fori(1, sections) as s:
                n = section(s, False)
                assert n == SEND_STEPS, n
            link, count = links(dve, end_step)
            dve.wait_ge(out1_done, sections)
            link(add_out(sections - 1))
            link(nc.vector.tensor_scalar(k.inv_deg[:, :], acc[:, :, HID:HID + 1].rearrange("n c o -> n (c o)"), 1.0, None,
                                         ALU.max))
            link(nc.vector.reciprocal(k.inv_deg[:, :], k.inv_deg[:, :]))
            link(nc.vector.tensor_tensor(v1[:, :, :], acc[:, :, 0:HID],
                                         k.inv_deg[:, :].unsqueeze(2).to_broadcast([CN, NC, HID]), ALU.mult))
            link(nc.vector.tensor_tensor(v1[:, :, :], v1[:, :, :], b1[:, :].unsqueeze(1).to_broadcast([CN, NC, HID]),
                                         ALU.add))
            link(nc.vector.tensor_scalar(e1[:, :, :], v1[:, :, :], 0.0, None, ALU.min))
            dve.sem_inc(neg_set, 1)
            link(nc.vector.tensor_scalar(v1[:, :, :], v1[:, :, :], 0.0, None, ALU.max))
            dve.wait_ge(exp_set, 1)
            link(nc.vector.scalar_tensor_tensor(v1[:, :, :], e1[:, :, :], -1.0, v1[:, :, :], ALU.add, ALU.add))
            dve.sem_inc(h1_set, 1)


def conv_tiles(nc, ctx, fi, prefix):
    t = Keep()

    def sb(name, shape, dt=F32):
        return ctx.enter_context(nc.sbuf_tensor(prefix + name, shape, dt))

    t.slot = sb("slot", [P, BPC, SREC])
    t.index = [sb(f"index{g}", [P, GB], U32) for g in range(NGR)]
    t.oh = sb("oh", [P, BPC, NB])
    t.rise = sb("rise", [P, BPC, DIM, KS])
    t.fall = sb("fall", [P, BPC, DIM, KS])
    t.hat = sb("hat", [P, BPC, DIM, KS])
    t.uv = [sb(f"uv{g}", [P, GB, KS, KS]) for g in range(NGR)]
    t.bas = [sb(f"bas{g}", [P, GB, K]) for g in range(NGR)]
    t.mixed = [sb(f"mixed{g}", [P, GB, NB, fi]) for g in range(NGR)]
    t.sums = sb("sums", [K, CN, fi])
    return t


def basis_group(nc, t, g, link):
    w = t.hat[:, g * GB:(g + 1) * GB, :, :]
    link(nc.vector.tensor_tensor(t.uv[g][:, :, :, :], w[:, :, 0, :].unsqueeze(3).to_broadcast([P, GB, KS, KS]),
                                 w[:, :, 1, :].unsqueeze(2).to_broadcast([P, GB, KS, KS]), ALU.mult))
    return nc.vector.tensor_tensor(
        t.bas[g][:, :, :].rearrange("p b (u i) -> p b u i", i=KS),
        t.uv[g][:, :, :, :].rearrange("p b i j -> p b (i j)").unsqueeze(3).to_broadcast([P, GB, KS * KS, KS]),
        w[:, :, 2, :].unsqueeze(2).to_broadcast([P, GB, KS * KS, KS]), ALU.mult)


def build_mid(nc, a, k, slots_dram, drows_dram, h1_dram, acc, gacc):
    with ExitStack() as ctx:
        def sb(name, shape, dt=F32):
            return ctx.enter_context(nc.sbuf_tensor(name, shape, dt))

        def sem(name):
            return ctx.enter_context(nc.semaphore(name))

        t = conv_tiles(nc, ctx, HID, "mid_")
        rows = [sb(f"mid_rows{g}", [P, GB, HID]) for g in range(NGR)]
        w2 = sb("w2", [K, HID, HID])
        pos = sb("mid_pos", [P, BPC, DIM])
        drow = sb("drow", [P, BPC, DREC])
        drow_m = [sb(f"drow_m{h}", [P, BPC, DREC]) for h in range(2)]
        masked_m = [sb(f"masked_m{h}", [P, HEADS, BPC, NB]) for h in range(2)]
        top = [sb(f"top{h}", [CN, HEADS]) for h in range(2)]
        ohd = sb("ohd", [P, BPC, NB])
        pen = sb("pen", [P, BPC, NB])
        masked = sb("masked", [P, BPC, NB, HEADS])
        m_el = sb("m_el", [CN, NC, HEADS])
        er_m = sb("er_m", [CN, NC, 2 * HEADS])
        ohdT = sb("ohdT", [CN, P])
        bde = sb("bde", [CN, BPC, 2 * HEADS])
        score = sb("score", [P, BPC, HEADS])
        wexp = sb("wexp", [P, BPC, HEADS])
        bank = [ctx.enter_context(nc.psum_tensor(f"mid_bank{i}", [P, 512], F32)) for i in range(8)]

        w2_in = sem("w2_in")
        slot_in = sem("mid_slot_in")
        slot_used = sem("mid_slot_used")
        index_set = sem("mid_index_set")
        rows_in = [sem(f"mid_rows_in{g}") for g in range(NGR)]
        mixed_set = sem("mid_mixed_set")
        sum_done = sem("mid_sum_done")
        sum_set = sem("mid_sum_set")
        out_done = sem("mid_out_done")
        acc_set = sem("mid_acc_set")
        mid_step = sem("mid_step")
        max_step = sem("max_step")
        init_step = sem("mid_init_step")
        drow_in = [sem(f"drow_in{h}") for h in range(2)]
        drow_used = sem("drow_used")
        masked_set = sem("masked_set")
        masked_turned = sem("masked_turned")
        tops_set = sem("tops_set")
        w_in = sem("att_in")
        ohd_set = sem("ohd_set")
        ohdT_done = sem("ohdT_done")
        ohdT_set = sem("ohdT_set")
        bde_set = sem("bde_set")
        erm_done = sem("erm_done")
        score_set = sem("score_set")
        wexp_set = sem("wexp_set")
        weights_set = sem("weights_set")
        att_done = sem("att_done")
        gacc_set = sem("gacc_set")
        gacc_clear = sem("gacc_clear")

        block = ctx.enter_context(nc.Block())

        @block.sync
        def _(sp):
            def load_slots(s):
                sp.dma_start(t.slot[:, :, :].rearrange("p b w -> p (b w)"),
                             slots_dram[bass.ds(s * SROWS, SROWS), :].rearrange("(p b) w -> p (b w)", b=BPC))\
                  .then_inc(slot_in, 16)

            def load_drows(s, tile, signal):
                sp.dma_start(tile[:, :, :].rearrange("p b w -> p (b w)"),
                             drows_dram[bass.ds(s * SROWS, SROWS), :].rearrange("(p b) w -> p (b w)", b=BPC))\
                  .then_inc(signal, 16)

            sections = sp.value_load(k.sect_count[0:1, 0:1], min_val=NC, max_val=MAXSEC - 1)
            pairs = sp.value_load(k.sect_count[0:1, 2:3], min_val=1, max_val=MAXSEC // 2)
            load_slots(0)
            for h in range(2):
                load_drows(h, drow_m[h], drow_in[h])
            sp.dma_start(w2[:, :, :], a["L1_gnn_stn2_w"]).then_inc(w2_in, 16)
            with sp.Fori(1, pairs) as i:
                for h in range(2):
                    sp.wait_ge(drow_used, i * 2 + (h - 1))
                    load_drows(i * 2 + h, drow_m[h], drow_in[h])
            load_drows(0, drow, w_in)
            with sp.Fori(1, sections) as s:
                sp.wait_ge(slot_used, s)
                sp.nop(nofuse=True)
                sp.wait_ge(index_set, s * NGR)
                sp.nop(nofuse=True)
                load_slots(s)
                sp.wait_ge(att_done, s)
                load_drows(s, drow, w_in)
            sp.wait_ge(slot_used, sections)
            sp.nop(nofuse=True)
            sp.wait_ge(index_set, sections * NGR)
            sp.nop(nofuse=True)
            load_slots(sections)
            sp.wait_ge(slot_in, sections * 16 + 16)
            sp.nop(nofuse=True)

        @block.gpsimd
        def _(pool):
            sections = pool.value_load(k.sect_count[0:1, 0:1], min_val=NC, max_val=MAXSEC - 1)

            def fetch(s, first):
                for g in range(NGR):
                    pool.wait_ge(index_set, s * NGR + (g + 1))
                    if not first:
                        pool.wait_ge(mixed_set, s * NGR - (NGR - 1 - g))
                    pool.nop(nofuse=True)
                    for b in range(GB):
                        nc.gpsimd.indirect_dma_start(
                            rows[g][:, b, :], None, h1_dram[:, :],
                            bass.IndirectOffsetOnAxis(ap=t.index[g][:, b:b + 1], axis=0)).then_inc(rows_in[g], 16)
            fetch(0, True)
            nc.gpsimd.memset(gacc[:, :, :], 0.0).then_inc(gacc_clear, 1)
            with pool.Fori(1, sections) as s:
                fetch(s, False)

        @block.scalar
        def _(act):
            def indices(g):
                nc.scalar.copy(t.index[g][:, :], t.slot[:, g * GB:(g + 1) * GB, 1:2].bitcast(U32)
                               .rearrange("p b o -> p (b o)")).then_inc(index_set, 1)

            act.wait_ge(slot_in, 16)
            for g in range(NGR):
                indices(g)
            sections = act.value_load(k.sect_count[0:1, 0:1], min_val=NC, max_val=MAXSEC - 1)

            def section(s, first):
                act.wait_ge(ohdT_done, s + 1)
                if not first:
                    act.wait_ge(erm_done, s)
                nc.scalar.copy(ohdT[:, :], bank[4][0:CN, 0:P]).then_inc(ohdT_set, 1)
                for g in range(NGR):
                    act.wait_ge(slot_in, s * 16 + 32)
                    act.wait_ge(rows_in[g], s * (GB * 16) + GB * 16)
                    indices(g)
                    for b in range(g * GB, (g + 1) * GB):
                        act.wait_ge(sum_done, s * BPC + (b + 1))
                        if b == 0 and not first:
                            act.wait_ge(out_done, s)
                        nc.scalar.copy(t.sums[:, b * NB:(b + 1) * NB, :].rearrange("k n f -> k (n f)"),
                                       bank[b % 3][0:K, 0:NB * HID]).then_inc(sum_set, 1)
                        if b == GB + 2:
                            act.wait_ge(score_set, s + 1)
                            nc.scalar.activation(wexp[:, :, :], score[:, :, :], ACT.Exp).then_inc(wexp_set, 1)

            section(0, True)
            with act.Fori(1, sections) as s:
                section(s, False)

        @block.tensor
        def _(pe):
            sections = pe.value_load(k.sect_count[0:1, 0:1], min_val=NC, max_val=MAXSEC - 1)

            def turn(s, h, first):
                pe.wait_ge(masked_set, s + 1)
                if not first:
                    pe.wait_ge(tops_set, s - 1)
                for q in range(HEADS):
                    last = nc.tensor.transpose(bank[h][0:CN, q * P:(q + 1) * P],
                                               masked_m[h][:, q, :, :].rearrange("p b j -> p (b j)"), k.ident[:, :])
                last.then_inc(masked_turned, 1)
            pairs = pe.value_load(k.sect_count[0:1, 2:3], min_val=1, max_val=MAXSEC // 2)
            for h in range(2):
                turn(h, h, True)
            with pe.Fori(1, pairs) as i:
                for h in range(2):
                    turn(i * 2 + h, h, False)
            pe.wait_ge(w2_in, 16)

            def section(s, first):
                pe.wait_ge(ohd_set, s + 1)
                nc.tensor.transpose(bank[4][0:CN, 0:P], ohd[:, :, :].rearrange("p b j -> p (b j)"), k.ident[:, :])\
                    .then_inc(ohdT_done, 1)
                for g in range(NGR):
                    pe.wait_ge(mixed_set, s * NGR + (g + 1))
                    for b in range(g * GB, (g + 1) * GB):
                        if b >= 3 or not first:
                            pe.wait_ge(sum_set, s * BPC + (b - 2))
                        nc.tensor.matmul(bank[b % 3][0:K, 0:NB * HID], t.bas[g][:, b - g * GB, :],
                                         t.mixed[g][:, b - g * GB, :, :].rearrange("p j f -> p (j f)"),
                                         start=True, stop=True).then_inc(sum_done, 1)
                    if g == 0:
                        pe.wait_ge(ohdT_set, s + 1)
                        pe.wait_ge(bde_set, s + 1)
                        nc.tensor.matmul(bank[5][:, 0:BPC * 2 * HEADS], ohdT[:, :],
                                         bde[:, :, :].rearrange("n b w -> n (b w)"), start=True, stop=True)\
                            .then_inc(erm_done, 1)
                pe.wait_ge(weights_set, s + 1)
                if not first:
                    pe.wait_ge(gacc_set, s)
                for b in range(BPC):
                    last = nc.tensor.matmul(bank[6][0:FEAT + 1, b * NB * HEADS:(b + 1) * NB * HEADS],
                                            drow[:, b, 0:FEAT + 1],
                                            masked[:, b, :, :].rearrange("p j h -> p (j h)"), start=True, stop=True)
                last.then_inc(att_done, 1)
                pe.wait_ge(sum_set, s * BPC + BPC)
                if not first:
                    pe.wait_ge(acc_set, s)
                for i in range(HID):
                    last = nc.tensor.matmul(bank[3][0:CN, 0:HID], t.sums[:, :, i], w2[:, i, :],
                                            start=(i == 0), stop=(i == HID - 1))
                last.then_inc(out_done, 1)

            section(0, True)
            with pe.Fori(1, sections) as s:
                section(s, False)

        @block.vector
        def _(dve):
            sections = dve.value_load(k.sect_count[0:1, 0:1], min_val=NC, max_val=MAXSEC - 1)
            link, count = links(dve, init_step)
            nc.vector.memset(acc[:, :, :], 0.0)
            link(nc.vector.memset(m_el[:, :, :], -BIG))

            def one_hot_d(tile):
                return nc.vector.tensor_tensor(
                    ohd[:, :, :], k.iota_j[:, :].unsqueeze(1).to_broadcast([P, BPC, NB]),
                    tile[:, :, DREC - 1:DREC].to_broadcast([P, BPC, NB]), ALU.is_equal)

            def mask(s, i, h, link):
                dve.wait_ge(drow_in[h], i * 16 + 16)
                link(one_hot_d(drow_m[h]))
                link(nc.vector.tensor_scalar(pen[:, :, :], ohd[:, :, :], -1.0, BIG, ALU.add, ALU.mult))
                link(nc.vector.tensor_tensor(
                    masked_m[h][:, :, :, :].rearrange("p q b j -> p b j q"),
                    pen[:, :, :].unsqueeze(3).to_broadcast([P, BPC, NB, HEADS]),
                    drow_m[h][:, :, FEAT + 1:TROW].unsqueeze(2).to_broadcast([P, BPC, NB, HEADS]), ALU.add))
                dve.sem_inc(masked_set, 1)
                dve.sem_inc(drow_used, 1)

            def find_max(s, h, link):
                dve.wait_ge(masked_turned, s + 1)
                link(nc.vector.tensor_reduce(top[h][:, :], bank[h][0:CN, 0:HEADS * P].rearrange("n (q e) -> n q e", e=P),
                                             AX_X, ALU.max))
                c = dve.value_load(k.sect[0:1, 1, bass.ds(s, 1)], min_val=0, max_val=NC - 1)
                sl = m_el[:, bass.ds(c, 1), :].rearrange("n c q -> n (c q)")
                link(nc.vector.tensor_tensor(sl, sl, top[h][:, :], ALU.max))
                dve.sem_inc(tops_set, 1)

            pairs = dve.value_load(k.sect_count[0:1, 2:3], min_val=1, max_val=MAXSEC // 2)

            def pair(i):
                link, count = links(dve, max_step, i * 10)
                for h in range(2):
                    mask(i * 2 + h, i, h, link)
                for h in range(2):
                    find_max(i * 2 + h, h, link)
                assert count[0] == 10
            pair(0)
            with dve.Fori(1, pairs) as i:
                pair(i)
            link(nc.vector.tensor_copy(er_m[:, :, 0:HEADS], k.er[:, :, :]))
            link(nc.vector.tensor_tensor(m_el[:, :, :], m_el[:, :, :], k.er[:, :, :], ALU.add))
            link(nc.vector.scalar_tensor_tensor(er_m[:, :, HEADS:2 * HEADS], m_el[:, :, :], 0.2, m_el[:, :, :],
                                                ALU.mult, ALU.max))

            def add_outs(s_last):
                cs = dve.value_load(k.sect[0:1, 0, bass.ds(s_last, 1)], min_val=0, max_val=NC - 1)
                sl = acc[:, bass.ds(cs, 1), :].rearrange("n c f -> n (c f)")
                link1 = nc.vector.tensor_tensor(sl, sl, bank[3][0:CN, 0:HID], ALU.add)
                cd = dve.value_load(k.sect[0:1, 1, bass.ds(s_last, 1)], min_val=0, max_val=NC - 1)
                sg = gacc[:, bass.ds(cd, 1), :].rearrange("f c w -> f (c w)")
                return link1, nc.vector.tensor_tensor(sg, sg, bank[6][0:FEAT + 1, 0:BPC * NB * HEADS], ALU.add)

            def section(s, first):
                link, count = links(dve, mid_step, s * MID_STEPS)
                dve.wait_ge(slot_in, s * 16 + 16)
                link(nc.vector.tensor_tensor(t.oh[:, :, :], k.iota_j[:, :].unsqueeze(1).to_broadcast([P, BPC, NB]),
                                             t.slot[:, :, 0:1].to_broadcast([P, BPC, NB]), ALU.is_equal))
                link(nc.vector.tensor_scalar(pos[:, :, :], t.slot[:, :, 3:3 + DIM], float(KS - 1), None, ALU.mult))
                dve.sem_inc(slot_used, 1)
                hat_weights(nc, link, k, pos[:, :, :], t.hat[:, :, :, :], t.rise[:, :, :, :], t.fall[:, :, :, :], BPC)
                for g in range(NGR):
                    if not first:
                        dve.wait_ge(sum_done, s * BPC - (NGR - 1 - g) * GB)
                    basis_group(nc, t, g, link)
                    dve.wait_ge(rows_in[g], s * (GB * 16) + GB * 16)
                    link(nc.vector.tensor_tensor(
                        t.mixed[g][:, :, :, :],
                        t.oh[:, g * GB:(g + 1) * GB, :].unsqueeze(3).to_broadcast([P, GB, NB, HID]),
                        rows[g][:, :, :].unsqueeze(2).to_broadcast([P, GB, NB, HID]), ALU.mult))
                    dve.sem_inc(mixed_set, 1)
                    if g == 1:
                        dve.wait_ge(w_in, s * 16 + 16)
                        link(one_hot_d(drow))
                        dve.sem_inc(ohd_set, 1)
                        if not first:
                            dve.wait_ge(erm_done, s)
                        cd = dve.value_load(k.sect[0:1, 1, bass.ds(s, 1)], min_val=0, max_val=NC - 1)
                        link(nc.vector.tensor_tensor(
                            bde[:, :, :], er_m[:, bass.ds(cd, 1), :].to_broadcast([CN, BPC, 2 * HEADS]),
                            k.bmask[:, :].unsqueeze(2).to_broadcast([CN, BPC, 2 * HEADS]), ALU.mult))
                        dve.sem_inc(bde_set, 1)
                if not first:
                    dve.wait_ge(out_done, s)
                    one, two = add_outs(s - 1)
                    link(one)
                    link(two)
                    dve.sem_inc(acc_set, 1)
                    dve.sem_inc(gacc_set, 1)
                else:
                    dve.sem_inc(mid_step, 2)
                    count[0] += 2
                dve.wait_ge(erm_done, s + 1)
                erm = bank[5][:, 0:BPC * 2 * HEADS].rearrange("p (b w) -> p b w", b=BPC)
                link(nc.vector.tensor_tensor(score[:, :, :], drow[:, :, FEAT + 1:TROW], erm[:, :, 0:HEADS],
                                             ALU.add))
                link(nc.vector.scalar_tensor_tensor(score[:, :, :], score[:, :, :], 0.2, score[:, :, :],
                                                    ALU.mult, ALU.max))
                link(nc.vector.tensor_tensor(score[:, :, :], score[:, :, :], erm[:, :, HEADS:2 * HEADS],
                                             ALU.subtract))
                dve.sem_inc(score_set, 1)
                dve.wait_ge(wexp_set, s + 1)
                link(nc.vector.tensor_tensor(
                    masked[:, :, :, :], ohd[:, :, :].unsqueeze(3).to_broadcast([P, BPC, NB, HEADS]),
                    wexp[:, :, :].unsqueeze(2).to_broadcast([P, BPC, NB, HEADS]), ALU.mult))
                dve.sem_inc(weights_set, 1)
                return count[0]

            MID_STEPS = 19
            dve.wait_ge(gacc_clear, 1)
            section(0, True)
            with dve.Fori(1, sections) as s:
                n = section(s, False)
                assert n == MID_STEPS, n
            dve.wait_ge(out_done, sections)
            one, two = add_outs(sections - 1)
            link, count = links(dve, init_step, 4)
            link(one)
            link(two)


def build_nodes(nc, a, k, acc, gacc, node3_dram):
    with ExitStack() as ctx:
        def sb(name, shape, dt=F32):
            return ctx.enter_context(nc.sbuf_tensor(name, shape, dt))

        def sem(name):
            return ctx.enter_context(nc.semaphore(name))

        b2 = sb("n_b2", [CN, HID])
        b3 = sb("n_b3", [CN, HID])
        b4 = sb("n_b4", [CN, DIM])
        w3 = sb("n_w3", [HID, HID])
        w4 = sb("n_w4", [HID, DIM])
        rden = sb("n_rden", [CN, 2, HEADS])
        gih = [sb(f"n_gih{i}", [CN, HEADS, G3]) for i in range(2)]
        gi = sb("n_gi", [CN, NC, G3])
        v = sb("n_v", [CN, NC, HID])
        e = sb("n_e", [CN, NC, HID])
        y3 = sb("n_y3", [CN, NC, HID])
        yT = [sb(f"n_yT{i}", [HID, 4, CN]) for i in range(2)]
        nn = sb("n_n", [CN, NC, FEAT])
        xm = sb("n_xm", [CN, NC, FEAT])
        sq = sb("n_sq", [CN, NC, FEAT])
        stat = sb("n_stat", [CN, 4, NC])
        node3 = sb("n_node3", [CN, NC, NROW])
        bank = [ctx.enter_context(nc.psum_tensor(f"n_bank{i}", [P, 512], F32)) for i in range(8)]
        NQ = -(-NC // 4)
        SECOND = 2 * NQ + 4
        assert SECOND + NQ == NC

        w_in = sem("n_w_in")
        gi_done = sem("gi_done")
        gi_out = sem("gi_out")
        act_in = sem("act_in")
        act_out = sem("act_out")
        v_set = sem("v_set")
        yT_done = sem("yT_done")
        yT_set = sem("yT_set")
        lin_done = sem("lin_done")
        lin_out = sem("lin_out")
        node3_set = sem("node3_set")
        node3_out = sem("node3_out")
        n_step = sem("n_step")
        var_set = sem("n_var_set")
        sd_set = sem("n_sd_set")

        block = ctx.enter_context(nc.Block())

        def row(name, n, parts):
            return a[name].rearrange("(o f) -> o f", o=1).to_broadcast([parts, n])

        @block.sync
        def _(sp):
            for tile, source in (
                    (b2[:, :], row("L1_gnn_stn2_b", HID, CN)), (w3[:, :], a["L1_gnn_stn3_w"]),
                    (w4[:, :], a["L1_gnn_stn4_w"]), (b3[:, :], row("L1_gnn_stn3_b", HID, CN)),
                    (b4[:, :], row("L1_gnn_stn4_b", DIM, CN))):
                sp.dma_start(tile, source).then_inc(w_in, 16)
            sp.wait_ge(node3_set, 2)
            sp.dma_start(rows_of(node3_dram, NROW), node3[:, :, :]).then_inc(node3_out, 16)
            sp.wait_ge(node3_out, 16)

        @block.gpsimd
        def _(pool):
            nc.gpsimd.memset(node3[:, :, FEAT + DIM:NROW], 0.0).then_inc(node3_set, 1)

        @block.scalar
        def _(act):
            def apply(i, ap, function):
                act.wait_ge(act_in, i)
                nc.scalar.activation(ap, ap, function).then_inc(act_out, 1)

            def turned_rows(base):
                for q in range(NQ):
                    n = min(4, NC - 4 * q)
                    act.wait_ge(yT_done, base + q + 1)
                    if base + q >= 2:
                        act.wait_ge(lin_done, base + q - 1)
                    nc.scalar.copy(yT[(base + q) % 2][:, 0:n, :].rearrange("f c n -> f (c n)"),
                                   bank[4 + (base + q) % 2][0:HID, 0:n * CN]).then_inc(yT_set, 1)
            apply(1, e[:, :, :], ACT.Exp)
            turned_rows(0)
            apply(2, e[:, :, :], ACT.Exp)
            turned_rows(NQ)
            apply(3, gi[:, :, 0:2 * FEAT], ACT.Sigmoid)
            apply(4, nn[:, :, :], ACT.Tanh)
            apply(5, nn[:, :, :], ACT.Exp)
            act.wait_ge(var_set, 1)
            nc.scalar.activation(stat[:, 2, :], stat[:, 1, :], ACT.Sqrt).then_inc(sd_set, 1)

        @block.tensor
        def _(pe):
            pe.wait_ge(w_in, 80)

            def gates(c):
                if c >= 2:
                    pe.wait_ge(gi_out, c - 1)
                for h in range(HEADS):
                    last = nc.tensor.matmul(
                        bank[c % 2][0:CN, h * HW:(h + 1) * HW],
                        gacc[:, c, :].rearrange("f (n h) -> f n h", h=HEADS)[:, :, h], k.wc[:, h, :], start=True, stop=True)
                last.then_inc(gi_done, 1)

            def turn(base, q, x):
                if base + q >= 2:
                    pe.wait_ge(yT_set, base + q - 1)
                for c in range(min(4, NC - 4 * q)):
                    last = nc.tensor.transpose(bank[4 + (base + q) % 2][0:HID, c * CN:(c + 1) * CN],
                                               x[:, 4 * q + c, :], k.ident[0:CN, 0:CN])
                last.then_inc(yT_done, 1)

            def layer(base, q, w, n_out, bank_of):
                pe.wait_ge(yT_set, base + q + 1)
                for c in range(min(4, NC - 4 * q)):
                    last = nc.tensor.matmul(bank_of(q, c, n_out), yT[(base + q) % 2][:, c, :], w, start=True, stop=True)
                last.then_inc(lin_done, 1)

            def lin_bank(q, c, n_out):
                if c == 0 and q >= 2:
                    pe.wait_ge(lin_out, q - 1)
                return bank[2 + q % 2][0:CN, c * n_out:(c + 1) * n_out]

            def shift_bank(q, c, n_out):
                return bank[6][0:CN, (4 * q + c) * n_out:(4 * q + c + 1) * n_out]

            for c in (0, 1):
                gates(c)
            pe.wait_ge(v_set, 1)
            for q in range(NQ):
                turn(0, q, v)
                gates(2 * q + 2)
                gates(2 * q + 3)
                layer(0, q, w3[:, :], HID, lin_bank)
            for c in (SECOND - 2, SECOND - 1):
                gates(c)
            pe.wait_ge(v_set, 2)
            for q in range(NQ):
                turn(NQ, q, y3)
                gates(SECOND + q)
                layer(NQ, q, w4[:, :], DIM, shift_bank)

        @block.vector
        def _(dve):
            link, count = links(dve, n_step)
            link(nc.vector.tensor_tensor(v[:, :, :], acc[:, :, :], k.inv_deg[:, :].unsqueeze(2)
                                         .to_broadcast([CN, NC, HID]), ALU.mult))
            dve.wait_ge(w_in, 80)
            link(nc.vector.tensor_tensor(v[:, :, :], v[:, :, :], b2[:, :].unsqueeze(1).to_broadcast([CN, NC, HID]), ALU.add))

            def elu(v, e, i, between=None):
                link(nc.vector.tensor_scalar(e, v, 0.0, None, ALU.min))
                dve.sem_inc(act_in, 1)
                link(nc.vector.tensor_scalar(v, v, 0.0, None, ALU.max))
                if between:
                    between()
                dve.wait_ge(act_out, i)
                link(nc.vector.scalar_tensor_tensor(v, e, -1.0, v, ALU.add, ALU.add))

            def gates_out(c):
                ps = bank[c % 2][0:CN, 0:HEADS * HW].rearrange("n (h g) -> n h g", h=HEADS)
                dve.wait_ge(gi_done, c + 1)
                link(nc.vector.tensor_scalar(rden[:, c % 2, :], ps[:, :, G3:HW].rearrange("n h o -> n (h o)"), 1e-30, None,
                                             ALU.max))
                link(nc.vector.reciprocal(rden[:, c % 2, :], rden[:, c % 2, :]))
                link(nc.vector.tensor_tensor(gih[c % 2][:, :, :], ps[:, :, 0:G3],
                                             rden[:, c % 2, :].unsqueeze(2).to_broadcast([CN, HEADS, G3]), ALU.mult))
                dve.sem_inc(gi_out, 1)
                link(nc.vector.tensor_reduce(gi[:, c, :], gih[c % 2][:, :, :].rearrange("n h g -> n g h"), AX_X, ALU.add))

            def gates_out_2(c):
                gates_out(c)
                gates_out(c + 1)

            elu(v[:, :, :], e[:, :, :], 1, lambda: gates_out_2(0))
            dve.sem_inc(v_set, 1)
            for q in range(NQ):
                gates_out_2(2 * q + 2)
                n = min(4, NC - 4 * q)
                dve.wait_ge(lin_done, q + 1)
                nc.vector.tensor_tensor(y3[:, 4 * q:4 * q + n, :],
                                        bank[2 + q % 2][0:CN, 0:n * HID].rearrange("n (c f) -> n c f", c=n),
                                        b3[:, :].unsqueeze(1).to_broadcast([CN, n, HID]), ALU.add).then_inc(lin_out, 1)
            dve.wait_ge(lin_out, NQ)
            elu(y3[:, :, :], e[:, :, :], 2, lambda: gates_out_2(SECOND - 2))
            dve.sem_inc(v_set, 1)
            for c in range(SECOND, NC):
                gates_out(c)
            rz = gi[:, :, 0:2 * FEAT]
            link(nc.vector.tensor_tensor(rz, rz, k.gh[:, :, 0:2 * FEAT], ALU.add))
            dve.sem_inc(act_in, 1)
            link(nc.vector.tensor_tensor(gi[:, :, 2 * FEAT:G3], gi[:, :, 2 * FEAT:G3],
                                         k.bih[:, 2 * FEAT:G3].unsqueeze(1).to_broadcast([CN, NC, FEAT]), ALU.add))
            dve.wait_ge(act_out, 3)
            link(nc.vector.tensor_tensor(nn[:, :, :], gi[:, :, 0:FEAT], k.gh[:, :, 2 * FEAT:G3], ALU.mult))
            link(nc.vector.tensor_tensor(nn[:, :, :], nn[:, :, :], gi[:, :, 2 * FEAT:G3], ALU.add))
            dve.sem_inc(act_in, 1)
            dve.wait_ge(act_out, 4)
            link(nc.vector.tensor_tensor(xm[:, :, :], k.tab_a[:, :, 0:FEAT], nn[:, :, :], ALU.subtract))
            link(nc.vector.tensor_tensor(xm[:, :, :], xm[:, :, :], gi[:, :, FEAT:2 * FEAT], ALU.mult))
            link(nc.vector.tensor_tensor(xm[:, :, :], xm[:, :, :], nn[:, :, :], ALU.add))
            elu(xm[:, :, :], nn[:, :, :], 5)
            link(nc.vector.tensor_tensor(k.x1[:, :, :], k.x[:, :, :], xm[:, :, :], ALU.add))
            layer_norm(nc, dve, link, k.x1[:, :, :], xm, sq, stat, node3[:, :, 0:FEAT], var_set, sd_set, 1)
            dve.wait_ge(lin_done, 2 * NQ)
            link(nc.vector.tensor_tensor(node3[:, :, FEAT:FEAT + DIM],
                                         bank[6][0:CN, 0:NC * DIM].rearrange("n (c d) -> n c d", d=DIM),
                                         b4[:, :].unsqueeze(1).to_broadcast([CN, NC, DIM]), ALU.add))
            link(nc.vector.tensor_copy(k.shift[:, :, :], node3[:, :, FEAT:FEAT + DIM]))
            dve.sem_inc(node3_set, 1)


def build_last(nc, a, k, slots_dram, node3_dram, out_dram):
    with ExitStack() as ctx:
        def sb(name, shape, dt=F32):
            return ctx.enter_context(nc.sbuf_tensor(name, shape, dt))

        def sem(name):
            return ctx.enter_context(nc.semaphore(name))

        t = conv_tiles(nc, ctx, FEAT, "last_")
        rows = [sb(f"last_rows{g}", [P, GB, NROW]) for g in range(NGR)]
        wt = sb("last_w", [K, FEAT, FEAT])
        bias = sb("last_bias", [CN, FEAT])
        ohn = sb("last_ohn", [P, BPC, NB])
        ohT = sb("last_ohT", [CN, P])
        bds = sb("last_bds", [CN, BPC, DIM])
        moved = sb("moved", [P, BPC, DIM])
        pos = sb("last_pos", [P, BPC, DIM])
        acc = sb("acc3", [CN, NC, FEAT])
        bank = [ctx.enter_context(nc.psum_tensor(f"last_bank{i}", [P, 512], F32)) for i in range(8)]

        w_in = sem("last_w_in")
        slot_in = sem("last_slot_in")
        slot_used = sem("last_slot_used")
        index_set = sem("last_index_set")
        rows_in = [sem(f"last_rows_in{g}") for g in range(NGR)]
        oh_set = sem("last_oh_set")
        ohT_done = sem("last_ohT_done")
        ohT_set = sem("last_ohT_set")
        bds_set = sem("last_bds_set")
        shift_done = sem("last_shift_done")
        mixed_set = sem("last_mixed_set")
        sum_done = sem("last_sum_done")
        sum_set = sem("last_sum_set")
        out_done = sem("last_out_done")
        acc_set = sem("last_acc_set")
        last_step = sem("last_step")
        end_step = sem("last_end_step")
        result_set = sem("result_set")
        result_out = sem("result_out")

        block = ctx.enter_context(nc.Block())

        @block.sync
        def _(sp):
            def load_slots(s):
                sp.dma_start(t.slot[:, :, :].rearrange("p b w -> p (b w)"),
                             slots_dram[bass.ds(s * SROWS, SROWS), :].rearrange("(p b) w -> p (b w)", b=BPC))\
                  .then_inc(slot_in, 16)

            sections = sp.value_load(k.sect_count[0:1, 0:1], min_val=NC, max_val=MAXSEC - 1)
            load_slots(0)
            sp.dma_start(wt[:, :, :], a["L1_gnn_conv_w"]).then_inc(w_in, 16)
            sp.dma_start(bias[:, :], a["L1_gnn_conv_b"].rearrange("(o f) -> o f", o=1).to_broadcast([CN, FEAT]))\
              .then_inc(w_in, 16)
            with sp.Fori(1, sections + 1) as s:
                sp.wait_ge(slot_used, s)
                sp.nop(nofuse=True)
                sp.wait_ge(index_set, s * NGR)
                sp.nop(nofuse=True)
                load_slots(s)
            sp.wait_ge(slot_in, sections * 16 + 16)
            sp.nop(nofuse=True)
            sp.wait_ge(result_set, 1)
            sp.dma_start(out_dram[0:(NC - 1) * CN, :].rearrange("(c p) f -> p c f", p=CN), acc[:, 0:NC - 1, :])\
              .then_inc(result_out, 16)
            sp.dma_start(out_dram[(NC - 1) * CN:N, :], acc[0:LAST, NC - 1, :]).then_inc(result_out, 16)
            sp.wait_ge(result_out, 32)

        @block.gpsimd
        def _(pool):
            sections = pool.value_load(k.sect_count[0:1, 0:1], min_val=NC, max_val=MAXSEC - 1)

            def fetch(s, first):
                for g in range(NGR):
                    pool.wait_ge(index_set, s * NGR + (g + 1))
                    if not first:
                        pool.wait_ge(mixed_set, s * NGR - (NGR - 1 - g))
                    pool.nop(nofuse=True)
                    for b in range(GB):
                        nc.gpsimd.indirect_dma_start(
                            rows[g][:, b, :], None, node3_dram[:, :],
                            bass.IndirectOffsetOnAxis(ap=t.index[g][:, b:b + 1], axis=0)).then_inc(rows_in[g], 16)
            fetch(0, True)
            with pool.Fori(1, sections) as s:
                fetch(s, False)

        @block.scalar
        def _(act):
            def indices(g):
                nc.scalar.copy(t.index[g][:, :], t.slot[:, g * GB:(g + 1) * GB, 1:2].bitcast(U32)
                               .rearrange("p b o -> p (b o)")).then_inc(index_set, 1)

            act.wait_ge(slot_in, 16)
            for g in range(NGR):
                indices(g)
            sections = act.value_load(k.sect_count[0:1, 0:1], min_val=NC, max_val=MAXSEC - 1)

            def one_hots_out(s):
                act.wait_ge(ohT_done, s + 1)
                nc.scalar.copy(ohT[:, :], bank[4][0:CN, 0:P]).then_inc(ohT_set, 1)

            def section(s, first):
                for g in range(NGR):
                    act.wait_ge(slot_in, s * 16 + 32)
                    act.wait_ge(rows_in[g], s * (GB * 16) + GB * 16)
                    indices(g)
                    for b in range(g * GB, (g + 1) * GB):
                        act.wait_ge(sum_done, s * BPC + (b + 1))
                        if b == 0 and not first:
                            act.wait_ge(out_done, s)
                        nc.scalar.copy(t.sums[:, b * NB:(b + 1) * NB, :].rearrange("k n f -> k (n f)"),
                                       bank[b % 3][0:K, 0:NB * FEAT]).then_inc(sum_set, 1)
                    if g == 0:
                        one_hots_out(s + 1)

            one_hots_out(0)
            section(0, True)
            with act.Fori(1, sections) as s:
                section(s, False)

        @block.tensor
        def _(pe):
            sections = pe.value_load(k.sect_count[0:1, 0:1], min_val=NC, max_val=MAXSEC - 1)
            pe.wait_ge(w_in, 32)

            def turn(s):
                pe.wait_ge(oh_set, s + 1)
                nc.tensor.transpose(bank[4][0:CN, 0:P], ohn[:, :, :].rearrange("p b j -> p (b j)"), k.ident[:, :])\
                    .then_inc(ohT_done, 1)

            def shift(s):
                pe.wait_ge(ohT_set, s + 1)
                pe.wait_ge(bds_set, s + 1)
                nc.tensor.matmul(bank[5][:, 0:BPC * DIM], ohT[:, :], bds[:, :, :].rearrange("n b w -> n (b w)"),
                                 start=True, stop=True).then_inc(shift_done, 1)

            def section(s, first):
                for g in range(NGR):
                    pe.wait_ge(mixed_set, s * NGR + (g + 1))
                    for b in range(g * GB, (g + 1) * GB):
                        if b >= 3 or not first:
                            pe.wait_ge(sum_set, s * BPC + (b - 2))
                        nc.tensor.matmul(bank[b % 3][0:K, 0:NB * FEAT], t.bas[g][:, b - g * GB, :],
                                         t.mixed[g][:, b - g * GB, :, :].rearrange("p j f -> p (j f)"),
                                         start=True, stop=True).then_inc(sum_done, 1)
                    if g == 0:
                        turn(s + 1)
                    if g == 1:
                        shift(s + 1)
                pe.wait_ge(sum_set, s * BPC + BPC)
                if not first:
                    pe.wait_ge(acc_set, s)
                for i in range(FEAT):
                    last = nc.tensor.matmul(bank[3][0:CN, 0:FEAT], t.sums[:, :, i], wt[:, i, :],
                                            start=(i == 0), stop=(i == FEAT - 1))
                last.then_inc(out_done, 1)

            turn(0)
            shift(0)
            section(0, True)
            with pe.Fori(1, sections) as s:
                section(s, False)

        @block.vector
        def _(dve):
            sections = dve.value_load(k.sect_count[0:1, 0:1], min_val=NC, max_val=MAXSEC - 1)
            link, count = links(dve, end_step)
            link(nc.vector.memset(acc[:, :, :], 0.0))

            def add_out(s_last):
                c = dve.value_load(k.sect[0:1, 0, bass.ds(s_last, 1)], min_val=0, max_val=NC - 1)
                sl = acc[:, bass.ds(c, 1), :].rearrange("n c f -> n (c f)")
                return nc.vector.tensor_tensor(sl, sl, bank[3][0:CN, 0:FEAT], ALU.add)

            def one_hot(tile):
                return nc.vector.tensor_tensor(tile[:, :, :], k.iota_j[:, :].unsqueeze(1).to_broadcast([P, BPC, NB]),
                                               t.slot[:, :, 0:1].to_broadcast([P, BPC, NB]), ALU.is_equal)

            def sources(s, link):
                dve.wait_ge(slot_in, s * 16 + 16)
                link(one_hot(ohn))
                dve.sem_inc(oh_set, 1)
                c = dve.value_load(k.sect[0:1, 0, bass.ds(s, 1)], min_val=0, max_val=NC - 1)
                link(nc.vector.tensor_tensor(
                    bds[:, :, :], k.shift[:, bass.ds(c, 1), :].to_broadcast([CN, BPC, DIM]),
                    k.bmask[:, :].unsqueeze(2).to_broadcast([CN, BPC, DIM]), ALU.mult))
                dve.sem_inc(bds_set, 1)

            def section(s, first):
                link, count = links(dve, last_step, s * LAST_STEPS)
                dve.wait_ge(slot_in, s * 16 + 16)
                link(one_hot(t.oh))
                dve.wait_ge(shift_done, s + 1)
                link(nc.vector.tensor_tensor(moved[:, :, :], t.slot[:, :, 3:3 + DIM],
                                             bank[5][:, 0:BPC * DIM].rearrange("p (b d) -> p b d", b=BPC),
                                             ALU.subtract))
                dve.sem_inc(slot_used, 1)
                for g in range(NGR):
                    b0, b1 = g * GB, (g + 1) * GB
                    dve.wait_ge(rows_in[g], s * (GB * 16) + GB * 16)
                    link(nc.vector.tensor_tensor(pos[:, b0:b1, :], moved[:, b0:b1, :], rows[g][:, :, FEAT:FEAT + DIM],
                                                 ALU.add))
                    link(nc.vector.tensor_scalar(pos[:, b0:b1, :], pos[:, b0:b1, :], 0.0, 1.0, ALU.max, ALU.min))
                    link(nc.vector.tensor_scalar(pos[:, b0:b1, :], pos[:, b0:b1, :], float(KS - 1), None, ALU.mult))
                    hat_weights(nc, link, k, pos[:, b0:b1, :], t.hat[:, b0:b1, :, :], t.rise[:, b0:b1, :, :],
                                t.fall[:, b0:b1, :, :], GB)
                    if not first:
                        dve.wait_ge(sum_done, s * BPC - (NGR - 1 - g) * GB)
                    link(basis_group(nc, t, g, link))
                    link(nc.vector.tensor_tensor(
                        t.mixed[g][:, :, :, :],
                        t.oh[:, b0:b1, :].unsqueeze(3).to_broadcast([P, GB, NB, FEAT]),
                        rows[g][:, :, 0:FEAT].unsqueeze(2).to_broadcast([P, GB, NB, FEAT]), ALU.mult))
                    dve.sem_inc(mixed_set, 1)
                    if g == 0:
                        sources(s + 1, link)
                    if g == 1:
                        if not first:
                            dve.wait_ge(out_done, s)
                            link(add_out(s - 1))
                            dve.sem_inc(acc_set, 1)
                        else:
                            dve.sem_inc(last_step, 1)
                            count[0] += 1
                return count[0]

            LAST_STEPS = 32
            sources(0, link)
            section(0, True)
            with dve.Fori(1, sections) as s:
                n = section(s, False)
                assert n == LAST_STEPS, n
            dve.wait_ge(out_done, sections)
            link(add_out(sections - 1))
            shape = [CN, NC, FEAT]
            link(nc.vector.tensor_tensor(acc[:, :, :], acc[:, :, :], k.inv_deg[:, :].unsqueeze(2).to_broadcast(shape),
                                         ALU.mult))
            link(nc.vector.tensor_tensor(acc[:, :, :], acc[:, :, :], bias[:, :].unsqueeze(1).to_broadcast(shape), ALU.add))
            link(nc.vector.tensor_tensor(acc[:, :, :], acc[:, :, :], k.x1[:, :, :], ALU.add))
            dve.sem_inc(result_set, 1)



_INS = ["x", "src", "dst", "edge_attr_3", "L0_gnn_W_gat", "L0_gnn_attn_l", "L0_gnn_attn_r", "L0_gnn_W_ih",
        "L0_gnn_W_hh", "L0_gnn_b_ih", "L0_gnn_b_hh", "L1_gnn_stn1_w", "L1_gnn_stn1_b", "L1_gnn_stn2_w",
        "L1_gnn_stn2_b", "L1_gnn_stn3_w", "L1_gnn_stn3_b", "L1_gnn_stn4_w", "L1_gnn_stn4_b", "L1_gnn_conv_w",
        "L1_gnn_conv_b"]


def build(nc, a, out):
    slots_dram = nc.dram_tensor("slots", ((MAXSEC + 1) * SROWS, SREC), F32).ap()
    drows_dram = nc.dram_tensor("drows", ((MAXSEC + 1) * SROWS, DREC), F32).ap()
    h1_dram = nc.dram_tensor("h1rows", (NC * CN, HID), F32).ap()
    node3_dram = nc.dram_tensor("node3", (NC * CN, NROW), F32).ap()
    rows_dram = nc.dram_tensor("key_rows", (4, E), F16).ap()
    with ExitStack() as ctx:
        k = keep_tiles(nc, ctx)
        keep_node_tiles(nc, ctx, k)
        build_sort(nc, a, k, a["src"].rearrange("(p t) -> p t", p=EP), a["dst"].rearrange("(p t) -> p t", p=EP),
                   a["edge_attr_3"].rearrange("(p t) d -> p t d", p=EP), k.sect, k.sect_count, slots_dram,
                   drows_dram, rows_dram, k.ident)
        build_send(nc, a, k, slots_dram, drows_dram, h1_dram)
        k.x1 = ctx.enter_context(nc.sbuf_tensor("x1", [CN, NC, FEAT], F32))
        with nc.sbuf_tensor("acc2", [CN, NC, HID], F32) as acc, \
                nc.sbuf_tensor("gacc", [FEAT + 1, NC, BPC * NB * HEADS], F32) as gacc:
            build_mid(nc, a, k, slots_dram, drows_dram, h1_dram, acc, gacc)
            build_nodes(nc, a, k, acc, gacc, node3_dram)
        build_last(nc, a, k, slots_dram, node3_dram, out)


def kernel(**inputs):
    import numpy as _np
    import concourse.bacc as _bacc
    from concourse import mybir as _mybir
    from concourse.bass_utils import run_bass_kernel_spmd as _run

    nc = _bacc.Bacc("TRN2", target_bir_lowering=False, num_devices=1)
    arrays, args = {}, {}
    for name in _INS:
        a = _np.ascontiguousarray(inputs[name])
        arrays[f"in_{name}_dram"] = a
        args[name] = nc.dram_tensor(f"in_{name}_dram", a.shape, _mybir.dt.from_np(a.dtype),
                                    kind="ExternalInput").ap()
    out = nc.dram_tensor("out_0_dram", (N, FEAT), F32, kind="ExternalOutput").ap()
    build(nc, args, out)
    r = _run(nc, [arrays], core_ids=[0])
    return r.results[0]["out_0_dram"]
```

```python
from contextlib import ExitStack

import concourse.bass as bass
from concourse import mybir

F32 = mybir.dt.float32
F16 = mybir.dt.float16
BF16 = mybir.dt.bfloat16
I32 = mybir.dt.int32
U32 = mybir.dt.uint32
ALU = mybir.AluOpType
ACT = mybir.ActivationFunctionType
AX_X = mybir.AxisListType.X

N, FEAT, HEADS = 3125, 32, 4
E = 50000
KS, DIM = 5, 3
K = KS ** DIM
HID = 64

NB, BPC = 6, 21
CN = NB * BPC
NC = -(-N // CN)
LAST = N - (NC - 1) * CN
P = 128
SROWS = P * BPC
MAXSEC = NC + E // P + 2
FIXED = NC + 2
GB, NGR = 7, 3
HI = 7
LO = NC * BPC // HI
LPC = BPC // HI
EP, ET = 125, 400
GT = 25
GD = 8
NG = ET // GT
assert EP * ET == E and NC * BPC == LO * HI and NG % 2 == 0 and NGR * GB == BPC

SREC = 8
DREC = FEAT + 1 + HEADS + 1
TROW = FEAT + 1 + HEADS
G3 = 3 * FEAT
HW = G3 + 1
NROW = FEAT + DIM + 1
MAGIC = 12582912.0
BIG = 1.0e30


def links(eng, sem, base=0):
    count = [0]

    def link(ins):
        count[0] += 1
        ins.then_inc(sem, 1)
        eng.wait_ge(sem, base + count[0])
    return link, count


def node_prep(nc, ctx, a, k, bank):
    def sb(name, shape, dt=F32):
        return ctx.enter_context(nc.sbuf_tensor(name, shape, dt))

    def sem(name):
        return ctx.enter_context(nc.semaphore(name))

    xm = k.gh[:, :, 0:FEAT]
    sq = k.gh[:, :, FEAT:2 * FEAT]
    stat = sb("stat", [CN, 4, NC])
    wgat = sb("wgat", [FEAT, HEADS, FEAT])
    attn = sb("attn", [FEAT, 2, HEADS, FEAT])
    wat = sb("wat", [FEAT, 2, HEADS, FEAT])
    wa = sb("wa", [FEAT, 2 * HEADS])
    hT = [sb(f"hT{i}", [FEAT, 4, CN]) for i in range(2)]
    wih = sb("wih", [G3, HEADS, FEAT])
    whh = sb("whh", [G3, FEAT])
    bhh = sb("bhh", [CN, G3])
    wgatT = sb("wgatT", [FEAT, HEADS, FEAT])
    wihT = sb("wihT", [FEAT, HEADS, G3])
    whhT = sb("whhT", [FEAT, G3])

    x_in = sem("x_in")
    w_in = sem("w_in")
    gru_in = sem("gru_in")
    x_pad = sem("x_pad")
    wc_clear = sem("wc_clear")
    var_set = sem("var_set")
    sd_set = sem("sd_set")
    ln_step = sem("ln_step")
    h_set = sem("h_set")
    h_turned = sem("h_turned")
    hT_set = sem("hT_set")
    weights_turned = sem("weights_turned")
    turned_out = sem("turned_out")
    wc_done = sem("wc_done")
    wc_set = sem("wc_set")
    gh_done = sem("gh_done")
    gh_set = sem("gh_set")
    NQ = -(-NC // 4)

    def on_sync(sp):
        sp.wait_ge(x_pad, 1)
        sp.dma_start(k.x[:, 0:NC - 1, :], a["x"][0:(NC - 1) * CN, :].rearrange("(c p) f -> p c f", p=CN))\
          .then_inc(x_in, 16)
        sp.dma_start(k.x[0:LAST, NC - 1, :], a["x"][(NC - 1) * CN:N, :]).then_inc(x_in, 16)
        sp.dma_start(wgat[:, :, :], a["L0_gnn_W_gat"].rearrange("i (h o) -> i h o", h=HEADS)).then_inc(w_in, 16)
        for i, name in enumerate(("L0_gnn_attn_l", "L0_gnn_attn_r")):
            sp.dma_start(attn[:, i, :, :].rearrange("p h f -> p (h f)"),
                         a[name].rearrange("(o h) f -> o (h f)", o=1).to_broadcast([FEAT, HEADS * FEAT]))\
              .then_inc(w_in, 16)
        for tile, source in (
                (wih[:, :, :].rearrange("g h o -> g (h o)"), a["L0_gnn_W_ih"]), (whh[:, :], a["L0_gnn_W_hh"]),
                (k.bih[:, :], a["L0_gnn_b_ih"].rearrange("(o f) -> o f", o=1).to_broadcast([CN, G3])),
                (bhh[:, :], a["L0_gnn_b_hh"].rearrange("(o f) -> o f", o=1).to_broadcast([CN, G3]))):
            sp.dma_start(tile, source).then_inc(gru_in, 16)

    def on_gpsimd(pool):
        nc.gpsimd.memset(k.x[:, NC - 1, :], 0.0).then_inc(x_pad, 1)
        nc.gpsimd.memset(k.wc[:, :, :], 0.0).then_inc(wc_clear, 1)
        pool.wait_ge(wc_clear, 1)
        nc.gpsimd.affine_select(out=k.wc[:, :, G3:HW], in_=k.wc[:, :, G3:HW], compare_op=ALU.not_equal, fill=1.0,
                                base=-FEAT, pattern=[[0, HEADS], [0, 1]], channel_multiplier=1).then_inc(wc_clear, 1)

    def on_scalar(act):
        act.wait_ge(var_set, 1)
        nc.scalar.activation(stat[:, 2, :], stat[:, 1, :], ACT.Sqrt).then_inc(sd_set, 1)
        act.wait_ge(weights_turned, 1)
        nc.scalar.copy(wihT[:, :, :].rearrange("o h g -> o (h g)"), bank[6][0:FEAT, 0:HEADS * G3]).then_inc(turned_out, 1)
        nc.scalar.copy(wgatT[:, :, :].rearrange("o h f -> o (h f)"), bank[7][0:FEAT, 0:HEADS * FEAT])\
            .then_inc(turned_out, 1)
        nc.scalar.copy(whhT[:, :], bank[7][0:FEAT, HEADS * FEAT:HEADS * FEAT + G3]).then_inc(turned_out, 1)
        act.wait_ge(wc_done, 1)
        act.wait_ge(wc_clear, 2)
        nc.scalar.copy(k.wc[0:FEAT, :, 0:G3], bank[3][0:FEAT, 0:HEADS * G3].rearrange("f (h g) -> f h g", h=HEADS))\
            .then_inc(wc_set, 1)
        def gates_out(q):
            n = min(4, NC - 4 * q)
            act.wait_ge(gh_done, q + 1)
            nc.scalar.copy(k.gh[:, 4 * q:4 * q + n, :].rearrange("n c g -> n (c g)"), bank[6 + q % 2][0:CN, 0:n * G3])\
                .then_inc(gh_set, 1)

        for q in range(NQ):
            cs = range(4 * q, min(4 * q + 4, NC))
            act.wait_ge(h_turned, q + 1)
            if q >= 2:
                act.wait_ge(gh_done, q - 1)
            nc.scalar.copy(hT[q % 2][:, 0:len(cs), :].rearrange("f c n -> f (c n)"),
                           bank[q % 2][0:FEAT, 0:len(cs) * CN]).then_inc(hT_set, 1)
            if q >= 1:
                gates_out(q - 1)
        gates_out(NQ - 1)

    def on_tensor(pe):
        pe.wait_ge(gru_in, 64)
        pe.wait_ge(w_in, 48)
        for h in range(HEADS):
            nc.tensor.transpose(bank[6][0:FEAT, h * G3:(h + 1) * G3], wih[:, h, :], k.ident[0:G3, 0:G3])
            nc.tensor.transpose(bank[7][0:FEAT, h * FEAT:(h + 1) * FEAT], wgat[:, h, :], k.ident[0:FEAT, 0:FEAT])
        nc.tensor.transpose(bank[7][0:FEAT, HEADS * FEAT:HEADS * FEAT + G3], whh[:, :], k.ident[0:G3, 0:G3])\
            .then_inc(weights_turned, 1)
        pe.wait_ge(turned_out, 3)
        for h in range(HEADS):
            last = nc.tensor.matmul(bank[3][0:FEAT, h * G3:(h + 1) * G3], wgatT[:, h, :], wihT[:, h, :],
                                    start=True, stop=True)
        last.then_inc(wc_done, 1)
        pe.wait_ge(h_set, 1)

        def turn(q):
            for c in range(4 * q, min(4 * q + 4, NC)):
                last = nc.tensor.transpose(bank[q % 2][0:FEAT, (c - 4 * q) * CN:(c - 4 * q + 1) * CN],
                                           k.tab_a[:, c, 0:FEAT], k.ident[0:CN, 0:CN])
            last.then_inc(h_turned, 1)

        turn(0)
        for q in range(NQ):
            if q + 1 < NQ:
                turn(q + 1)
            pe.wait_ge(hT_set, q + 1)
            if q >= 2:
                pe.wait_ge(gh_set, q - 1)
            for c in range(4 * q, min(4 * q + 4, NC)):
                nc.tensor.matmul(bank[2][0:CN, c * 8:(c + 1) * 8], hT[q % 2][:, c - 4 * q, :], wa[:, :],
                                 start=True, stop=True)
                last = nc.tensor.matmul(bank[6 + q % 2][0:CN, (c - 4 * q) * G3:(c - 4 * q + 1) * G3],
                                        hT[q % 2][:, c - 4 * q, :], whhT[:, :], start=True, stop=True)
            last.then_inc(gh_done, 1)

    def on_vector(dve):
        link, _ = links(dve, ln_step)
        link(nc.vector.memset(k.tab_a[:, :, FEAT:FEAT + 1], 1.0))
        dve.wait_ge(w_in, 48)
        for i in range(2):
            link(nc.vector.tensor_tensor(wat[:, i, :, :], wgat[:, :, :], attn[:, i, :, :], ALU.mult))
        link(nc.vector.tensor_reduce(wa[:, :], wat[:, :, :, :].rearrange("p i h f -> p (i h) f"), AX_X, ALU.add))
        dve.wait_ge(x_in, 32)
        layer_norm(nc, dve, link, k.x[:, :, :], xm, sq, stat, k.tab_a[:, :, 0:FEAT], var_set, sd_set, 1)
        dve.sem_inc(h_set, 1)
        dve.wait_ge(gh_done, NQ)
        el = bank[2][0:CN, 0:NC * 8].rearrange("n (c w) -> n c w", w=8)
        link(nc.vector.tensor_copy(k.tab_a[:, :, FEAT + 1:TROW], el[:, :, 0:HEADS]))
        link(nc.vector.tensor_copy(k.er[:, :, :], el[:, :, HEADS:2 * HEADS]))
        dve.wait_ge(gh_set, NQ)
        link(nc.vector.tensor_tensor(k.gh[:, :, :], k.gh[:, :, :],
                                     bhh[:, :].unsqueeze(1).to_broadcast([CN, NC, G3]), ALU.add))
        link(nc.vector.tensor_tensor(k.gh[:, :, 0:2 * FEAT], k.gh[:, :, 0:2 * FEAT],
                                     k.bih[:, 0:2 * FEAT].unsqueeze(1).to_broadcast([CN, NC, 2 * FEAT]), ALU.add))

    return on_sync, on_gpsimd, on_scalar, on_tensor, on_vector


def build_sort(nc, a, k_nodes, src, dst, attr, sect, sect_count, slots_dram, drows_dram, rows_dram, ident):
    with ExitStack() as ctx:
        def sb(name, shape, dt):
            return ctx.enter_context(nc.sbuf_tensor(name, shape, dt))

        def ps(name, shape, dt=F32):
            return ctx.enter_context(nc.psum_tensor(name, shape, dt))

        def sem(name):
            return ctx.enter_context(nc.semaphore(name))

        key_i = [sb("src_i", [EP, ET], I32), sb("dst_i", [EP, ET], I32)]
        attr_sb = sb("attr_sb", [EP, ET, DIM], F32)
        r42 = [sb(f"r42{k}", [EP, ET], F32) for k in range(2)]
        cm = sb("cm", [EP, ET], F32)
        lo = [sb(f"lo{k}", [EP, ET], F32) for k in range(2)]
        hi = [sb(f"hi{k}", [EP, ET], F32) for k in range(2)]
        jn = [sb(f"jn{k}", [EP, ET], F32) for k in range(2)]
        bc = [sb(f"bc{k}", [EP, ET], F32) for k in range(2)]
        blk = [sb(f"blk{k}", [EP, ET], F32) for k in range(2)]
        rowT = sb("rowT", [ET // 4, 4, 4 * EP], F16)
        iota_f = sb("iota_f", [P, LO], F32)
        iota_s = sb("iota_s", [NC, MAXSEC], F32)
        part = sb("part", [P, 1], F32)
        ltri = sb("ltri", [EP, EP], F32)
        ones = sb("ones", [P, 1], F32)
        empty_s = sb("empty_s", [P, BPC, SREC], F32)
        empty_d = sb("empty_d", [P, BPC, DREC], F32)
        oh_lo = [[sb(f"oh_lo{k}{h}", [EP, GT, LO], BF16) for h in range(2)] for k in range(2)]
        oh_hi = [[sb(f"oh_hi{k}{h}", [EP, GT, HI], BF16) for h in range(2)] for k in range(2)]
        hist = [sb(f"hist{k}", [LO, HI, ET], F32) for k in range(2)]
        pref = [sb(f"pref{k}", [LO, HI, ET], F32) for k in range(2)]
        zeros = sb("zeros", [LO, ET], F32)
        cmax = sb("cmax", [LO, 2], F32)
        crow = sb("crow", [1, 2, LO], F32)
        sq = sb("sq", [1, 2, NC], F32)
        scum = sb("scum", [1, 2, NC], F32)
        sbase = sb("sbase", [1, 2, NC], F32)
        sbase3 = sb("sbase3", [1, 2, LO], F32)
        zero_row = sb("zero_row", [1, NC], F32)
        basecol = sb("basecol", [LO, 2], F32)
        cumcol = sb("cumcol", [NC, 2], F32)
        past = [sb(f"past{k}", [NC, MAXSEC], F32) for k in range(2)]
        scount = sb("scount", [1, 4], F32)
        pg = [sb(f"pg{k}", [LO, GT, HI], F32) for k in range(2)]
        pg_hi = [sb(f"pg_hi{k}", [LO, GT, HI], BF16) for k in range(2)]
        pg_lo = [sb(f"pg_lo{k}", [LO, GT, HI], BF16) for k in range(2)]
        blkrow = [[sb(f"blkrow{k}{h}", [EP, GT * EP], F16) for h in range(2)] for k in range(2)]
        lorow = [[sb(f"lorow{k}{h}", [LO, GT * EP], F16) for h in range(2)] for k in range(2)]
        oh_loT = [sb(f"oh_loT{k}", [LO, GT * EP], BF16) for k in range(2)]
        blk_g = [sb(f"blk_g{k}", [EP, GT], F32) for k in range(2)]
        unused = [flat[:, i * EP:(i + 1) * EP]
                  for flat in (oh_lo[0][h][:, :, :].rearrange("e t l -> e (t l)") for h in range(2))
                  for i in range(GT * LO // EP)]
        in_tile = [sb(f"in_tile{k}", [EP, GT], F32) for k in range(2)]
        hsel = [sb(f"hsel{k}", [EP, GT, HI], F32) for k in range(2)]
        before = [sb(f"before{k}", [EP, GT], F32) for k in range(2)]
        row21 = [sb(f"row21{k}", [EP, GT], F32) for k in range(2)]
        rec = [sb(f"rec{h}", [EP, GT, SREC], F32) for h in range(2)]
        srow = [sb(f"srow{h}", [EP, GT], U32) for h in range(2)]

        bank = [ps(f"sort_bank{i}", [P, 512]) for i in range(8)]
        prep_sync, prep_gpsimd, prep_scalar, prep_tensor, prep_vector = node_prep(nc, ctx, a, k_nodes, bank)

        edges_in = [sem("edges_in0"), sem("edges_in1"), sem("edges_in2")]
        consts_set = sem("consts_set")
        ident_step = sem("ident_step")
        empties_set = sem("empties_set")
        tables_empty = sem("tables_empty")
        more_empty = sem("more_empty")
        keys_split = sem("keys_split")
        keys_turned = sem("keys_turned")
        rowT_set = sem("rowT_set")
        rowT_out = [sem(f"rowT_out{a}") for a in range(4)]
        lohi_set = sem("lohi_set")
        hist_used = sem("hist_used")
        hist_done = sem("hist_done")
        apart_set = sem("apart_set")
        apart_step = sem("apart_step")
        lo1_set = sem("lo1_set")
        zeros_set = sem("zeros_set")
        cmax_set = sem("cmax_set")
        cmax_turned = sem("cmax_turned")
        sec_set = sem("sec_set")
        sec_turned = sem("sec_turned")
        past_set = sem("past_set")
        past_summed = sem("past_summed")
        sect_set = sem("sect_set")
        rows_in = [sem(f"rows_in{h}") for h in range(2)]
        rows_used = sem("rows_used")
        loT_set = sem("loT_set")
        before_done = sem("before_done")
        rec_set = sem("rec_set")
        rec_out = [sem(f"rec_out{h}") for h in range(2)]
        split_step = sem("split_step")
        sec_step = sem("sec_step")
        rank_step = sem("rank_step")

        block = ctx.enter_context(nc.Block())

        def bcast_rows(a, g, parts):
            return rows_dram[a:a + 1, bass.ds(g * (GT * EP), GT * EP)].to_broadcast([parts, GT * EP])

        @block.sync
        def _(sp):
            sp.dma_start(key_i[0][:, :], src).then_inc(edges_in[0], 16)
            sp.dma_start(key_i[1][:, :], dst).then_inc(edges_in[1], 16)
            sp.dma_start(attr_sb[:, :, :], attr).then_inc(edges_in[2], 16)
            prep_sync(sp)
            for a in range(4):
                sp.wait_ge(rowT_set, a + 1)
                sp.dma_start(rows_dram[a, :].rearrange("(q r x) -> r q x", q=4, x=EP),
                             rowT[:, a, :].rearrange("r (q x) -> r q x", q=4)).then_inc(rowT_out[a], 16)
            for a in range(4):
                sp.wait_ge(rowT_out[a], 16)
            sp.sem_inc(rows_used, 2)
            with sp.Fori(0, NG // 2) as i:
                for h in range(2):
                    sp.wait_ge(rows_used, i * 2 + (h + 1))
                    for k in range(2):
                        sp.dma_start(blkrow[k][h][:, :], bcast_rows(k, i * 2 + h, EP)).then_inc(rows_in[h], 16)
                        sp.dma_start(lorow[k][h][:, :], bcast_rows(2 + k, i * 2 + h, LO)).then_inc(rows_in[h], 16)

        @block.scalar
        def _(act):
            act.wait_ge(empties_set, 5)
            act.dma_start(slots_dram[0:FIXED * SROWS, :].rearrange("(s p b) w -> p s (b w)", p=P, b=BPC),
                          empty_s[:, :, :].rearrange("p b w -> p (b w)").unsqueeze(1)
                          .to_broadcast([P, FIXED, BPC * SREC])).then_inc(tables_empty, 16)
            act.dma_start(drows_dram[0:FIXED * SROWS, :].rearrange("(s p b) w -> p s (b w)", p=P, b=BPC),
                          empty_d[:, :, :].rearrange("p b w -> p (b w)").unsqueeze(1)
                          .to_broadcast([P, FIXED, BPC * DREC])).then_inc(tables_empty, 16)
            for a in range(4):
                act.wait_ge(keys_turned, a + 1)
                nc.scalar.copy(rowT[:, a, :], bank[a][0:ET // 4, 0:4 * EP]).then_inc(rowT_set, 1)

            def one_hots(g, h):
                act.wait_ge(apart_set, g + 1)
                rest = oh_lo[1][h][:, GD:GT, :]
                nc.scalar.activation(rest, rest, ACT.Square).then_inc(apart_step, 1)
                act.wait_ge(apart_step, g + 1)
                nc.scalar.activation(rest, rest, ACT.Relu, bias=1.0, scale=-1.0)\
                    .then_inc(lo1_set, 1)

            def counts_out(g, h):
                act.wait_ge(hist_done, g + 1)
                for k in range(2):
                    last = nc.scalar.copy(
                        hist[k][:, :, bass.ds(g * GT, GT)],
                        bank[4 + 2 * k + h][0:LO, 0:GT * HI].rearrange("l (t h) -> l h t", h=HI))
                last.then_inc(hist_used, 1)

            one_hots(0, 0)
            one_hots(1, 1)
            counts_out(0, 0)
            with act.Fori(1, NG // 2) as i:
                one_hots(i * 2, 0)
                counts_out(i * 2 - 1, 1)
                one_hots(i * 2 + 1, 1)
                counts_out(i * 2, 0)
            counts_out(NG - 1, 1)
            act.wait_ge(sect_set, 1)
            upto = act.value_load(sect_count[0:1, 1:2], min_val=FIXED + 1, max_val=MAXSEC)
            with act.Fori(FIXED, upto) as s:
                act.dma_start(slots_dram[bass.ds(s * SROWS, SROWS), :].rearrange("(p b) w -> p (b w)", b=BPC),
                              empty_s[:, :, :].rearrange("p b w -> p (b w)")).then_inc(more_empty, 16)
                act.dma_start(drows_dram[bass.ds(s * SROWS, SROWS), :].rearrange("(p b) w -> p (b w)", b=BPC),
                              empty_d[:, :, :].rearrange("p b w -> p (b w)")).then_inc(more_empty, 16)
                act.wait_ge(more_empty, (s - (FIXED - 1)) * 32)
            act.sem_inc(sect_set, 1)
            prep_scalar(act)

        @block.gpsimd
        def _(pool):
            nc.gpsimd.memset(ident[:, :], 0.0).then_inc(ident_step, 1)
            nc.gpsimd.memset(ltri[:, :], 1.0).then_inc(ident_step, 1)
            pool.wait_ge(ident_step, 2)
            nc.gpsimd.affine_select(out=ident[:, :], in_=ident[:, :], compare_op=ALU.not_equal, fill=1.0, base=0,
                                    pattern=[[-1, P]], channel_multiplier=1).then_inc(ident_step, 1)
            nc.gpsimd.affine_select(out=ltri[:, :], in_=ltri[:, :], compare_op=ALU.is_gt, fill=0.0, base=0,
                                    pattern=[[-1, EP]], channel_multiplier=1).then_inc(ident_step, 1)
            nc.gpsimd.iota(iota_f[:, :], pattern=[[1, LO]], base=0, channel_multiplier=0,
                           allow_small_or_imprecise_dtypes=True).then_inc(consts_set, 1)
            nc.gpsimd.iota(iota_s[:, :], pattern=[[1, MAXSEC]], base=0, channel_multiplier=0,
                           allow_small_or_imprecise_dtypes=True).then_inc(consts_set, 1)
            nc.gpsimd.iota(part[:, :], pattern=[[0, 1]], base=0, channel_multiplier=1,
                           allow_small_or_imprecise_dtypes=True).then_inc(consts_set, 1)
            nc.gpsimd.memset(ones[:, :], 1.0).then_inc(consts_set, 1)
            nc.gpsimd.memset(empty_s[:, :, :], 0.0).then_inc(empties_set, 1)
            nc.gpsimd.memset(empty_d[:, :, :], 0.0).then_inc(empties_set, 1)
            pool.wait_ge(empties_set, 2)
            nc.gpsimd.memset(empty_s[:, :, 0:1], -1.0).then_inc(empties_set, 1)
            nc.gpsimd.memset(empty_d[:, :, DREC - 1:DREC], -1.0).then_inc(empties_set, 1)
            pool.wait_ge(empties_set, 4)
            nc.gpsimd.memset(empty_s[:, :, 2:3].bitcast(I32), 1 << 28).then_inc(empties_set, 1)
            nc.gpsimd.memset(zero_row[:, :], 0.0).then_inc(zeros_set, 1)
            nc.gpsimd.memset(zeros[:, :], 0.0).then_inc(zeros_set, 1)
            pool.wait_ge(keys_split, 2)

            def distances(g, h):
                nc.gpsimd.tensor_tensor(
                    oh_lo[1][h][:, GD:GT, :], iota_f[0:EP, 0:LO].unsqueeze(1).to_broadcast([EP, GT - GD, LO]),
                    lo[1][:, bass.ds(g * GT + GD, GT - GD)].unsqueeze(2).to_broadcast([EP, GT - GD, LO]),
                    ALU.subtract).then_inc(apart_set, 1)
            for h in range(2):
                distances(h, h)
            with pool.Fori(1, NG // 2) as i:
                for h in range(2):
                    pool.wait_ge(hist_done, i * 2 + (h - 1))
                    distances(i * 2 + h, h)
            prep_gpsimd(pool)
            pool.wait_ge(tables_empty, 32)
            pool.wait_ge(sect_set, 2)
            with pool.Fori(0, NG // 2) as i:
                for h in range(2):
                    pool.wait_ge(rec_set, i * 2 + (h + 1))
                    pool.nop(nofuse=True)
                    for t in range(GT):
                        nc.gpsimd.indirect_dma_start(
                            slots_dram[:, :], bass.IndirectOffsetOnAxis(ap=srow[h][:, t:t + 1], axis=0),
                            rec[h][:, t, :], None).then_inc(rec_out[h], 16)
            for h in range(2):
                pool.wait_ge(rec_out[h], NG // 2 * GT * 16)

        @block.tensor
        def _(pe):
            pe.wait_ge(ident_step, 4)
            for a in range(4):
                pe.wait_ge(keys_split, a % 2 + 1)
                arr = (blk[0], blk[1], lo[0], lo[1])[a]
                for q in range(4):
                    last = nc.tensor.transpose(bank[a][0:ET // 4, q * EP:(q + 1) * EP],
                                               arr[:, q * (ET // 4):(q + 1) * (ET // 4)], ident[0:EP, 0:EP])
                last.then_inc(keys_turned, 1)
            with pe.Fori(0, NG // 2) as i:
                for h in range(2):
                    pe.wait_ge(lohi_set, i * 2 + (h + 1))
                    pe.wait_ge(hist_used, i * 2 + (h + 1))
                    for k in range(2):
                        for t in range(GT):
                            if k == 1 and t == GD:
                                pe.wait_ge(lo1_set, i * 2 + (h + 1))
                            last = nc.tensor.matmul(bank[4 + 2 * k + h][0:LO, t * HI:(t + 1) * HI],
                                                    oh_lo[k][h][:, t, :], oh_hi[k][h][:, t, :], start=True, stop=True)
                    last.then_inc(hist_done, 1)
            pe.wait_ge(cmax_set, 1)
            pe.wait_ge(rowT_set, 4)
            for k in range(2):
                last = nc.tensor.transpose(bank[0][0:1, k * P:k * P + LO], cmax[:, k:k + 1], ident[0:LO, 0:LO])
            last.then_inc(cmax_turned, 1)
            pe.wait_ge(sec_set, 1)
            for k in range(2):
                nc.tensor.matmul(bank[1][0:LO, k:k + 1], sbase3[0:1, k, :], ones[0:1, 0:1], start=True, stop=True)
                last = nc.tensor.matmul(bank[1][0:NC, 4 + k:5 + k], scum[0:1, k, :], ones[0:1, 0:1],
                                        start=True, stop=True)
            last.then_inc(sec_turned, 1)
            pe.wait_ge(past_set, 1)
            for k in range(2):
                last = nc.tensor.matmul(bank[2 + k][0:1, 0:MAXSEC], ones[0:NC, 0:1], past[k][:, :],
                                        start=True, stop=True)
            last.then_inc(past_summed, 1)
            with pe.Fori(0, NG) as g:
                pe.wait_ge(loT_set, g + 1)
                for k in range(2):
                    for t in range(GT):
                        nc.tensor.matmul(bank[4 + k][0:EP, t * HI:(t + 1) * HI],
                                         oh_loT[k][:, t * EP:(t + 1) * EP], pg_hi[k][:, t, :],
                                         start=True, stop=False)
                        last = nc.tensor.matmul(bank[4 + k][0:EP, t * HI:(t + 1) * HI],
                                                oh_loT[k][:, t * EP:(t + 1) * EP], pg_lo[k][:, t, :],
                                                start=False, stop=True)
                last.then_inc(before_done, 1)
            prep_tensor(pe)

        @block.vector
        def _(dve):
            link, _ = links(dve, split_step)
            dve.wait_ge(consts_set, 4)

            def floor_div(out, x, d, link=link):
                link(nc.vector.tensor_scalar(out, x, 1.0 / d, 0.5 / d - 0.5, ALU.mult, ALU.add))
                link(nc.vector.tensor_scalar(out, out, MAGIC, -MAGIC, ALU.add, ALU.add))

            for k in range(2):
                dve.wait_ge(edges_in[k], 16)
                floor_div(lo[k][:, :], key_i[k][:, :], NB * HI)
                link(nc.vector.scalar_tensor_tensor(r42[k][:, :], lo[k][:, :], -float(NB * HI), key_i[k][:, :],
                                                    ALU.mult, ALU.add))
                floor_div(hi[k][:, :], r42[k][:, :], NB)
                link(nc.vector.scalar_tensor_tensor(blk[k][:, :], lo[k][:, :], float(HI), hi[k][:, :],
                                                    ALU.mult, ALU.add))
                dve.sem_inc(keys_split, 1)
            dve.sem_inc(hist_used, 2)

            def one_hots(g, h):
                for k, n in enumerate((GT, GD)):
                    nc.vector.tensor_tensor(
                        oh_lo[k][h][:, 0:n, :], iota_f[0:EP, 0:LO].unsqueeze(1).to_broadcast([EP, n, LO]),
                        lo[k][:, bass.ds(g * GT, n)].unsqueeze(2).to_broadcast([EP, n, LO]), ALU.is_equal)
                    last = nc.vector.tensor_tensor(
                        oh_hi[k][h][:, :, :], iota_f[0:EP, 0:HI].unsqueeze(1).to_broadcast([EP, GT, HI]),
                        hi[k][:, bass.ds(g * GT, GT)].unsqueeze(2).to_broadcast([EP, GT, HI]), ALU.is_equal)
                last.then_inc(lohi_set, 1)

            for h in range(2):
                one_hots(h, h)
            with dve.Fori(1, NG // 2) as i:
                for h in range(2):
                    dve.wait_ge(hist_done, i * 2 + (h - 1))
                    one_hots(i * 2 + h, h)
            link, count = links(dve, sec_step)
            for k in range(2):
                floor_div(cm[:, :], lo[k][:, :], LPC, link)
                link(nc.vector.scalar_tensor_tensor(bc[k][:, :], cm[:, :], -float(BPC), blk[k][:, :],
                                                    ALU.mult, ALU.add))
                link(nc.vector.scalar_tensor_tensor(jn[k][:, :], hi[k][:, :], -float(NB), r42[k][:, :],
                                                    ALU.mult, ALU.add))
            dve.wait_ge(zeros_set, 2)
            dve.wait_ge(hist_used, NG + 2)
            for k in range(2):
                for h in range(HI):
                    last = nc.vector.tensor_tensor_scan(pref[k][:, h, :], hist[k][:, h, :], zeros[:, :], 0.0,
                                                        ALU.add, ALU.add)
                link(last)
                link(nc.vector.tensor_reduce(cmax[:, k:k + 1], pref[k][:, :, ET - 1:ET].rearrange("l h o -> l (h o)"),
                                             AX_X, ALU.max))
            dve.sem_inc(cmax_set, 1)
            dve.wait_ge(cmax_turned, 1)
            link(nc.vector.tensor_copy(crow[:, :, :], bank[0][0:1, 0:2 * P].rearrange("o (k l) -> o k l", k=2)[:, :, 0:LO]))
            for k in range(2):
                link(nc.vector.tensor_reduce(sq[:, k, :], crow[:, k, :].rearrange("o (c l) -> o c l", l=LPC),
                                             AX_X, ALU.max))
            sqf = sq[:, :, :].rearrange("o k c -> o (k c)")
            link(nc.vector.tensor_scalar(sqf, sqf, float(P - 1), None, ALU.add))
            floor_div(sqf, sqf, P, link)
            link(nc.vector.tensor_scalar(sqf, sqf, 1.0, None, ALU.max))
            for k in range(2):
                link(nc.vector.tensor_tensor_scan(scum[:, k, :], sq[:, k, :], zero_row[:, :], 0.0, ALU.add, ALU.add))
                link(nc.vector.tensor_tensor(sbase[:, k, :], scum[:, k, :], sq[:, k, :], ALU.subtract))
                link(nc.vector.tensor_scalar(
                    sbase3[:, k, :].rearrange("o (c l) -> o c l", l=LPC),
                    sbase[:, k, :].unsqueeze(2).to_broadcast([1, NC, LPC]), float(P), None, ALU.mult))
            dve.sem_inc(sec_set, 1)
            link(nc.vector.tensor_tensor(scount[:, 0:1], scum[:, 0, NC - 1:NC], scum[:, 1, NC - 1:NC], ALU.max))
            link(nc.vector.tensor_scalar(scount[:, 1:2], scount[:, 0:1], 2.0, float(FIXED + 1), ALU.add, ALU.max))
            link(nc.vector.tensor_scalar(scount[:, 2:3], scount[:, 0:1], 0.5, 0.25, ALU.mult, ALU.add))
            link(nc.vector.tensor_scalar(scount[:, 2:3], scount[:, 2:3], MAGIC, -MAGIC, ALU.add, ALU.add))
            link(nc.vector.tensor_tensor(scount[:, 3:4], scount[:, 0:1], scount[:, 2:3], ALU.subtract))
            link(nc.vector.tensor_copy(sect_count[:, :], scount[:, :]))
            dve.wait_ge(sec_turned, 1)
            link(nc.vector.tensor_copy(basecol[:, :], bank[1][0:LO, 0:2]))
            link(nc.vector.tensor_copy(cumcol[:, :], bank[1][0:NC, 4:6]))
            for k in range(2):
                link(nc.vector.tensor_scalar(past[k][:, :], iota_s[:, :], cumcol[:, k:k + 1], None, ALU.is_ge))
            dve.sem_inc(past_set, 1)

            def section_chunks():
                dve.wait_ge(past_summed, 1)
                for k in range(2):
                    link(nc.vector.tensor_scalar(sect[:, k, :], bank[2 + k][0:1, 0:MAXSEC], float(NC - 1), None,
                                                 ALU.min))
                dve.sem_inc(sect_set, 1)

            dve.wait_ge(edges_in[2], 16)

            def rank_group(g, i, h, first=False, between=None):
                link, count = links(dve, rank_step, g * RANK_STEPS)
                dve.wait_ge(rows_in[h], i * 64 + 64)
                for k in range(2):
                    nc.vector.tensor_scalar(oh_loT[k][:, :], lorow[k][h][:, :], part[0:LO, :], None, ALU.is_equal)
                    link(nc.vector.scalar_tensor_tensor(
                        pg[k][:, :, :].rearrange("l t h -> l h t"), pref[k][:, :, bass.ds(g * GT, GT)],
                        basecol[:, k:k + 1], hist[k][:, :, bass.ds(g * GT, GT)], ALU.add, ALU.subtract))
                    link(nc.vector.tensor_scalar(pg_hi[k][:, :, :], pg[k][:, :, :], 256 * MAGIC, -256 * MAGIC,
                                                 ALU.add, ALU.add))
                    link(nc.vector.tensor_tensor(pg_lo[k][:, :, :], pg[k][:, :, :], pg_hi[k][:, :, :], ALU.subtract))
                dve.sem_inc(loT_set, 1)
                if between:
                    between()
                for k in range(2):
                    link(nc.vector.tensor_scalar(blk_g[k][:, :], blk[k][:, bass.ds(g * GT, GT)], 1.0, None, ALU.mult))
                    nc.vector.tensor_tensor(
                        hsel[k][:, :, :], iota_f[0:EP, 0:HI].unsqueeze(1).to_broadcast([EP, GT, HI]),
                        hi[k][:, bass.ds(g * GT, GT)].unsqueeze(2).to_broadcast([EP, GT, HI]), ALU.is_equal)
                    for t in range(GT):
                        last = nc.vector.scalar_tensor_tensor(
                            unused[t], blkrow[k][h][:, t * EP:(t + 1) * EP], blk_g[k][:, t:t + 1], ltri[:, :],
                            ALU.is_equal, ALU.mult, accum_out=in_tile[k][:, t:t + 1])
                    link(last)
                dve.sem_inc(rows_used, 1)
                dve.wait_ge(before_done, g + 1)
                for k in range(2):
                    link(nc.vector.tensor_tensor(hsel[k][:, :, :], hsel[k][:, :, :],
                                                 bank[4 + k][0:EP, 0:GT * HI].rearrange("e (t h) -> e t h", h=HI),
                                                 ALU.mult))
                    link(nc.vector.tensor_reduce(before[k][:, :], hsel[k][:, :, :], AX_X, ALU.add))
                    link(nc.vector.tensor_tensor(before[k][:, :], before[k][:, :], in_tile[k][:, :], ALU.add))
                    link(nc.vector.tensor_scalar(row21[k][:, :], bc[k][:, bass.ds(g * GT, GT)], 1.0, None, ALU.mult))
                    link(nc.vector.scalar_tensor_tensor(row21[k][:, :], before[k][:, :], float(BPC), row21[k][:, :],
                                                        ALU.mult, ALU.add))
                if not first:
                    dve.wait_ge(rec_out[h], i * (GT * 16))
                link(nc.vector.tensor_copy(srow[h][:, :], row21[0][:, :]))
                link(nc.vector.tensor_copy(rec[h][:, :, 2:3].bitcast(U32).rearrange("e t o -> e (t o)"), row21[1][:, :]))
                for c, a in ((0, jn[0]), (6, jn[1]), (7, jn[1])):
                    link(nc.vector.tensor_scalar(rec[h][:, :, c:c + 1].rearrange("e t o -> e (t o)"),
                                                 a[:, bass.ds(g * GT, GT)], 1.0, None, ALU.mult))
                link(nc.vector.tensor_scalar(rec[h][:, :, 1:2].bitcast(I32).rearrange("e t o -> e (t o)"),
                                             key_i[1][:, bass.ds(g * GT, GT)], 1.0, None, ALU.mult))
                link(nc.vector.tensor_scalar(rec[h][:, :, 3:3 + DIM], attr_sb[:, bass.ds(g * GT, GT), :], 1.0, None,
                                             ALU.mult))
                dve.sem_inc(rec_set, 1)
                return count[0]

            RANK_STEPS = 27
            for h in range(2):
                rank_group(h, 0, h, first=True, between=section_chunks if h == 0 else None)
            with dve.Fori(1, NG // 2) as i:
                for h in range(2):
                    n = rank_group(i * 2 + h, i, h)
                    assert n == RANK_STEPS, n
            prep_vector(dve)



class Keep:
    pass


def keep_tiles(nc, ctx):
    k = Keep()

    def sb(name, shape, dt=F32):
        return ctx.enter_context(nc.sbuf_tensor(name, shape, dt))

    k.sect = sb("sect", [1, 2, MAXSEC], I32)
    k.sect_count = sb("sect_count", [1, 4], I32)
    k.ident = sb("ident", [P, P])
    return k


def keep_node_tiles(nc, ctx, k):
    def sb(name, shape, dt=F32):
        return ctx.enter_context(nc.sbuf_tensor(name, shape, dt))

    k.iota_j = sb("iota_j", [P, NB])
    k.bmask = sb("bmask", [CN, BPC])
    k.pieces = sb("pieces", [P, 4, KS])
    k.x = sb("x_sb", [CN, NC, FEAT])
    k.tab_a = sb("tab_a", [CN, NC, TROW])
    k.er = sb("er", [CN, NC, HEADS])
    k.wc = sb("wc", [FEAT + 1, HEADS, HW])
    k.gh = sb("gh", [CN, NC, G3])
    k.bih = sb("bih", [CN, G3])
    k.b2 = sb("b2", [CN, HID])
    k.b3 = sb("b3", [CN, HID])
    k.b4 = sb("b4", [CN, DIM])
    k.w3 = sb("w3", [HID, HID])
    k.w4 = sb("w4", [HID, DIM])
    k.inv_deg = sb("inv_deg", [CN, NC])
    k.shift = sb("shift", [CN, NC, DIM])


def hat_weights(nc, link, k, pos, w, rise, fall, blocks):
    def knots(row):
        return k.pieces[:, row:row + 1, :].to_broadcast([P, blocks * DIM, KS])
    wv, rv, fv = (t.rearrange("p b d i -> p (b d) i") for t in (w, rise, fall))
    pv = pos.rearrange("p b d -> p (b d)").unsqueeze(2).to_broadcast([P, blocks * DIM, KS])
    nc.vector.tensor_tensor(rv, pv, knots(0), ALU.add)
    link(nc.vector.tensor_tensor(fv, knots(2), pv, ALU.subtract))
    nc.vector.tensor_tensor(rv, rv, knots(1), ALU.max)
    link(nc.vector.tensor_tensor(fv, fv, knots(3), ALU.max))
    link(nc.vector.tensor_tensor(wv, rv, fv, ALU.min))


def layer_norm(nc, dve, link, x, xm, sq, stat, h, var_set, sd_set, at):
    shape = [CN, NC, FEAT]
    link(nc.vector.tensor_reduce(stat[:, 0, :], x, AX_X, ALU.add))
    link(nc.vector.tensor_scalar(stat[:, 0, :], stat[:, 0, :], 1.0 / FEAT, None, ALU.mult))
    link(nc.vector.tensor_tensor(xm[:, :, :], x, stat[:, 0, :].unsqueeze(2).to_broadcast(shape), ALU.subtract))
    link(nc.vector.tensor_tensor(sq[:, :, :], xm[:, :, :], xm[:, :, :], ALU.mult))
    link(nc.vector.tensor_reduce(stat[:, 1, :], sq[:, :, :], AX_X, ALU.add))
    link(nc.vector.tensor_scalar(stat[:, 1, :], stat[:, 1, :], 1.0 / FEAT, 1e-5, ALU.mult, ALU.add))
    dve.sem_inc(var_set, 1)
    dve.wait_ge(sd_set, at)
    link(nc.vector.reciprocal(stat[:, 3, :], stat[:, 2, :]))
    link(nc.vector.tensor_tensor(xm[:, :, :], xm[:, :, :], stat[:, 3, :].unsqueeze(2).to_broadcast(shape), ALU.mult))
    link(nc.vector.tensor_scalar(h, xm[:, :, :], 0.0, None, ALU.max))


def rows_of(dram, f):
    return dram.rearrange("(c p) f -> p c f", p=CN)


def build_send(nc, a, k, slots_dram, drows_dram, h1_dram):
    with ExitStack() as ctx:
        def sb(name, shape, dt=F32):
            return ctx.enter_context(nc.sbuf_tensor(name, shape, dt))

        def sem(name):
            return ctx.enter_context(nc.semaphore(name))

        w1 = sb("w1", [K + 1, HID + 1])
        b1 = sb("b1", [CN, HID])
        slot = sb("slot", [P, BPC, SREC])
        oh = sb("oh", [P, BPC, NB])
        ohT = sb("ohT", [CN, P])
        bd = sb("bd", [CN, BPC, TROW])
        posd = [sb(f"posd{g}", [P, GB], U32) for g in range(NGR)]
        load = [sb(f"load{g}", [P, GB, DREC]) for g in range(NGR)]
        pos = sb("pos", [P, BPC, DIM])
        rise = sb("rise", [P, BPC, DIM, KS])
        fall = sb("fall", [P, BPC, DIM, KS])
        hat = sb("hat", [P, BPC, DIM, KS])
        uv = [sb(f"uv{g}", [P, GB, KS, KS]) for g in range(NGR)]
        bas = [sb(f"bas{g}", [P, GB, K + 1]) for g in range(NGR)]
        t1 = sb("t1", [K + 1, CN])
        acc = sb("acc", [CN, NC, HID + 1])
        v1 = sb("v1", [CN, NC, HID])
        e1 = sb("e1", [CN, NC, HID])
        bank = [ctx.enter_context(nc.psum_tensor(f"send_bank{i}", [P, 512], F32)) for i in range(8)]

        w1_in = sem("w1_in")
        const_step = sem("const_step")
        const2_step = sem("const2_step")
        slot_in = sem("slot_in")
        slot_used = sem("slot_used")
        oh_set = sem("oh_set")
        ohT_done = sem("ohT_done")
        ohT_set = sem("ohT_set")
        bd_set = sem("bd_set")
        spread_done = sem("spread_done")
        load_set = sem("load_set")
        posd_set = sem("posd_set")
        sent = [sem(f"sent{g}") for g in range(NGR)]
        bas_set = sem("bas_set")
        t1_done = sem("t1_done")
        t1_set = sem("t1_set")
        out1_done = sem("out1_done")
        acc_set = sem("acc_set")
        sec_step = sem("sec_step2")
        neg_set = sem("neg_set")
        exp_set = sem("exp_set")
        h1_set = sem("h1_set")
        h1_out = sem("h1_out")
        end_step = sem("end_step")

        block = ctx.enter_context(nc.Block())

        @block.sync
        def _(sp):
            sp.wait_ge(const_step, 4)
            sp.dma_start(w1[0:K, 0:HID], a["L1_gnn_stn1_w"].rearrange("k o f -> k (o f)")).then_inc(w1_in, 16)
            sp.dma_start(b1[:, :], a["L1_gnn_stn1_b"].rearrange("(o f) -> o f", o=1).to_broadcast([CN, HID]))\
              .then_inc(w1_in, 16)

            def load_slots(s):
                sp.dma_start(slot[:, :, :].rearrange("p b w -> p (b w)"),
                             slots_dram[bass.ds(s * SROWS, SROWS), :].rearrange("(p b) w -> p (b w)", b=BPC))\
                  .then_inc(slot_in, 16)

            sections = sp.value_load(k.sect_count[0:1, 0:1], min_val=NC, max_val=MAXSEC - 2)
            load_slots(0)
            with sp.Fori(1, sections) as s:
                sp.wait_ge(slot_used, s)
                load_slots(s)
            sp.wait_ge(h1_set, 1)
            sp.dma_start(rows_of(h1_dram, HID), v1[:, :, :]).then_inc(h1_out, 16)
            sp.wait_ge(h1_out, 16)

        @block.gpsimd
        def _(pool):
            nc.gpsimd.iota(k.iota_j[:, :], pattern=[[1, NB]], base=0, channel_multiplier=0,
                           allow_small_or_imprecise_dtypes=True).then_inc(const_step, 1)
            nc.gpsimd.memset(k.bmask[:, :], 1.0).then_inc(const_step, 1)
            nc.gpsimd.memset(w1[:, :], 0.0).then_inc(const_step, 1)
            pool.wait_ge(const_step, 3)
            nc.gpsimd.affine_select(out=w1[:, HID:HID + 1], in_=w1[:, HID:HID + 1], compare_op=ALU.not_equal, fill=1.0,
                                    base=-K, pattern=[[0, 1]], channel_multiplier=1).then_inc(const_step, 1)
            nc.gpsimd.affine_select(out=k.bmask[:, :], in_=k.bmask[:, :], compare_op=ALU.is_ge, fill=0.0,
                                    base=0, pattern=[[-NB, BPC]], channel_multiplier=1).then_inc(const_step, 1)
            pool.wait_ge(const_step, 5)
            nc.gpsimd.affine_select(out=k.bmask[:, :], in_=k.bmask[:, :], compare_op=ALU.is_ge, fill=0.0,
                                    base=NB - 1, pattern=[[NB, BPC]], channel_multiplier=-1).then_inc(const_step, 1)
            sections = pool.value_load(k.sect_count[0:1, 0:1], min_val=NC, max_val=MAXSEC - 2)

            def send(s):
                for g in range(NGR):
                    pool.wait_ge(load_set, s * NGR + (g + 1))
                    pool.wait_ge(posd_set, s * NGR + (g + 1))
                    pool.nop(nofuse=True)
                    for b in range(GB):
                        nc.gpsimd.indirect_dma_start(
                            drows_dram[:, :], bass.IndirectOffsetOnAxis(ap=posd[g][:, b:b + 1], axis=0),
                            load[g][:, b, :], None, bounds_check=MAXSEC * SROWS - 1, oob_is_err=False)\
                            .then_inc(sent[g], 16)
            send(0)
            with pool.Fori(1, sections) as s:
                send(s)
            for g in range(NGR):
                pool.wait_ge(sent[g], sections * (GB * 16))

        @block.scalar
        def _(act):
            sections = act.value_load(k.sect_count[0:1, 0:1], min_val=NC, max_val=MAXSEC - 2)

            def section(s, first):
                act.wait_ge(ohT_done, s + 1)
                if not first:
                    act.wait_ge(spread_done, s * NGR)
                nc.scalar.copy(ohT[:, :], bank[0][0:CN, 0:P]).then_inc(ohT_set, 1)
                for g in range(NGR):
                    act.wait_ge(spread_done, s * NGR + (g + 1))
                    if not first:
                        act.wait_ge(sent[g], s * (GB * 16))
                    nc.scalar.copy(load[g][:, :, 0:TROW],
                                   bank[1 + g][:, 0:GB * TROW].rearrange("p (b f) -> p b f", b=GB)).then_inc(load_set, 1)
                act.wait_ge(t1_done, s + 1)
                if not first:
                    act.wait_ge(out1_done, s)
                nc.scalar.copy(t1[:, :], bank[4][0:K + 1, 0:CN]).then_inc(t1_set, 1)

            section(0, True)
            with act.Fori(1, sections) as s:
                section(s, False)
            act.wait_ge(neg_set, 1)
            nc.scalar.activation(e1[:, :, :], e1[:, :, :], ACT.Exp).then_inc(exp_set, 1)

        @block.tensor
        def _(pe):
            pe.wait_ge(w1_in, 32)
            sections = pe.value_load(k.sect_count[0:1, 0:1], min_val=NC, max_val=MAXSEC - 2)

            def section(s, first):
                pe.wait_ge(oh_set, s + 1)
                nc.tensor.transpose(bank[0][0:CN, 0:P], oh[:, :, :].rearrange("p b j -> p (b j)"), k.ident[:, :])\
                    .then_inc(ohT_done, 1)
                pe.wait_ge(ohT_set, s + 1)
                pe.wait_ge(bd_set, s + 1)
                for g in range(NGR):
                    if not first:
                        pe.wait_ge(load_set, s * NGR - (NGR - 1 - g))
                    nc.tensor.matmul(bank[1 + g][:, 0:GB * TROW], ohT[:, :],
                                     bd[:, g * GB:(g + 1) * GB, :].rearrange("n b f -> n (b f)"),
                                     start=True, stop=True).then_inc(spread_done, 1)
                if not first:
                    pe.wait_ge(t1_set, s)
                for g in range(NGR):
                    pe.wait_ge(bas_set, s * NGR + (g + 1))
                    for b in range(g * GB, (g + 1) * GB):
                        last = nc.tensor.matmul(bank[4][0:K + 1, b * NB:(b + 1) * NB], bas[g][:, b - g * GB, :],
                                                oh[:, b, :], start=True, stop=True)
                last.then_inc(t1_done, 1)
                pe.wait_ge(t1_set, s + 1)
                if not first:
                    pe.wait_ge(acc_set, s)
                nc.tensor.matmul(bank[5][0:CN, 0:HID + 1], t1[:, :], w1[:, :], start=True, stop=True)\
                    .then_inc(out1_done, 1)

            section(0, True)
            with pe.Fori(1, sections) as s:
                section(s, False)

        @block.vector
        def _(dve):
            link, count = links(dve, const2_step)
            for row, (v, odd, at) in enumerate(((0.0, 0.0, None), (0.0, -BIG, 1), (0.0, 0.0, None), (0.0, -BIG, 3))):
                if row in (0, 2):
                    for i in range(KS):
                        val = (BIG if i == 0 else 1.0 - i) if row == 0 else (BIG if i == KS - 1 else 1.0 + i)
                        last = nc.vector.memset(k.pieces[:, row, i:i + 1], val)
                else:
                    link(nc.vector.memset(k.pieces[:, row, :], v))
                    last = nc.vector.memset(k.pieces[:, row, at:at + 1], odd)
            for g in range(NGR):
                last = nc.vector.memset(bas[g][:, :, K:K + 1], 1.0)
            link(nc.vector.memset(acc[:, :, :], 0.0))
            dve.wait_ge(const_step, 6)
            sections = dve.value_load(k.sect_count[0:1, 0:1], min_val=NC, max_val=MAXSEC - 2)

            def add_out(s_last):
                c = dve.value_load(k.sect[0:1, 0, bass.ds(s_last, 1)], min_val=0, max_val=NC - 1)
                sl = acc[:, bass.ds(c, 1), :].rearrange("n c f -> n (c f)")
                return nc.vector.tensor_tensor(sl, sl, bank[5][0:CN, 0:HID + 1], ALU.add)

            def section(s, first):
                link, count = links(dve, sec_step, s * SEND_STEPS)
                c = dve.value_load(k.sect[0:1, 0, bass.ds(s, 1)], min_val=0, max_val=NC - 1)
                dve.wait_ge(slot_in, s * 16 + 16)
                if not first:
                    dve.wait_ge(t1_done, s)
                link(nc.vector.tensor_tensor(oh[:, :, :], k.iota_j[:, :].unsqueeze(1).to_broadcast([P, BPC, NB]),
                                             slot[:, :, 0:1].to_broadcast([P, BPC, NB]), ALU.is_equal))
                dve.sem_inc(oh_set, 1)
                if not first:
                    dve.wait_ge(spread_done, s * NGR)
                link(nc.vector.tensor_tensor(
                    bd[:, :, :], k.tab_a[:, bass.ds(c, 1), :].to_broadcast([CN, BPC, TROW]),
                    k.bmask[:, :].unsqueeze(2).to_broadcast([CN, BPC, TROW]), ALU.mult))
                dve.sem_inc(bd_set, 1)

                def places(g):
                    if not first:
                        dve.wait_ge(sent[g], s * (GB * 16))
                    part = slot[:, g * GB:(g + 1) * GB, :]
                    nc.vector.tensor_copy(load[g][:, :, DREC - 1:DREC], part[:, :, 6:7])
                    nc.vector.tensor_copy(posd[g][:, :], part[:, :, 2:3].bitcast(U32).rearrange("p b o -> p (b o)"))\
                        .then_inc(posd_set, 1)
                for g in range(NGR - 1):
                    places(g)
                link(nc.vector.tensor_scalar(pos[:, :, :], slot[:, :, 3:3 + DIM], float(KS - 1), None, ALU.mult))
                hat_weights(nc, link, k, pos[:, :, :], hat[:, :, :, :], rise[:, :, :, :], fall[:, :, :, :], BPC)
                for g in range(NGR):
                    w = hat[:, g * GB:(g + 1) * GB, :, :]
                    link(nc.vector.tensor_tensor(uv[g][:, :, :, :], w[:, :, 0, :].unsqueeze(3).to_broadcast([P, GB, KS, KS]),
                                                 w[:, :, 1, :].unsqueeze(2).to_broadcast([P, GB, KS, KS]), ALU.mult))
                    nc.vector.tensor_tensor(
                        bas[g][:, :, 0:K].rearrange("p b (u i) -> p b u i", i=KS),
                        uv[g][:, :, :, :].rearrange("p b i j -> p b (i j)").unsqueeze(3).to_broadcast([P, GB, KS * KS, KS]),
                        w[:, :, 2, :].unsqueeze(2).to_broadcast([P, GB, KS * KS, KS]), ALU.mult).then_inc(bas_set, 1)
                places(NGR - 1)
                dve.wait_ge(posd_set, s * NGR + NGR)
                dve.sem_inc(slot_used, 1)
                if not first:
                    dve.wait_ge(out1_done, s)
                    link(add_out(s - 1))
                    dve.sem_inc(acc_set, 1)
                else:
                    dve.sem_inc(sec_step, 1)
                return count[0]

            SEND_STEPS = 10
            section(0, True)
            with dve.Fori(1, sections) as s:
                n = section(s, False)
                assert n == SEND_STEPS, n
            link, count = links(dve, end_step)
            dve.wait_ge(out1_done, sections)
            link(add_out(sections - 1))
            link(nc.vector.tensor_scalar(k.inv_deg[:, :], acc[:, :, HID:HID + 1].rearrange("n c o -> n (c o)"), 1.0, None,
                                         ALU.max))
            link(nc.vector.reciprocal(k.inv_deg[:, :], k.inv_deg[:, :]))
            link(nc.vector.tensor_tensor(v1[:, :, :], acc[:, :, 0:HID],
                                         k.inv_deg[:, :].unsqueeze(2).to_broadcast([CN, NC, HID]), ALU.mult))
            link(nc.vector.tensor_tensor(v1[:, :, :], v1[:, :, :], b1[:, :].unsqueeze(1).to_broadcast([CN, NC, HID]),
                                         ALU.add))
            link(nc.vector.tensor_scalar(e1[:, :, :], v1[:, :, :], 0.0, None, ALU.min))
            dve.sem_inc(neg_set, 1)
            link(nc.vector.tensor_scalar(v1[:, :, :], v1[:, :, :], 0.0, None, ALU.max))
            dve.wait_ge(exp_set, 1)
            link(nc.vector.scalar_tensor_tensor(v1[:, :, :], e1[:, :, :], -1.0, v1[:, :, :], ALU.add, ALU.add))
            dve.sem_inc(h1_set, 1)


def conv_tiles(nc, ctx, fi, prefix):
    t = Keep()

    def sb(name, shape, dt=F32):
        return ctx.enter_context(nc.sbuf_tensor(prefix + name, shape, dt))

    t.slot = sb("slot", [P, BPC, SREC])
    t.index = [sb(f"index{g}", [P, GB], U32) for g in range(NGR)]
    t.oh = sb("oh", [P, BPC, NB])
    t.rise = sb("rise", [P, BPC, DIM, KS])
    t.fall = sb("fall", [P, BPC, DIM, KS])
    t.hat = sb("hat", [P, BPC, DIM, KS])
    t.uv = [sb(f"uv{g}", [P, GB, KS, KS]) for g in range(NGR)]
    t.bas = [sb(f"bas{g}", [P, GB, K]) for g in range(NGR)]
    t.mixed = [sb(f"mixed{g}", [P, GB, NB, fi]) for g in range(NGR)]
    t.sums = sb("sums", [K, CN, fi])
    return t


def basis_group(nc, t, g, link):
    w = t.hat[:, g * GB:(g + 1) * GB, :, :]
    link(nc.vector.tensor_tensor(t.uv[g][:, :, :, :], w[:, :, 0, :].unsqueeze(3).to_broadcast([P, GB, KS, KS]),
                                 w[:, :, 1, :].unsqueeze(2).to_broadcast([P, GB, KS, KS]), ALU.mult))
    return nc.vector.tensor_tensor(
        t.bas[g][:, :, :].rearrange("p b (u i) -> p b u i", i=KS),
        t.uv[g][:, :, :, :].rearrange("p b i j -> p b (i j)").unsqueeze(3).to_broadcast([P, GB, KS * KS, KS]),
        w[:, :, 2, :].unsqueeze(2).to_broadcast([P, GB, KS * KS, KS]), ALU.mult)


def build_mid(nc, a, k, slots_dram, drows_dram, h1_dram, acc, gacc):
    with ExitStack() as ctx:
        def sb(name, shape, dt=F32):
            return ctx.enter_context(nc.sbuf_tensor(name, shape, dt))

        def sem(name):
            return ctx.enter_context(nc.semaphore(name))

        B2 = 2 * BPC
        t = conv_tiles(nc, ctx, HID, "mid_")
        rows = [sb(f"mid_rows{g}", [P, GB, HID]) for g in range(NGR)]
        w2 = sb("w2", [K, HID, HID])
        pos = sb("mid_pos", [P, BPC, DIM])
        drow = sb("drow", [P, B2, DREC])
        ohd = sb("ohd", [P, B2, NB])
        pen = sb("pen", [P, B2, NB])
        masked_el = sb("masked_el", [P, 2, HEADS, BPC, NB])
        top = sb("top", [CN, 2, HEADS])
        m_el = sb("m_el", [CN, NC, HEADS])
        er_m = sb("er_m", [CN, NC, 2 * HEADS])
        ohdT = sb("ohdT", [CN, 2, P])
        bde = sb("bde", [CN, B2, 2 * HEADS])
        score = sb("score", [P, B2, HEADS])
        wexp = sb("wexp", [P, B2, HEADS])
        masked = sb("masked", [P, B2, NB, HEADS])
        bank = [ctx.enter_context(nc.psum_tensor(f"mid_bank{i}", [P, 512], F32)) for i in range(8)]

        w2_in = sem("w2_in")
        layers_in = sem("layers_in")
        slot_in = sem("mid_slot_in")
        slot_used = sem("mid_slot_used")
        index_set = sem("mid_index_set")
        rows_in = [sem(f"mid_rows_in{g}") for g in range(NGR)]
        mixed_set = sem("mid_mixed_set")
        sum_done = sem("mid_sum_done")
        sum_set = sem("mid_sum_set")
        out_done = sem("mid_out_done")
        acc_set = sem("mid_acc_set")
        first_half = sem("first_half_step")
        second_half = sem("second_half_step")
        init_step = sem("mid_init_step")
        tail_step = sem("mid_tail_step")
        drow_in = sem("drow_in")
        drow_used = sem("drow_used")
        masked_set = sem("masked_set")
        masked_turned = sem("masked_turned")
        tops_set = sem("tops_set")
        ohd_set = sem("ohd_set")
        ohdT_done = sem("ohdT_done")
        ohdT_set = sem("ohdT_set")
        bde_set = sem("bde_set")
        erm_done = sem("erm_done")
        score_set = sem("score_set")
        wexp_set = sem("wexp_set")
        weights_set = sem("weights_set")
        att_done = sem("att_done")
        gacc_set = sem("gacc_set")
        gacc_clear = sem("gacc_clear")

        EW = BPC * 2 * HEADS

        def row(name, n):
            return a[name].rearrange("(o f) -> o f", o=1).to_broadcast([CN, n])

        def counts(eng):
            return (eng.value_load(k.sect_count[0:1, 0:1], min_val=NC, max_val=MAXSEC - 2),
                    eng.value_load(k.sect_count[0:1, 2:3], min_val=NC // 2, max_val=(MAXSEC - 1) // 2),
                    eng.value_load(k.sect_count[0:1, 3:4], min_val=NC // 2, max_val=(MAXSEC - 2) // 2))

        block = ctx.enter_context(nc.Block())

        @block.sync
        def _(sp):
            def load_slots(s):
                sp.dma_start(t.slot[:, :, :].rearrange("p b w -> p (b w)"),
                             slots_dram[bass.ds(s * SROWS, SROWS), :].rearrange("(p b) w -> p (b w)", b=BPC))\
                  .then_inc(slot_in, 16)

            def load_drows(i):
                sp.dma_start(drow[:, :, :].rearrange("p (h b) w -> p h (b w)", h=2),
                             drows_dram[bass.ds(i * (2 * SROWS), 2 * SROWS), :]
                             .rearrange("(h p b) w -> p h (b w)", h=2, b=BPC)).then_inc(drow_in, 16)

            def next_slots(s):
                sp.wait_ge(slot_used, s)
                sp.nop(nofuse=True)
                sp.wait_ge(index_set, s * NGR)
                sp.nop(nofuse=True)
                load_slots(s)

            def next_drows(s, i):
                sp.wait_ge(drow_used, s)
                sp.nop(nofuse=True)
                load_drows(i)

            sections, pairs, halves = counts(sp)
            load_slots(0)
            load_drows(0)
            sp.dma_start(w2[:, :, :], a["L1_gnn_stn2_w"]).then_inc(w2_in, 16)
            for tile, source in (
                    (k.b2, row("L1_gnn_stn2_b", HID)), (k.w3, a["L1_gnn_stn3_w"]), (k.w4, a["L1_gnn_stn4_w"]),
                    (k.b3, row("L1_gnn_stn3_b", HID)), (k.b4, row("L1_gnn_stn4_b", DIM))):
                sp.dma_start(tile[:, :], source).then_inc(layers_in, 16)
            with sp.Fori(1, pairs) as s:
                next_slots(s)
                next_drows(s, s)
            with sp.Fori(0, halves) as i:
                s = i + pairs
                next_slots(s)
                next_drows(s, i)
            next_slots(sections)
            next_drows(sections, halves)
            sp.wait_ge(slot_in, sections * 16 + 16)
            sp.nop(nofuse=True)
            sp.wait_ge(layers_in, 80)
            sp.nop(nofuse=True)

        @block.gpsimd
        def _(pool):
            sections = pool.value_load(k.sect_count[0:1, 0:1], min_val=NC, max_val=MAXSEC - 2)

            def fetch(s, first):
                for g in range(NGR):
                    pool.wait_ge(index_set, s * NGR + (g + 1))
                    if not first:
                        pool.wait_ge(mixed_set, s * NGR - (NGR - 1 - g))
                    pool.nop(nofuse=True)
                    for b in range(GB):
                        nc.gpsimd.indirect_dma_start(
                            rows[g][:, b, :], None, h1_dram[:, :],
                            bass.IndirectOffsetOnAxis(ap=t.index[g][:, b:b + 1], axis=0)).then_inc(rows_in[g], 16)
            fetch(0, True)
            nc.gpsimd.memset(gacc[:, :, :], 0.0).then_inc(gacc_clear, 1)
            with pool.Fori(1, sections) as s:
                fetch(s, False)

        @block.scalar
        def _(act):
            def indices(g):
                nc.scalar.copy(t.index[g][:, :], t.slot[:, g * GB:(g + 1) * GB, 1:2].bitcast(U32)
                               .rearrange("p b o -> p (b o)")).then_inc(index_set, 1)

            act.wait_ge(slot_in, 16)
            for g in range(NGR):
                indices(g)
            sections, pairs, halves = counts(act)

            def turned_out(i, first):
                act.wait_ge(ohdT_done, i + 1)
                if not first:
                    act.wait_ge(erm_done, i)
                nc.scalar.copy(ohdT[:, :, :].rearrange("n h e -> n (h e)"), bank[4][0:CN, 0:2 * P]).then_inc(ohdT_set, 1)

            def weights(i):
                act.wait_ge(score_set, i + 1)
                nc.scalar.activation(wexp[:, :, :], score[:, :, :], ACT.Exp).then_inc(wexp_set, 1)

            def convolve(s, first, i=None):
                for g in range(NGR):
                    act.wait_ge(slot_in, s * 16 + 32)
                    act.wait_ge(rows_in[g], s * (GB * 16) + GB * 16)
                    indices(g)
                    for b in range(g * GB, (g + 1) * GB):
                        act.wait_ge(sum_done, s * BPC + (b + 1))
                        if b == 0 and not first:
                            act.wait_ge(out_done, s)
                        nc.scalar.copy(t.sums[:, b * NB:(b + 1) * NB, :].rearrange("k n f -> k (n f)"),
                                       bank[b % 3][0:K, 0:NB * HID]).then_inc(sum_set, 1)
                        if b == GB + 2 and i is not None:
                            weights(i)

            convolve(0, True)
            with act.Fori(1, pairs) as s:
                convolve(s, False)
            turned_out(0, True)
            convolve(pairs, False, 0)
            with act.Fori(1, halves) as i:
                turned_out(i, False)
                convolve(i + pairs, False, i)
            turned_out(halves, False)
            weights(halves)

        @block.tensor
        def _(pe):
            sections, pairs, halves = counts(pe)
            pe.wait_ge(w2_in, 16)

            def sums_of(s, g):
                pe.wait_ge(mixed_set, s * NGR + (g + 1))
                for b in range(g * GB, (g + 1) * GB):
                    if b >= 3:
                        pe.wait_ge(sum_set, s * BPC + (b - 2))
                    nc.tensor.matmul(bank[b % 3][0:K, 0:NB * HID], t.bas[g][:, b - g * GB, :],
                                     t.mixed[g][:, b - g * GB, :, :].rearrange("p j f -> p (j f)"),
                                     start=True, stop=True).then_inc(sum_done, 1)

            def products(s, first):
                pe.wait_ge(sum_set, s * BPC + BPC)
                if not first:
                    pe.wait_ge(acc_set, s)
                for i in range(HID):
                    last = nc.tensor.matmul(bank[3][0:CN, 0:HID], t.sums[:, :, i], w2[:, i, :],
                                            start=(i == 0), stop=(i == HID - 1))
                last.then_inc(out_done, 1)

            def turn_el(s, first):
                pe.wait_ge(masked_set, s + 1)
                if not first:
                    pe.wait_ge(tops_set, s)
                for h in range(2):
                    for q in range(HEADS):
                        last = nc.tensor.transpose(bank[4 + h][0:CN, q * P:(q + 1) * P],
                                                   masked_el[:, h, q, :, :].rearrange("p b j -> p (b j)"), k.ident[:, :])
                last.then_inc(masked_turned, 1)

            def turn_one_hots(i):
                pe.wait_ge(ohd_set, i + 1)
                for h in range(2):
                    last = nc.tensor.transpose(bank[4][0:CN, h * P:(h + 1) * P],
                                               ohd[:, h * BPC:(h + 1) * BPC, :].rearrange("p b j -> p (b j)"),
                                               k.ident[:, :])
                last.then_inc(ohdT_done, 1)

            def spread(i):
                pe.wait_ge(ohdT_set, i + 1)
                pe.wait_ge(bde_set, i + 1)
                for h in range(2):
                    last = nc.tensor.matmul(bank[5][:, h * EW:(h + 1) * EW], ohdT[:, h, :],
                                            bde[:, h * BPC:(h + 1) * BPC, :].rearrange("n b w -> n (b w)"),
                                            start=True, stop=True)
                last.then_inc(erm_done, 1)

            def attend(i, first):
                pe.wait_ge(weights_set, i + 1)
                if not first:
                    pe.wait_ge(gacc_set, i)
                for b in range(B2):
                    at = b % BPC * (NB * HEADS)
                    last = nc.tensor.matmul(bank[6 + b // BPC][0:FEAT + 1, at:at + NB * HEADS],
                                            drow[:, b, 0:FEAT + 1],
                                            masked[:, b, :, :].rearrange("p j h -> p (j h)"), start=True, stop=True)
                last.then_inc(att_done, 1)

            def section_and_maxima(s, first):
                sums_of(s, 0)
                turn_el(s, first)
                sums_of(s, 1)
                sums_of(s, 2)
                products(s, first)

            def section_and_sums(s, i, first):
                turn_one_hots(i)
                sums_of(s, 0)
                spread(i)
                sums_of(s, 1)
                sums_of(s, 2)
                attend(i, first)
                products(s, False)

            section_and_maxima(0, True)
            with pe.Fori(1, pairs) as s:
                section_and_maxima(s, False)
            section_and_sums(pairs, 0, True)
            with pe.Fori(1, halves) as i:
                section_and_sums(i + pairs, i, False)
            turn_one_hots(halves)
            spread(halves)
            attend(halves, False)

        @block.vector
        def _(dve):
            sections, pairs, halves = counts(dve)
            link, count = links(dve, init_step)
            nc.vector.memset(acc[:, :, :], 0.0)
            link(nc.vector.memset(m_el[:, :, :], -BIG))

            def chunk(key, s):
                return dve.value_load(k.sect[0:1, key, bass.ds(s, 1)], min_val=0, max_val=NC - 1)

            def front(s, link):
                dve.wait_ge(slot_in, s * 16 + 16)
                link(nc.vector.tensor_tensor(t.oh[:, :, :], k.iota_j[:, :].unsqueeze(1).to_broadcast([P, BPC, NB]),
                                             t.slot[:, :, 0:1].to_broadcast([P, BPC, NB]), ALU.is_equal))
                link(nc.vector.tensor_scalar(pos[:, :, :], t.slot[:, :, 3:3 + DIM], float(KS - 1), None, ALU.mult))
                dve.sem_inc(slot_used, 1)
                hat_weights(nc, link, k, pos[:, :, :], t.hat[:, :, :, :], t.rise[:, :, :, :], t.fall[:, :, :, :], BPC)

            def mix(s, g, used, link):
                if used is not None:
                    dve.wait_ge(sum_done, used)
                basis_group(nc, t, g, link)
                dve.wait_ge(rows_in[g], s * (GB * 16) + GB * 16)
                link(nc.vector.tensor_tensor(
                    t.mixed[g][:, :, :, :],
                    t.oh[:, g * GB:(g + 1) * GB, :].unsqueeze(3).to_broadcast([P, GB, NB, HID]),
                    rows[g][:, :, :].unsqueeze(2).to_broadcast([P, GB, NB, HID]), ALU.mult))
                dve.sem_inc(mixed_set, 1)

            def add_products(s):
                dve.wait_ge(out_done, s)
                sl = acc[:, bass.ds(chunk(0, s - 1), 1), :].rearrange("n c f -> n (c f)")
                return nc.vector.tensor_tensor(sl, sl, bank[3][0:CN, 0:HID], ALU.add)

            def one_hot_d():
                return nc.vector.tensor_tensor(
                    ohd[:, :, :], k.iota_j[:, :].unsqueeze(1).to_broadcast([P, B2, NB]),
                    drow[:, :, DREC - 1:DREC].to_broadcast([P, B2, NB]), ALU.is_equal)

            def mask_el(s, link):
                dve.wait_ge(drow_in, s * 16 + 16)
                link(one_hot_d())
                link(nc.vector.tensor_scalar(pen[:, :, :], ohd[:, :, :], -1.0, BIG, ALU.add, ALU.mult))
                for h in range(2):
                    blocks = slice(h * BPC, (h + 1) * BPC)
                    last = nc.vector.tensor_tensor(
                        masked_el[:, h, :, :, :].rearrange("p q b j -> p b j q"),
                        pen[:, blocks, :].unsqueeze(3).to_broadcast([P, BPC, NB, HEADS]),
                        drow[:, blocks, FEAT + 1:TROW].unsqueeze(2).to_broadcast([P, BPC, NB, HEADS]), ALU.add)
                link(last)
                dve.sem_inc(masked_set, 1)
                dve.sem_inc(drow_used, 1)

            def find_max(s, link):
                dve.wait_ge(masked_turned, s + 1)
                for h in range(2):
                    last = nc.vector.tensor_reduce(top[:, h, :], bank[4 + h][0:CN, 0:HEADS * P]
                                                   .rearrange("n (q e) -> n q e", e=P), AX_X, ALU.max)
                link(last)
                for h in range(2):
                    sl = m_el[:, bass.ds(chunk(1, s * 2 + h), 1), :].rearrange("n c q -> n (c q)")
                    link(nc.vector.tensor_tensor(sl, sl, top[:, h, :], ALU.max))
                dve.sem_inc(tops_set, 1)

            def destinations(s, i, first, link):
                dve.wait_ge(drow_in, s * 16 + 16)
                link(one_hot_d())
                dve.sem_inc(ohd_set, 1)
                if not first:
                    dve.wait_ge(erm_done, i)
                for h in range(2):
                    last = nc.vector.tensor_tensor(
                        bde[:, h * BPC:(h + 1) * BPC, :],
                        er_m[:, bass.ds(chunk(1, i * 2 + h), 1), :].to_broadcast([CN, BPC, 2 * HEADS]),
                        k.bmask[:, :].unsqueeze(2).to_broadcast([CN, BPC, 2 * HEADS]), ALU.mult)
                link(last)
                dve.sem_inc(bde_set, 1)

            def weigh(i, link):
                dve.wait_ge(erm_done, i + 1)
                erm = bank[5][:, 0:2 * EW].rearrange("p (b w) -> p b w", b=B2)
                link(nc.vector.tensor_tensor(score[:, :, :], drow[:, :, FEAT + 1:TROW], erm[:, :, 0:HEADS], ALU.add))
                link(nc.vector.scalar_tensor_tensor(score[:, :, :], score[:, :, :], 0.2, score[:, :, :],
                                                    ALU.mult, ALU.max))
                link(nc.vector.tensor_tensor(score[:, :, :], score[:, :, :], erm[:, :, HEADS:2 * HEADS], ALU.subtract))
                dve.sem_inc(score_set, 1)
                dve.wait_ge(wexp_set, i + 1)
                link(nc.vector.tensor_tensor(
                    masked[:, :, :, :], ohd[:, :, :].unsqueeze(3).to_broadcast([P, B2, NB, HEADS]),
                    wexp[:, :, :].unsqueeze(2).to_broadcast([P, B2, NB, HEADS]), ALU.mult))
                dve.sem_inc(weights_set, 1)

            def add_sums(i, link):
                dve.wait_ge(att_done, i)
                for h in range(2):
                    sl = gacc[:, bass.ds(chunk(1, i * 2 + (h - 2)), 1), :].rearrange("f c w -> f (c w)")
                    link(nc.vector.tensor_tensor(sl, sl, bank[6 + h][0:FEAT + 1, 0:BPC * NB * HEADS], ALU.add))

            def section_and_maxima(s, first):
                link, count = links(dve, first_half, s * FIRST_STEPS)
                front(s, link)
                mix(s, 0, None if first else s * BPC - 2 * GB, link)
                mix(s, 1, None if first else s * BPC - GB, link)
                mask_el(s, link)
                mix(s, 2, None if first else s * BPC, link)
                if not first:
                    link(add_products(s))
                    dve.sem_inc(acc_set, 1)
                else:
                    dve.sem_inc(first_half, 1)
                    count[0] += 1
                find_max(s, link)
                assert count[0] == FIRST_STEPS, count[0]

            def section_and_sums(s, i, first):
                link, count = links(dve, second_half, i * SECOND_STEPS)
                front(s, link)
                mix(s, 0, s * BPC if first else s * BPC - 2 * GB, link)
                if not first:
                    add_sums(i, link)
                    dve.sem_inc(gacc_set, 1)
                    dve.sem_inc(drow_used, 1)
                else:
                    dve.sem_inc(second_half, 2)
                    count[0] += 2
                mix(s, 1, s * BPC if first else s * BPC - GB, link)
                destinations(s, i, first, link)
                mix(s, 2, s * BPC if first else s * BPC, link)
                link(add_products(s))
                dve.sem_inc(acc_set, 1)
                weigh(i, link)
                assert count[0] == SECOND_STEPS, count[0]

            FIRST_STEPS, SECOND_STEPS = 18, 20
            section_and_maxima(0, True)
            with dve.Fori(1, pairs) as s:
                section_and_maxima(s, False)
            link(nc.vector.tensor_copy(er_m[:, :, 0:HEADS], k.er[:, :, :]))
            link(nc.vector.tensor_tensor(m_el[:, :, :], m_el[:, :, :], k.er[:, :, :], ALU.add))
            link(nc.vector.scalar_tensor_tensor(er_m[:, :, HEADS:2 * HEADS], m_el[:, :, :], 0.2, m_el[:, :, :],
                                                ALU.mult, ALU.max))
            dve.wait_ge(gacc_clear, 1)
            section_and_sums(pairs, 0, True)
            with dve.Fori(1, halves) as i:
                section_and_sums(i + pairs, i, False)
            link, count = links(dve, tail_step)
            add_sums(halves, link)
            dve.sem_inc(gacc_set, 1)
            dve.sem_inc(drow_used, 1)
            destinations(sections, halves, False, link)
            link(add_products(sections))
            weigh(halves, link)
            add_sums(halves + 1, link)


def build_nodes(nc, a, k, acc, gacc, node3_dram):
    with ExitStack() as ctx:
        def sb(name, shape, dt=F32):
            return ctx.enter_context(nc.sbuf_tensor(name, shape, dt))

        def sem(name):
            return ctx.enter_context(nc.semaphore(name))

        rden = sb("n_rden", [CN, 2, HEADS])
        gih = [sb(f"n_gih{i}", [CN, HEADS, G3]) for i in range(2)]
        gi = sb("n_gi", [CN, NC, G3])
        v = sb("n_v", [CN, NC, HID])
        e = sb("n_e", [CN, NC, HID])
        y3 = sb("n_y3", [CN, NC, HID])
        yT = [sb(f"n_yT{i}", [HID, 4, CN]) for i in range(2)]
        nn = sb("n_n", [CN, NC, FEAT])
        xm = sb("n_xm", [CN, NC, FEAT])
        sq = sb("n_sq", [CN, NC, FEAT])
        stat = sb("n_stat", [CN, 4, NC])
        node3 = sb("n_node3", [CN, NC, NROW])
        bank = [ctx.enter_context(nc.psum_tensor(f"n_bank{i}", [P, 512], F32)) for i in range(8)]
        gate_bank = (bank[0], bank[1], bank[7])
        NQ = -(-NC // 4)

        gi_done = sem("gi_done")
        gi_out = sem("gi_out")
        act_in = sem("act_in")
        act_out = sem("act_out")
        v_set = sem("v_set")
        yT_done = sem("yT_done")
        yT_set = sem("yT_set")
        lin_done = sem("lin_done")
        lin_out = sem("lin_out")
        node3_set = sem("node3_set")
        node3_out = sem("node3_out")
        n_step = sem("n_step")
        var_set = sem("n_var_set")
        sd_set = sem("n_sd_set")

        block = ctx.enter_context(nc.Block())

        @block.sync
        def _(sp):
            sp.wait_ge(node3_set, 2)
            sp.dma_start(rows_of(node3_dram, NROW), node3[:, :, :]).then_inc(node3_out, 16)
            sp.wait_ge(node3_out, 16)

        @block.gpsimd
        def _(pool):
            nc.gpsimd.memset(node3[:, :, FEAT + DIM:NROW], 0.0).then_inc(node3_set, 1)

        @block.scalar
        def _(act):
            def apply(i, ap, function):
                act.wait_ge(act_in, i)
                nc.scalar.activation(ap, ap, function).then_inc(act_out, 1)

            def turned_rows(base, steps):
                for q in steps:
                    n = min(4, NC - 4 * q)
                    act.wait_ge(yT_done, base + q + 1)
                    if base + q >= 2:
                        act.wait_ge(lin_done, base + q - 1)
                    nc.scalar.copy(yT[(base + q) % 2][:, 0:n, :].rearrange("f c n -> f (c n)"),
                                   bank[4 + (base + q) % 2][0:HID, 0:n * CN]).then_inc(yT_set, 1)
            apply(1, e[:, :, :], ACT.Exp)
            turned_rows(0, range(NQ))
            apply(2, e[:, :, :], ACT.Exp)
            turned_rows(NQ, (0,))
            apply(3, gi[:, :, 0:2 * FEAT], ACT.Sigmoid)
            turned_rows(NQ, (1,))
            apply(4, nn[:, :, :], ACT.Tanh)
            turned_rows(NQ, (2,))
            apply(5, nn[:, :, :], ACT.Exp)
            turned_rows(NQ, (3, 4))
            act.wait_ge(var_set, 1)
            nc.scalar.activation(stat[:, 2, :], stat[:, 1, :], ACT.Sqrt).then_inc(sd_set, 1)
            turned_rows(NQ, range(5, NQ))

        @block.tensor
        def _(pe):
            def gates(c):
                if c >= 3:
                    pe.wait_ge(gi_out, c - 2)
                for h in range(HEADS):
                    last = nc.tensor.matmul(
                        gate_bank[c % 3][0:CN, h * HW:(h + 1) * HW],
                        gacc[:, c, :].rearrange("f (n h) -> f n h", h=HEADS)[:, :, h], k.wc[:, h, :], start=True, stop=True)
                last.then_inc(gi_done, 1)

            def turn(base, q, x):
                if base + q >= 2:
                    pe.wait_ge(yT_set, base + q - 1)
                for c in range(min(4, NC - 4 * q)):
                    last = nc.tensor.transpose(bank[4 + (base + q) % 2][0:HID, c * CN:(c + 1) * CN],
                                               x[:, 4 * q + c, :], k.ident[0:CN, 0:CN])
                last.then_inc(yT_done, 1)

            def layer(base, q, w, n_out, bank_of):
                pe.wait_ge(yT_set, base + q + 1)
                for c in range(min(4, NC - 4 * q)):
                    last = nc.tensor.matmul(bank_of(q, c, n_out), yT[(base + q) % 2][:, c, :], w, start=True, stop=True)
                last.then_inc(lin_done, 1)

            def lin_bank(q, c, n_out):
                if c == 0 and q >= 2:
                    pe.wait_ge(lin_out, q - 1)
                return bank[2 + q % 2][0:CN, c * n_out:(c + 1) * n_out]

            def shift_bank(q, c, n_out):
                return bank[6][0:CN, (4 * q + c) * n_out:(4 * q + c + 1) * n_out]

            for c in (0, 1, 2):
                gates(c)
            pe.wait_ge(v_set, 1)
            for q in range(NQ):
                turn(0, q, v)
                gates(2 * q + 3)
                gates(2 * q + 4)
                layer(0, q, k.w3[:, :], HID, lin_bank)
            for c in range(2 * NQ + 3, NC):
                gates(c)
            pe.wait_ge(v_set, 2)
            for q in range(NQ):
                turn(NQ, q, y3)
                layer(NQ, q, k.w4[:, :], DIM, shift_bank)

        @block.vector
        def _(dve):
            link, count = links(dve, n_step)
            link(nc.vector.tensor_tensor(v[:, :, :], acc[:, :, :], k.inv_deg[:, :].unsqueeze(2)
                                         .to_broadcast([CN, NC, HID]), ALU.mult))
            link(nc.vector.tensor_tensor(v[:, :, :], v[:, :, :], k.b2[:, :].unsqueeze(1).to_broadcast([CN, NC, HID]), ALU.add))

            def elu(v, e, i, between=None):
                link(nc.vector.tensor_scalar(e, v, 0.0, None, ALU.min))
                dve.sem_inc(act_in, 1)
                link(nc.vector.tensor_scalar(v, v, 0.0, None, ALU.max))
                if between:
                    between()
                dve.wait_ge(act_out, i)
                link(nc.vector.scalar_tensor_tensor(v, e, -1.0, v, ALU.add, ALU.add))

            def gates_out(c):
                ps = gate_bank[c % 3][0:CN, 0:HEADS * HW].rearrange("n (h g) -> n h g", h=HEADS)
                dve.wait_ge(gi_done, c + 1)
                link(nc.vector.tensor_scalar(rden[:, c % 2, :], ps[:, :, G3:HW].rearrange("n h o -> n (h o)"), 1e-30, None,
                                             ALU.max))
                link(nc.vector.reciprocal(rden[:, c % 2, :], rden[:, c % 2, :]))
                link(nc.vector.tensor_tensor(gih[c % 2][:, :, :], ps[:, :, 0:G3],
                                             rden[:, c % 2, :].unsqueeze(2).to_broadcast([CN, HEADS, G3]), ALU.mult))
                dve.sem_inc(gi_out, 1)
                link(nc.vector.tensor_reduce(gi[:, c, :], gih[c % 2][:, :, :].rearrange("n h g -> n g h"), AX_X, ALU.add))

            def several_out(first, n):
                for c in range(first, first + n):
                    gates_out(c)

            elu(v[:, :, :], e[:, :, :], 1, lambda: several_out(0, 2))
            dve.sem_inc(v_set, 1)
            for q in range(NQ):
                several_out(2 * q + 2, 2)
                n = min(4, NC - 4 * q)
                dve.wait_ge(lin_done, q + 1)
                nc.vector.tensor_tensor(y3[:, 4 * q:4 * q + n, :],
                                        bank[2 + q % 2][0:CN, 0:n * HID].rearrange("n (c f) -> n c f", c=n),
                                        k.b3[:, :].unsqueeze(1).to_broadcast([CN, n, HID]), ALU.add).then_inc(lin_out, 1)
            dve.wait_ge(lin_out, NQ)
            elu(y3[:, :, :], e[:, :, :], 2, lambda: several_out(2 * NQ + 2, 2))
            dve.sem_inc(v_set, 1)
            several_out(2 * NQ + 4, NC - (2 * NQ + 4))
            rz = gi[:, :, 0:2 * FEAT]
            link(nc.vector.tensor_tensor(rz, rz, k.gh[:, :, 0:2 * FEAT], ALU.add))
            dve.sem_inc(act_in, 1)
            link(nc.vector.tensor_tensor(gi[:, :, 2 * FEAT:G3], gi[:, :, 2 * FEAT:G3],
                                         k.bih[:, 2 * FEAT:G3].unsqueeze(1).to_broadcast([CN, NC, FEAT]), ALU.add))
            dve.wait_ge(act_out, 3)
            link(nc.vector.tensor_tensor(nn[:, :, :], gi[:, :, 0:FEAT], k.gh[:, :, 2 * FEAT:G3], ALU.mult))
            link(nc.vector.tensor_tensor(nn[:, :, :], nn[:, :, :], gi[:, :, 2 * FEAT:G3], ALU.add))
            dve.sem_inc(act_in, 1)
            dve.wait_ge(act_out, 4)
            link(nc.vector.tensor_tensor(xm[:, :, :], k.tab_a[:, :, 0:FEAT], nn[:, :, :], ALU.subtract))
            link(nc.vector.tensor_tensor(xm[:, :, :], xm[:, :, :], gi[:, :, FEAT:2 * FEAT], ALU.mult))
            link(nc.vector.tensor_tensor(xm[:, :, :], xm[:, :, :], nn[:, :, :], ALU.add))
            elu(xm[:, :, :], nn[:, :, :], 5)
            link(nc.vector.tensor_tensor(k.x1[:, :, :], k.x[:, :, :], xm[:, :, :], ALU.add))
            layer_norm(nc, dve, link, k.x1[:, :, :], xm, sq, stat, node3[:, :, 0:FEAT], var_set, sd_set, 1)
            dve.wait_ge(lin_done, 2 * NQ)
            link(nc.vector.tensor_tensor(node3[:, :, FEAT:FEAT + DIM],
                                         bank[6][0:CN, 0:NC * DIM].rearrange("n (c d) -> n c d", d=DIM),
                                         k.b4[:, :].unsqueeze(1).to_broadcast([CN, NC, DIM]), ALU.add))
            link(nc.vector.tensor_copy(k.shift[:, :, :], node3[:, :, FEAT:FEAT + DIM]))
            dve.sem_inc(node3_set, 1)


def build_last(nc, a, k, slots_dram, node3_dram, out_dram):
    with ExitStack() as ctx:
        def sb(name, shape, dt=F32):
            return ctx.enter_context(nc.sbuf_tensor(name, shape, dt))

        def sem(name):
            return ctx.enter_context(nc.semaphore(name))

        t = conv_tiles(nc, ctx, FEAT, "last_")
        rows = [sb(f"last_rows{g}", [P, GB, NROW]) for g in range(NGR)]
        wt = sb("last_w", [K, FEAT, FEAT])
        bias = sb("last_bias", [CN, FEAT])
        ohn = sb("last_ohn", [P, BPC, NB])
        ohT = sb("last_ohT", [CN, P])
        bds = sb("last_bds", [CN, BPC, DIM])
        moved = sb("moved", [P, BPC, DIM])
        pos = sb("last_pos", [P, BPC, DIM])
        acc = sb("acc3", [CN, NC, FEAT])
        bank = [ctx.enter_context(nc.psum_tensor(f"last_bank{i}", [P, 512], F32)) for i in range(8)]

        w_in = sem("last_w_in")
        slot_in = sem("last_slot_in")
        slot_used = sem("last_slot_used")
        index_set = sem("last_index_set")
        rows_in = [sem(f"last_rows_in{g}") for g in range(NGR)]
        oh_set = sem("last_oh_set")
        ohT_done = sem("last_ohT_done")
        ohT_set = sem("last_ohT_set")
        bds_set = sem("last_bds_set")
        shift_done = sem("last_shift_done")
        mixed_set = sem("last_mixed_set")
        sum_done = sem("last_sum_done")
        sum_set = sem("last_sum_set")
        out_done = sem("last_out_done")
        acc_set = sem("last_acc_set")
        last_step = sem("last_step")
        end_step = sem("last_end_step")
        result_set = sem("result_set")
        result_out = sem("result_out")

        block = ctx.enter_context(nc.Block())

        @block.sync
        def _(sp):
            def load_slots(s):
                sp.dma_start(t.slot[:, :, :].rearrange("p b w -> p (b w)"),
                             slots_dram[bass.ds(s * SROWS, SROWS), :].rearrange("(p b) w -> p (b w)", b=BPC))\
                  .then_inc(slot_in, 16)

            sections = sp.value_load(k.sect_count[0:1, 0:1], min_val=NC, max_val=MAXSEC - 2)
            load_slots(0)
            sp.dma_start(wt[:, :, :], a["L1_gnn_conv_w"]).then_inc(w_in, 16)
            sp.dma_start(bias[:, :], a["L1_gnn_conv_b"].rearrange("(o f) -> o f", o=1).to_broadcast([CN, FEAT]))\
              .then_inc(w_in, 16)
            with sp.Fori(1, sections + 1) as s:
                sp.wait_ge(slot_used, s)
                sp.nop(nofuse=True)
                sp.wait_ge(index_set, s * NGR)
                sp.nop(nofuse=True)
                load_slots(s)
            sp.wait_ge(slot_in, sections * 16 + 16)
            sp.nop(nofuse=True)
            sp.wait_ge(result_set, 1)
            sp.dma_start(out_dram[0:(NC - 1) * CN, :].rearrange("(c p) f -> p c f", p=CN), acc[:, 0:NC - 1, :])\
              .then_inc(result_out, 16)
            sp.dma_start(out_dram[(NC - 1) * CN:N, :], acc[0:LAST, NC - 1, :]).then_inc(result_out, 16)
            sp.wait_ge(result_out, 32)

        @block.gpsimd
        def _(pool):
            sections = pool.value_load(k.sect_count[0:1, 0:1], min_val=NC, max_val=MAXSEC - 2)

            def fetch(s, first):
                for g in range(NGR):
                    pool.wait_ge(index_set, s * NGR + (g + 1))
                    if not first:
                        pool.wait_ge(mixed_set, s * NGR - (NGR - 1 - g))
                    pool.nop(nofuse=True)
                    for b in range(GB):
                        nc.gpsimd.indirect_dma_start(
                            rows[g][:, b, :], None, node3_dram[:, :],
                            bass.IndirectOffsetOnAxis(ap=t.index[g][:, b:b + 1], axis=0)).then_inc(rows_in[g], 16)
            fetch(0, True)
            with pool.Fori(1, sections) as s:
                fetch(s, False)

        @block.scalar
        def _(act):
            def indices(g):
                nc.scalar.copy(t.index[g][:, :], t.slot[:, g * GB:(g + 1) * GB, 1:2].bitcast(U32)
                               .rearrange("p b o -> p (b o)")).then_inc(index_set, 1)

            act.wait_ge(slot_in, 16)
            for g in range(NGR):
                indices(g)
            sections = act.value_load(k.sect_count[0:1, 0:1], min_val=NC, max_val=MAXSEC - 2)

            def one_hots_out(s):
                act.wait_ge(ohT_done, s + 1)
                nc.scalar.copy(ohT[:, :], bank[4][0:CN, 0:P]).then_inc(ohT_set, 1)

            def section(s, first):
                for g in range(NGR):
                    act.wait_ge(slot_in, s * 16 + 32)
                    act.wait_ge(rows_in[g], s * (GB * 16) + GB * 16)
                    indices(g)
                    for b in range(g * GB, (g + 1) * GB):
                        act.wait_ge(sum_done, s * BPC + (b + 1))
                        if b == 0 and not first:
                            act.wait_ge(out_done, s)
                        nc.scalar.copy(t.sums[:, b * NB:(b + 1) * NB, :].rearrange("k n f -> k (n f)"),
                                       bank[b % 3][0:K, 0:NB * FEAT]).then_inc(sum_set, 1)
                    if g == 0:
                        one_hots_out(s + 1)

            one_hots_out(0)
            section(0, True)
            with act.Fori(1, sections) as s:
                section(s, False)

        @block.tensor
        def _(pe):
            sections = pe.value_load(k.sect_count[0:1, 0:1], min_val=NC, max_val=MAXSEC - 2)
            pe.wait_ge(w_in, 32)

            def turn(s):
                pe.wait_ge(oh_set, s + 1)
                nc.tensor.transpose(bank[4][0:CN, 0:P], ohn[:, :, :].rearrange("p b j -> p (b j)"), k.ident[:, :])\
                    .then_inc(ohT_done, 1)

            def shift(s):
                pe.wait_ge(ohT_set, s + 1)
                pe.wait_ge(bds_set, s + 1)
                nc.tensor.matmul(bank[5][:, 0:BPC * DIM], ohT[:, :], bds[:, :, :].rearrange("n b w -> n (b w)"),
                                 start=True, stop=True).then_inc(shift_done, 1)

            def section(s, first):
                for g in range(NGR):
                    pe.wait_ge(mixed_set, s * NGR + (g + 1))
                    for b in range(g * GB, (g + 1) * GB):
                        if b >= 3 or not first:
                            pe.wait_ge(sum_set, s * BPC + (b - 2))
                        nc.tensor.matmul(bank[b % 3][0:K, 0:NB * FEAT], t.bas[g][:, b - g * GB, :],
                                         t.mixed[g][:, b - g * GB, :, :].rearrange("p j f -> p (j f)"),
                                         start=True, stop=True).then_inc(sum_done, 1)
                    if g == 0:
                        turn(s + 1)
                    if g == 1:
                        shift(s + 1)
                pe.wait_ge(sum_set, s * BPC + BPC)
                if not first:
                    pe.wait_ge(acc_set, s)
                for i in range(FEAT):
                    last = nc.tensor.matmul(bank[3][0:CN, 0:FEAT], t.sums[:, :, i], wt[:, i, :],
                                            start=(i == 0), stop=(i == FEAT - 1))
                last.then_inc(out_done, 1)

            turn(0)
            shift(0)
            section(0, True)
            with pe.Fori(1, sections) as s:
                section(s, False)

        @block.vector
        def _(dve):
            sections = dve.value_load(k.sect_count[0:1, 0:1], min_val=NC, max_val=MAXSEC - 2)
            link, count = links(dve, end_step)
            link(nc.vector.memset(acc[:, :, :], 0.0))

            def add_out(s_last):
                c = dve.value_load(k.sect[0:1, 0, bass.ds(s_last, 1)], min_val=0, max_val=NC - 1)
                sl = acc[:, bass.ds(c, 1), :].rearrange("n c f -> n (c f)")
                return nc.vector.tensor_tensor(sl, sl, bank[3][0:CN, 0:FEAT], ALU.add)

            def one_hot(tile):
                return nc.vector.tensor_tensor(tile[:, :, :], k.iota_j[:, :].unsqueeze(1).to_broadcast([P, BPC, NB]),
                                               t.slot[:, :, 0:1].to_broadcast([P, BPC, NB]), ALU.is_equal)

            def sources(s, link):
                dve.wait_ge(slot_in, s * 16 + 16)
                link(one_hot(ohn))
                dve.sem_inc(oh_set, 1)
                c = dve.value_load(k.sect[0:1, 0, bass.ds(s, 1)], min_val=0, max_val=NC - 1)
                link(nc.vector.tensor_tensor(
                    bds[:, :, :], k.shift[:, bass.ds(c, 1), :].to_broadcast([CN, BPC, DIM]),
                    k.bmask[:, :].unsqueeze(2).to_broadcast([CN, BPC, DIM]), ALU.mult))
                dve.sem_inc(bds_set, 1)

            def section(s, first):
                link, count = links(dve, last_step, s * LAST_STEPS)
                dve.wait_ge(slot_in, s * 16 + 16)
                link(one_hot(t.oh))
                dve.wait_ge(shift_done, s + 1)
                link(nc.vector.tensor_tensor(moved[:, :, :], t.slot[:, :, 3:3 + DIM],
                                             bank[5][:, 0:BPC * DIM].rearrange("p (b d) -> p b d", b=BPC),
                                             ALU.subtract))
                dve.sem_inc(slot_used, 1)
                for g in range(NGR):
                    b0, b1 = g * GB, (g + 1) * GB
                    dve.wait_ge(rows_in[g], s * (GB * 16) + GB * 16)
                    link(nc.vector.tensor_tensor(pos[:, b0:b1, :], moved[:, b0:b1, :], rows[g][:, :, FEAT:FEAT + DIM],
                                                 ALU.add))
                    link(nc.vector.tensor_scalar(pos[:, b0:b1, :], pos[:, b0:b1, :], 0.0, 1.0, ALU.max, ALU.min))
                    link(nc.vector.tensor_scalar(pos[:, b0:b1, :], pos[:, b0:b1, :], float(KS - 1), None, ALU.mult))
                    hat_weights(nc, link, k, pos[:, b0:b1, :], t.hat[:, b0:b1, :, :], t.rise[:, b0:b1, :, :],
                                t.fall[:, b0:b1, :, :], GB)
                    if not first:
                        dve.wait_ge(sum_done, s * BPC - (NGR - 1 - g) * GB)
                    link(basis_group(nc, t, g, link))
                    link(nc.vector.tensor_tensor(
                        t.mixed[g][:, :, :, :],
                        t.oh[:, b0:b1, :].unsqueeze(3).to_broadcast([P, GB, NB, FEAT]),
                        rows[g][:, :, 0:FEAT].unsqueeze(2).to_broadcast([P, GB, NB, FEAT]), ALU.mult))
                    dve.sem_inc(mixed_set, 1)
                    if g == 0:
                        sources(s + 1, link)
                    if g == 1:
                        if not first:
                            dve.wait_ge(out_done, s)
                            link(add_out(s - 1))
                            dve.sem_inc(acc_set, 1)
                        else:
                            dve.sem_inc(last_step, 1)
                            count[0] += 1
                return count[0]

            LAST_STEPS = 32
            sources(0, link)
            section(0, True)
            with dve.Fori(1, sections) as s:
                n = section(s, False)
                assert n == LAST_STEPS, n
            dve.wait_ge(out_done, sections)
            link(add_out(sections - 1))
            shape = [CN, NC, FEAT]
            link(nc.vector.tensor_tensor(acc[:, :, :], acc[:, :, :], k.inv_deg[:, :].unsqueeze(2).to_broadcast(shape),
                                         ALU.mult))
            link(nc.vector.tensor_tensor(acc[:, :, :], acc[:, :, :], bias[:, :].unsqueeze(1).to_broadcast(shape), ALU.add))
            link(nc.vector.tensor_tensor(acc[:, :, :], acc[:, :, :], k.x1[:, :, :], ALU.add))
            dve.sem_inc(result_set, 1)



_INS = ["x", "src", "dst", "edge_attr_3", "L0_gnn_W_gat", "L0_gnn_attn_l", "L0_gnn_attn_r", "L0_gnn_W_ih",
        "L0_gnn_W_hh", "L0_gnn_b_ih", "L0_gnn_b_hh", "L1_gnn_stn1_w", "L1_gnn_stn1_b", "L1_gnn_stn2_w",
        "L1_gnn_stn2_b", "L1_gnn_stn3_w", "L1_gnn_stn3_b", "L1_gnn_stn4_w", "L1_gnn_stn4_b", "L1_gnn_conv_w",
        "L1_gnn_conv_b"]


def build(nc, a, out):
    slots_dram = nc.dram_tensor("slots", ((MAXSEC + 1) * SROWS, SREC), F32).ap()
    drows_dram = nc.dram_tensor("drows", ((MAXSEC + 1) * SROWS, DREC), F32).ap()
    h1_dram = nc.dram_tensor("h1rows", (NC * CN, HID), F32).ap()
    node3_dram = nc.dram_tensor("node3", (NC * CN, NROW), F32).ap()
    rows_dram = nc.dram_tensor("key_rows", (4, E), F16).ap()
    with ExitStack() as ctx:
        k = keep_tiles(nc, ctx)
        keep_node_tiles(nc, ctx, k)
        build_sort(nc, a, k, a["src"].rearrange("(p t) -> p t", p=EP), a["dst"].rearrange("(p t) -> p t", p=EP),
                   a["edge_attr_3"].rearrange("(p t) d -> p t d", p=EP), k.sect, k.sect_count, slots_dram,
                   drows_dram, rows_dram, k.ident)
        build_send(nc, a, k, slots_dram, drows_dram, h1_dram)
        k.x1 = ctx.enter_context(nc.sbuf_tensor("x1", [CN, NC, FEAT], F32))
        with nc.sbuf_tensor("acc2", [CN, NC, HID], F32) as acc, \
                nc.sbuf_tensor("gacc", [FEAT + 1, NC, BPC * NB * HEADS], F32) as gacc:
            build_mid(nc, a, k, slots_dram, drows_dram, h1_dram, acc, gacc)
            build_nodes(nc, a, k, acc, gacc, node3_dram)
        build_last(nc, a, k, slots_dram, node3_dram, out)


def kernel(**inputs):
    import numpy as _np
    import concourse.bacc as _bacc
    from concourse import mybir as _mybir
    from concourse.bass_utils import run_bass_kernel_spmd as _run

    nc = _bacc.Bacc("TRN2", target_bir_lowering=False, num_devices=1)
    arrays, args = {}, {}
    for name in _INS:
        a = _np.ascontiguousarray(inputs[name])
        arrays[f"in_{name}_dram"] = a
        args[name] = nc.dram_tensor(f"in_{name}_dram", a.shape, _mybir.dt.from_np(a.dtype),
                                    kind="ExternalInput").ap()
    out = nc.dram_tensor("out_0_dram", (N, FEAT), F32, kind="ExternalOutput").ap()
    build(nc, args, out)
    r = _run(nc, [arrays], core_ids=[0])
    return r.results[0]["out_0_dram"]
```
